# Optimizing a Trainium2 kernel written in Bass

```python
import numpy as np
import jax
import jax.numpy as jnp

def _softmax(x, axis=-1):
    return jax.nn.softmax(x, axis=axis)

def _gelu(x):
    return jax.nn.gelu(x, approximate=True)

def _silu(x):
    return jax.nn.silu(x)

def _sigmoid(x):
    return jax.nn.sigmoid(x)

def _layernorm(x, axis=-1, eps=1e-05):
    m = jnp.mean(x, axis=axis, keepdims=True)
    v = jnp.var(x, axis=axis, keepdims=True)
    return (x - m) / jnp.sqrt(v + eps)

def _scatter_add(tgt, idx, src, axis=0):
    return tgt.at[idx].add(src)

def _segment_sum(src, seg, n):
    return jax.ops.segment_sum(src, seg, n)
kernel_name = 'mk_adj_seq_d2_adj_r2_54a68d'

def setup_inputs(seed: int=0):
    np.random.seed(seed)
    _w = jnp.asarray

    def _rec_inputs():
        import jax
        import jax.numpy as jnp
        _gk = jax.random.key(seed)
        x = -0.0005207 + 1.001 * jax.random.normal(jax.random.fold_in(_gk, 1), (32, 256, 128), jnp.float32)
        _a = jax.random.bernoulli(jax.random.fold_in(_gk, 2), 0.03125, (32, 256, 256))
        _a = jnp.logical_or(_a, jnp.swapaxes(_a, -1, -2))
        _a = jnp.logical_or(_a, jnp.eye(256, dtype=bool))
        adj = _a.astype(jnp.int32)
        return (x, adj)
    x, adj = _rec_inputs()

    def _L0_gnn_setup():
        import jax, jax.numpy as jnp
        import numpy as np
        B, N, D = (8, 512, 128)
        H = 8
        DH = D // H
        R = 4
        FF = 512
        EPS = 1e-05

        def _lin(k, fan_in, shape):
            return jax.random.normal(k, shape, jnp.float32) * (1.0 / np.sqrt(fan_in))

        def _ln(x, g, b):
            m = x.mean(-1, keepdims=True)
            v = ((x - m) ** 2).mean(-1, keepdims=True)
            return (x - m) * jax.lax.rsqrt(v + EPS) * g + b
        key = jax.random.key(seed)
        ks = jax.random.split(key, 16)
        src = jax.random.normal(ks[0], (B, N, D), jnp.float32)
        adj_matrix = jax.random.randint(ks[1], (B, N, N), 0, 5, dtype=jnp.int32)
        Wq = _lin(ks[2], D, (D, D))
        bq = jnp.zeros((D,), jnp.float32)
        Wk = _lin(ks[3], D, (D, D))
        bk = jnp.zeros((D,), jnp.float32)
        Wv = _lin(ks[4], D, (R, D, D))
        bv = jnp.zeros((R, D), jnp.float32)
        Wo = _lin(ks[5], D, (D, D))
        bo = jnp.zeros((D,), jnp.float32)
        W1 = _lin(ks[6], D, (D, FF))
        b1 = jnp.zeros((FF,), jnp.float32)
        W2 = _lin(ks[7], FF, (FF, D))
        b2 = jnp.zeros((D,), jnp.float32)
        g1 = jnp.ones((D,), jnp.float32)
        beta1 = jnp.zeros((D,), jnp.float32)
        g2 = jnp.ones((D,), jnp.float32)
        beta2 = jnp.zeros((D,), jnp.float32)
        return dict(src=src, adj_matrix=adj_matrix, Wq=Wq, bq=bq, Wk=Wk, bk=bk, Wv=Wv, bv=bv, Wo=Wo, bo=bo, W1=W1, b1=b1, W2=W2, b2=b2, g1=g1, beta1=beta1, g2=g2, beta2=beta2)
    _L0_gnn_all = _L0_gnn_setup()
    _L0_gnn_in = {k: v for k, v in _L0_gnn_all.items() if k in ('Wq', 'bq', 'Wk', 'bk', 'Wv', 'bv', 'Wo', 'bo', 'W1', 'b1', 'W2', 'b2', 'g1', 'beta1', 'g2', 'beta2')}
    del _L0_gnn_all

    def _L1_gnn_setup():
        import jax, jax.numpy as jnp
        import numpy as np
        ALPHA = 0.2
        NEG = -9000000000000000.0
        EPS = 1e-05

        def _gat(h, adj, W, a, out_features):
            Wh = jnp.matmul(h, W)
            Wh1 = jnp.matmul(Wh, a[:out_features])
            Wh2 = jnp.matmul(Wh, a[out_features:])
            e = Wh1 + jnp.swapaxes(Wh2, 1, 2)
            e = jax.nn.leaky_relu(e, negative_slope=ALPHA)
            scores = jnp.where(adj > 0, e, NEG)
            att = jax.nn.softmax(scores, axis=1)
            return jnp.matmul(att, Wh)

        def _layernorm(x, g, b):
            mu = jnp.mean(x, axis=-1, keepdims=True)
            var = jnp.var(x, axis=-1, keepdims=True)
            return (x - mu) * jax.lax.rsqrt(var + EPS) * g + b
        key = jax.random.key(seed)
        ks = jax.random.split(key, 8)
        B, N, F, H = (2, 2048, 128, 512)
        x = jax.random.normal(ks[0], (B, N, F), dtype=jnp.float32)
        adj = jax.random.randint(ks[1], (B, N, N), 0, 2, dtype=jnp.int32)

        def xavier(k, shape):
            fan_in, fan_out = (shape[0], shape[1])
            lim = np.sqrt(6.0 / (fan_in + fan_out))
            return jax.random.uniform(k, shape, jnp.float32, -lim, lim)
        return {'x': x, 'adj': adj, 'W1': xavier(ks[2], (F, F)), 'a1': xavier(ks[3], (2 * F, 1)), 'W2': xavier(ks[4], (F, F)), 'a2': xavier(ks[5], (2 * F, 1)), 'w_ff1': xavier(ks[6], (F, H)), 'b_ff1': jnp.zeros((H,), jnp.float32), 'w_ff2': xavier(ks[7], (H, F)), 'b_ff2': jnp.zeros((F,), jnp.float32), 'g_ln1': jnp.ones((F,), jnp.float32), 'b_ln1': jnp.zeros((F,), jnp.float32), 'g_ln2': jnp.ones((F,), jnp.float32), 'b_ln2': jnp.zeros((F,), jnp.float32)}
    _L1_gnn_all = _L1_gnn_setup()
    _L1_gnn_in = {k: v for k, v in _L1_gnn_all.items() if k in ('W1', 'a1', 'W2', 'a2', 'w_ff1', 'b_ff1', 'w_ff2', 'b_ff2', 'g_ln1', 'b_ln1', 'g_ln2', 'b_ln2')}
    del _L1_gnn_all
    return {'x': x, 'adj': adj, 'L0_gnn_Wq': _L0_gnn_in['Wq'], 'L0_gnn_bq': _L0_gnn_in['bq'], 'L0_gnn_Wk': _L0_gnn_in['Wk'], 'L0_gnn_bk': _L0_gnn_in['bk'], 'L0_gnn_Wv': _L0_gnn_in['Wv'], 'L0_gnn_bv': _L0_gnn_in['bv'], 'L0_gnn_Wo': _L0_gnn_in['Wo'], 'L0_gnn_bo': _L0_gnn_in['bo'], 'L0_gnn_W1': _L0_gnn_in['W1'], 'L0_gnn_b1': _L0_gnn_in['b1'], 'L0_gnn_W2': _L0_gnn_in['W2'], 'L0_gnn_b2': _L0_gnn_in['b2'], 'L0_gnn_g1': _L0_gnn_in['g1'], 'L0_gnn_beta1': _L0_gnn_in['beta1'], 'L0_gnn_g2': _L0_gnn_in['g2'], 'L0_gnn_beta2': _L0_gnn_in['beta2'], 'L1_gnn_W1': _L1_gnn_in['W1'], 'L1_gnn_a1': _L1_gnn_in['a1'], 'L1_gnn_W2': _L1_gnn_in['W2'], 'L1_gnn_a2': _L1_gnn_in['a2'], 'L1_gnn_w_ff1': _L1_gnn_in['w_ff1'], 'L1_gnn_b_ff1': _L1_gnn_in['b_ff1'], 'L1_gnn_w_ff2': _L1_gnn_in['w_ff2'], 'L1_gnn_b_ff2': _L1_gnn_in['b_ff2'], 'L1_gnn_g_ln1': _L1_gnn_in['g_ln1'], 'L1_gnn_b_ln1': _L1_gnn_in['b_ln1'], 'L1_gnn_g_ln2': _L1_gnn_in['g_ln2'], 'L1_gnn_b_ln2': _L1_gnn_in['b_ln2']}

def reference(x, adj, L0_gnn_Wq, L0_gnn_bq, L0_gnn_Wk, L0_gnn_bk, L0_gnn_Wv, L0_gnn_bv, L0_gnn_Wo, L0_gnn_bo, L0_gnn_W1, L0_gnn_b1, L0_gnn_W2, L0_gnn_b2, L0_gnn_g1, L0_gnn_beta1, L0_gnn_g2, L0_gnn_beta2, L1_gnn_W1, L1_gnn_a1, L1_gnn_W2, L1_gnn_a2, L1_gnn_w_ff1, L1_gnn_b_ff1, L1_gnn_w_ff2, L1_gnn_b_ff2, L1_gnn_g_ln1, L1_gnn_b_ln1, L1_gnn_g_ln2, L1_gnn_b_ln2):
    import jax
    import jax.numpy as jnp

    def _L0_gnn_ref(src, adj_matrix, Wq, bq, Wk, bk, Wv, bv, Wo, bo, W1, b1, W2, b2, g1, beta1, g2, beta2):
        import jax, jax.numpy as jnp
        import numpy as np
        B, N, D = (8, 512, 128)
        H = 8
        DH = D // H
        R = 4
        FF = 512
        EPS = 1e-05

        def _lin(k, fan_in, shape):
            return jax.random.normal(k, shape, jnp.float32) * (1.0 / np.sqrt(fan_in))

        def _ln(x, g, b):
            m = x.mean(-1, keepdims=True)
            v = ((x - m) ** 2).mean(-1, keepdims=True)
            return (x - m) * jax.lax.rsqrt(v + EPS) * g + b
        Bb, Nn, Dm = src.shape
        h, dh = (H, Dm // H)
        q = (src @ Wq + bq).reshape(Bb, Nn, h, dh).transpose(0, 2, 1, 3)
        k = (src @ Wk + bk).reshape(Bb, Nn, h, dh).transpose(0, 2, 1, 3)
        scores = jnp.einsum('bhid,bhjd->bhij', q, k) / np.sqrt(dh)
        attn = jax.nn.softmax(scores, axis=-1)
        out = jnp.zeros_like(q)
        for r in range(Wv.shape[0]):
            v_r = (src @ Wv[r] + bv[r]).reshape(Bb, Nn, h, dh).transpose(0, 2, 1, 3)
            mask = (adj_matrix == r)[:, None]
            out = out + jnp.einsum('bhij,bhjd->bhid', attn * mask, v_r)
        attn_out = out.transpose(0, 2, 1, 3).reshape(Bb, Nn, Dm) @ Wo + bo
        x = _ln(src + attn_out, g1, beta1)
        ff = jax.nn.gelu(x @ W1 + b1, approximate=False) @ W2 + b2
        return _ln(x + ff, g2, beta2)

    def _L1_gnn_ref(x, adj, W1, a1, W2, a2, w_ff1, b_ff1, w_ff2, b_ff2, g_ln1, b_ln1, g_ln2, b_ln2):
        import jax, jax.numpy as jnp
        import numpy as np
        ALPHA = 0.2
        NEG = -9000000000000000.0
        EPS = 1e-05

        def _gat(h, adj, W, a, out_features):
            Wh = jnp.matmul(h, W)
            Wh1 = jnp.matmul(Wh, a[:out_features])
            Wh2 = jnp.matmul(Wh, a[out_features:])
            e = Wh1 + jnp.swapaxes(Wh2, 1, 2)
            e = jax.nn.leaky_relu(e, negative_slope=ALPHA)
            scores = jnp.where(adj > 0, e, NEG)
            att = jax.nn.softmax(scores, axis=1)
            return jnp.matmul(att, Wh)

        def _layernorm(x, g, b):
            mu = jnp.mean(x, axis=-1, keepdims=True)
            var = jnp.var(x, axis=-1, keepdims=True)
            return (x - mu) * jax.lax.rsqrt(var + EPS) * g + b
        Fout = W1.shape[1]
        residual = x
        h = _gat(x, adj, W1, a1, Fout)
        h = _gat(h, adj, W2, a2, W2.shape[1])
        h = _layernorm(residual + h, g_ln1, b_ln1)
        residual2 = h
        ff = jnp.matmul(jax.nn.relu(jnp.matmul(h, w_ff1) + b_ff1), w_ff2) + b_ff2
        return _layernorm(residual2 + ff, g_ln2, b_ln2)
    x = _L0_gnn_ref(x, adj, L0_gnn_Wq, L0_gnn_bq, L0_gnn_Wk, L0_gnn_bk, L0_gnn_Wv, L0_gnn_bv, L0_gnn_Wo, L0_gnn_bo, L0_gnn_W1, L0_gnn_b1, L0_gnn_W2, L0_gnn_b2, L0_gnn_g1, L0_gnn_beta1, L0_gnn_g2, L0_gnn_beta2)
    x = _L1_gnn_ref(x, adj, L1_gnn_W1, L1_gnn_a1, L1_gnn_W2, L1_gnn_a2, L1_gnn_w_ff1, L1_gnn_b_ff1, L1_gnn_w_ff2, L1_gnn_b_ff2, L1_gnn_g_ln1, L1_gnn_b_ln1, L1_gnn_g_ln2, L1_gnn_b_ln2)
    return x

_drawn_inputs = setup_inputs


def setup_inputs(seed=0):
    import zlib

    import numpy as np

    out = dict(_drawn_inputs(seed))
    spreads = {'L0_gnn_bq': (0.0, 0.676),
     'L0_gnn_bk': (0.0, 0.8),
     'L0_gnn_bv': (0.0, 0.1),
     'L0_gnn_bo': (0.0, 0.1),
     'L0_gnn_b1': (0.0, 0.1),
     'L0_gnn_b2': (0.0, 0.1),
     'L0_gnn_g1': (1.0, 0.2),
     'L0_gnn_beta1': (0.0, 0.1),
     'L0_gnn_g2': (1.0, 0.2),
     'L0_gnn_beta2': (0.0, 0.1),
     'L1_gnn_b_ff1': (0.0, 0.1),
     'L1_gnn_b_ff2': (0.0, 0.1),
     'L1_gnn_g_ln1': (1.0, 0.2),
     'L1_gnn_b_ln1': (0.0, 0.1),
     'L1_gnn_g_ln2': (1.0, 0.2),
     'L1_gnn_b_ln2': (0.0, 0.1)}
    factors = {}
    for name, (base, spread) in spreads.items():
        noise = np.random.default_rng([zlib.crc32(name.encode()), seed]).standard_normal(out[name].shape)
        drawn = base * np.exp(spread * noise) if base else spread * noise
        out[name] = jnp.asarray(drawn.astype(out[name].dtype))
    for name, factor in factors.items():
        out[name] = (out[name] * factor).astype(out[name].dtype)
    return out
```

```python
from contextlib import ExitStack

import concourse.bass as bass
from concourse import mybir

F32 = mybir.dt.float32
BF16 = mybir.dt.bfloat16
I32 = mybir.dt.int32
I8 = mybir.dt.int8
ALU = mybir.AluOpType
ACT = mybir.ActivationFunctionType
AX = mybir.AxisListType.X
RMAX = bass.bass_isa.ReduceOp.max

B, N, D = 32, 256, 128
H, DH = 8, 16
R = 4
FF = 512
FC = FF // D
NC = N // 128
PAIRS = B // 2
W2G = 2 * N
EPS = 1e-5
SLOPE = 0.2
HIDDEN = -(2.0 ** 53)
PARTS = 3
TERMS = 6
ROWS = TERMS * DH
ROWSM = ROWS + PARTS
UNITS = 8
GRP = 4
ALLONE, OTHER = 0, 1

VECS = ["L0_gnn_bq", "L0_gnn_bk", "L0_gnn_g1", "L0_gnn_beta1", "L0_gnn_g2", "L0_gnn_beta2",
        "L1_gnn_g_ln1", "L1_gnn_b_ln1", "L1_gnn_g_ln2", "L1_gnn_b_ln2"]
CENTRED = ["L0_gnn_bo", "L0_gnn_b2", "L1_gnn_b_ff2"]
COL = {name: n for n, name in enumerate(VECS)}
COL_B1 = len(VECS)
COL_BFF1 = COL_B1 + FC
COL_A = COL_BFF1 + FC
NROWS = COL_A + 4


def due(value):
    return not isinstance(value, int) or value > 0


def pair_loop(eng, step, start, loop_from, loop_to, end):
    for p in range(start, 2 * loop_from):
        step(p // 2, p % 2)
    with eng.Fori(loop_from, loop_to) as i:
        for b in range(2):
            step(i, b)
    for p in range(2 * loop_to, end):
        step(p // 2, p % 2)


def attend_loop(eng, step):
    pair_loop(eng, step, -2, 1, PAIRS // 2 - 1, PAIRS + 1)


def at_most(value, most):
    return min(value, most) if isinstance(value, int) else value


def within(i, index, count):
    return not isinstance(i, int) or 0 <= index < count


def build(nc, a, out):
    ctx = ExitStack()
    with ctx:
        def sb(name, shape, dt=F32, where=ctx):
            return where.enter_context(nc.sbuf_tensor(name, shape, dt))

        def sem(name):
            return ctx.enter_context(nc.semaphore(name))

        bank = [ctx.enter_context(nc.psum_tensor(f"bank{n}", [128, 512], F32)) for n in range(8)]

        x_all = sb("x_all", [128, B * N])
        codes = sb("codes", [128, B, NC, N], I8)
        ident = sb("ident", [128, 128])
        identb = sb("identb", [128, 128], BF16)
        centre = sb("centre", [128, 128])
        mean_w = sb("mean_w", [128, 128])
        eps = sb("eps", [128, 1])
        cols = sb("cols", [128, NROWS])
        ccols = sb("ccols", [128, len(CENTRED)])
        w1 = sb("w1", [128, FF])
        w2 = sb("w2", [128, FC, D])
        wf1 = sb("wf1", [128, FF])
        wf2 = sb("wf2", [128, FC, D])
        gw = sb("gw", [128, 2, D + 1])
        ga = sb("ga", [128, 2, D])

        flag = sb("flag", [128, 1], I32)

        nodes_of = lambda pair: x_all[:, bass.ds(pair * W2G, W2G)]

        attend_ctx = ExitStack()
        A = lambda name, shape, dt=F32: sb(name, shape, dt, attend_ctx)
        wq = A("wq", [128, D])
        wk = A("wk", [128, D])
        wv = A("wv", [128, R + 1, D])
        bvb = A("bvb", [128, R + 1, D])
        wo = A("wo", [128, 2, D])

        setup_ctx = ExitStack()
        S = lambda name, shape, dt=F32: sb(name, shape, dt, setup_ctx)
        rows = S("rows", [NROWS, D])
        crows = S("crows", [len(CENTRED), D])
        crow_mean = S("crow_mean", [len(CENTRED), 1])
        graw = S("graw", [128, 2, D])
        gt = S("gt", [128, 2, D])
        abc = S("abc", [128, 2, D])
        wmean = S("wmean", [128, 12])
        adj_in = [S(f"adj_in{n}", [128, 2, NC, N], I32) for n in range(2)]
        adj_c = [S(f"adj_c{n}", [128, 2, NC, N], BF16) for n in range(2)]
        odd = S("odd", [128, PAIRS])
        odd_junk = S("odd_junk", [128, 2 * NC * N], BF16)
        mhalf = S("mhalf", [128, 1])
        odd_max = S("odd_max", [128, 1])
        odd_all = S("odd_all", [128, 1])

        rows_in, bo_in, wts_in, wo_in = sem("rows_in"), sem("bo_in"), sem("wts_in"), sem("wo_in")
        gat_in, bv_in = sem("gat_in"), sem("bv_in")
        adj_sem = [sem(f"adj_sem{n}") for n in range(2)]
        const_ready, wo_zero, prep, prep_pe = sem("const_ready"), sem("wo_zero"), sem("prep"), sem("prep_pe")
        clamped, turned, coded, counted = sem("clamped"), sem("turned"), sem("coded"), sem("counted")
        odd_sem = sem("odd_sem")
        vchain = sem("vchain")

        passed = sem("passed")
        with nc.Block() as block:
            @block.sync
            def _(sp):
                for n, name in enumerate(VECS):
                    sp.dma_start(rows[n:n + 1, :], a[name].rearrange("(o d) -> o d", o=1)).then_inc(rows_in, 16)
                for start, name in ((COL_B1, "L0_gnn_b1"), (COL_BFF1, "L1_gnn_b_ff1")):
                    sp.dma_start(rows[start:start + FC, :], a[name].rearrange("(c d) -> c d", c=FC)).then_inc(rows_in, 16)
                for n, name in enumerate(("L1_gnn_a1", "L1_gnn_a2")):
                    sp.dma_start(rows[COL_A + 2 * n:COL_A + 2 * n + 2, :],
                                 a[name].rearrange("(c d) o -> c (d o)", c=2)).then_inc(rows_in, 16)
                for n, name in enumerate(CENTRED):
                    sp.dma_start(crows[n:n + 1, :], a[name].rearrange("(o d) -> o d", o=1)).then_inc(bo_in, 16)

                def load_adj(i, n):
                    if due(2 * i + n - 1):
                        sp.wait_ge(clamped, 2 * i + n - 1)
                        sp.sem_inc(passed, 1)
                    sp.dma_start(adj_in[n][:], a["adj"][bass.ds(4 * i + 2 * n, 2)].rearrange(
                        "g (c p) j -> p g c j", c=NC)).then_inc(adj_sem[n], 16)
                pair_loop(sp, load_adj, 0, 1, PAIRS // 2, PAIRS)

            @block.gpsimd
            def _(pool):
                nc.gpsimd.memset(ident[:], 0.0).then_inc(const_ready, 1)
                pool.wait_ge(const_ready, 1)
                nc.gpsimd.affine_select(out=ident[:], in_=ident[:], compare_op=ALU.not_equal, fill=1.0, base=0,
                                        pattern=[[-1, 128]], channel_multiplier=1).then_inc(const_ready, 1)
                pool.wait_ge(const_ready, 2)
                nc.gpsimd.tensor_scalar(centre[:], ident[:], 1.0 / D, None, ALU.subtract).then_inc(const_ready, 1)
                nc.gpsimd.tensor_copy(identb[:], ident[:]).then_inc(const_ready, 1)
                nc.gpsimd.memset(mean_w[:], 1.0 / D).then_inc(const_ready, 1)
                nc.gpsimd.memset(eps[:], EPS).then_inc(const_ready, 1)
                nc.gpsimd.memset(mhalf[:], -0.5).then_inc(const_ready, 1)
                pool.wait_ge(odd_sem, 1)
                nc.gpsimd.partition_all_reduce(odd_all[:], odd_max[:], 128, RMAX).then_inc(odd_sem, 1)

            @block.scalar
            def _(act):
                act.dma_start(wq[:], a["L0_gnn_Wq"]).then_inc(wts_in, 16)
                act.dma_start(wk[:], a["L0_gnn_Wk"]).then_inc(wts_in, 16)
                act.dma_start(wv[:, 0:R, :], a["L0_gnn_Wv"].rearrange("r d e -> d r e")).then_inc(wts_in, 16)
                act.dma_start(w1[:], a["L0_gnn_W1"]).then_inc(wts_in, 16)
                act.dma_start(w2[:], a["L0_gnn_W2"].rearrange("(c k) d -> k c d", c=FC)).then_inc(wts_in, 16)
                act.dma_start(wf1[:], a["L1_gnn_w_ff1"]).then_inc(wts_in, 16)
                act.dma_start(wf2[:], a["L1_gnn_w_ff2"].rearrange("(c k) d -> k c d", c=FC)).then_inc(wts_in, 16)
                for n, name in enumerate(("L1_gnn_W1", "L1_gnn_W2")):
                    act.dma_start(graw[:, n, :], a[name]).then_inc(gat_in, 16)
                act.dma_start(bvb[:, 0:R, :], a["L0_gnn_bv"].partition_broadcast(128)).then_inc(bv_in, 16)
                act.wait_ge(wo_zero, 1)
                for h in range(H):
                    act.dma_start(wo[32 * (h % GRP):32 * (h % GRP) + DH, h // GRP, :],
                                  a["L0_gnn_Wo"][DH * h:DH * h + DH, :]).then_inc(wo_in, 16)
                act.wait_ge(const_ready, 7)
                def count_odd(p):
                    act.wait_ge(coded, p + 1)
                    if due(p):
                        act.wait_ge(counted, p)
                    nc.scalar.activation(odd_junk[:], codes[:, bass.ds(2 * p, 2)].rearrange("p g c i -> p (g c i)"),
                                         ACT.Square, bias=mhalf[:, 0:1],
                                         accum_out=odd[:, bass.ds(p, 1)]).then_inc(counted, 1)
                count_odd(0)
                with act.Fori(1, PAIRS) as p:
                    count_odd(p)

            @block.tensor
            def _(pe):
                def turn_codes(i, n):
                    pe.wait_ge(clamped, 2 * i + n + 1)
                    if due(2 * i + n - 1):
                        pe.wait_ge(coded, 2 * i + n - 1)
                    turned_bank = bank[n][:, :].bitcast(BF16).rearrange("p (g c i) -> p g c i", g=2, c=NC)
                    for g in range(2):
                        for c in range(NC):
                            for k in range(NC):
                                last = nc.tensor.transpose(turned_bank[:, g, c, 128 * k:128 * k + 128],
                                                           adj_c[n][:, g, k, 128 * c:128 * c + 128], identb[:])
                    last.then_inc(turned, 1)
                pe.wait_ge(const_ready, 4)
                pair_loop(pe, turn_codes, 0, 1, PAIRS // 2, PAIRS)
                pe.wait_ge(rows_in, 16 * (len(VECS) + 4))
                nc.tensor.transpose(bank[2][:, 0:NROWS], rows[:], ident[0:NROWS, 0:NROWS]).then_inc(prep_pe, 1)
                pe.wait_ge(prep, 1)
                nc.tensor.transpose(bank[3][:, 0:len(CENTRED)], crows[:],
                                    ident[0:len(CENTRED), 0:len(CENTRED)]).then_inc(prep_pe, 1)
                pe.wait_ge(gat_in, 32)
                for n in range(2):
                    last = nc.tensor.transpose(bank[4][:, 128 * n:128 * n + 128], graw[:, n, :], ident[:])
                last.then_inc(prep_pe, 1)
                pe.wait_ge(prep, 2)
                for n in range(2):
                    nc.tensor.matmul(bank[5 + n][:, 0:D], gt[:, n, :], abc[:, n, :], start=True, stop=True)
                for n in range(2):
                    last = nc.tensor.matmul(bank[5 + n][:, D:D + 1], gt[:, n, :],
                                            cols[:, COL_A + 2 * n + 1:COL_A + 2 * n + 2], start=True, stop=True)
                last.then_inc(prep_pe, 1)

            @block.vector
            def _(dve):
                links = [0]

                def link(ins):
                    links[0] += 1
                    ins.then_inc(vchain, 1)
                    dve.wait_ge(vchain, links[0])

                nc.vector.memset(wo[:], 0.0).then_inc(wo_zero, 1)

                def code(i, n):
                    P = 2 * i + n
                    if within(i, P, PAIRS):
                        dve.wait_ge(adj_sem[n], 16 * i + 16)
                        if due(P - 1):
                            dve.wait_ge(turned, P - 1)
                        nc.vector.tensor_scalar(adj_c[n][:], adj_in[n][:], -1.0, float(R), ALU.max,
                                                ALU.min).then_inc(clamped, 1)
                    if within(i, P - 1, PAIRS):
                        dve.wait_ge(turned, P)
                        nc.vector.tensor_copy(
                            codes[:, bass.ds(2 * (P - 1), 2)],
                            bank[1 - n][:, :].bitcast(BF16).rearrange("p (g c i) -> p g c i", g=2,
                                                                      c=NC)).then_inc(coded, 1)
                pair_loop(dve, code, 0, 1, PAIRS // 2, PAIRS + 1)
                dve.wait_ge(bo_in, 16 * len(CENTRED))
                link(nc.vector.tensor_reduce(crow_mean[:], crows[:], AX, ALU.add))
                link(nc.vector.tensor_scalar(crow_mean[:], crow_mean[:], 1.0 / D, None, ALU.mult))
                nc.vector.tensor_scalar(crows[:], crows[:], crow_mean[:, 0:1], None, ALU.subtract).then_inc(prep, 1)
                dve.wait_ge(prep_pe, 1)
                link(nc.vector.tensor_copy(cols[:], bank[2][:, 0:NROWS]))
                dve.wait_ge(prep_pe, 2)
                nc.vector.tensor_copy(ccols[:], bank[3][:, 0:len(CENTRED)])
                qcol = cols[:, COL["L0_gnn_bq"]:COL["L0_gnn_bq"] + 1]
                nc.vector.tensor_scalar(qcol, qcol, DH ** -0.5, None, ALU.mult)
                for n in range(2):
                    nc.vector.tensor_copy(abc[:, n, :], cols[:, COL_A + 2 * n:COL_A + 2 * n + 1].to_broadcast([128, D]))
                dve.wait_ge(prep_pe, 3)
                nc.vector.tensor_copy(gt[:], bank[4][:, 0:2 * D].rearrange("p (n d) -> p n d", n=2)).then_inc(prep, 1)
                dve.wait_ge(wts_in, 16 * 7)
                dve.wait_ge(wo_in, 16 * H)
                for at, w, k in ((0, wo, 2), (2, w2, FC), (6, wf2, FC)):
                    link(nc.vector.tensor_reduce(wmean[:, at:at + k], w[:], AX, ALU.add))
                    link(nc.vector.tensor_scalar(wmean[:, at:at + k], wmean[:, at:at + k], 1.0 / D, None, ALU.mult))
                    for c in range(k):
                        nc.vector.tensor_scalar(w[:, c, :], w[:, c, :], wmean[:, at + c:at + c + 1], None, ALU.subtract)
                link(nc.vector.tensor_reduce(wmean[:, 10:11], graw[:, 1, :], AX, ALU.add))
                link(nc.vector.tensor_scalar(wmean[:, 10:11], wmean[:, 10:11], 1.0 / D, None, ALU.mult))
                nc.vector.tensor_scalar(gw[:, 1, 0:D], graw[:, 1, :], wmean[:, 10:11], None, ALU.subtract)
                nc.vector.tensor_copy(gw[:, 0, 0:D], graw[:, 0, :])
                dve.wait_ge(prep_pe, 4)
                for n in range(2):
                    nc.vector.tensor_copy(ga[:, n, :], bank[5 + n][:, 0:D])
                    nc.vector.tensor_copy(gw[:, n, D:D + 1], bank[5 + n][:, D:D + 1])
                dve.wait_ge(bv_in, 16)
                for w in (wv, bvb):
                    nc.vector.tensor_scalar(w[:, R, :], w[:, 0, :], -1.0, None, ALU.mult)
                    for r in range(1, R):
                        nc.vector.tensor_tensor(w[:, r, :], w[:, r, :], w[:, 0, :], ALU.subtract)
                dve.wait_ge(counted, PAIRS)
                nc.vector.tensor_reduce(odd_max[:], odd[:], AX, ALU.max).then_inc(odd_sem, 1)
                dve.wait_ge(odd_sem, 2)
                nc.vector.tensor_scalar(flag[:], odd_all[:], 2 * NC * N / 4.0, None, ALU.is_gt)
        setup_ctx.close()

        parts = A("parts", [128, 2, PARTS, W2G], BF16)
        whole = A("whole", [128, 2, W2G])
        rest = A("rest", [128, 2, W2G])
        x_nat = [A(f"x_nat{n}", [128, 2 * NC, D]) for n in range(2)]
        x_t = [A(f"x_t{n}", [128, W2G]) for n in range(2)]
        q_st = [A(f"q_st{n}", [ROWSM, H, N], BF16) for n in range(4)]
        k_st = [A(f"k_st{n}", [ROWSM, H, N], BF16) for n in range(4)]
        v_base = [A(f"v_base{n}", [128, 2, NC, H, 32]) for n in range(2)]
        v_one = [A(f"v_one{n}", [128, 2, NC, H, DH]) for n in range(2)]
        v_more = [A(f"v_more{n}", [128, 2, NC, R - 1, H, DH]) for n in range(2)]
        probs = A("probs", [128, UNITS, 512])
        probs_one = A("probs_one", [128, UNITS, 512])
        probs_more = A("probs_more", [128, R - 1, 2, 512])
        more_tmp = A("more_tmp", [128, 512])
        row_max = [A(f"row_max{n}", [128, NC, H]) for n in range(2)]
        neg_max = A("neg_max", [128, NC, H])
        max_rest = A("max_rest", [128, NC, H])
        max_parts = A("max_parts", [128, NC, PARTS, H], BF16)
        max_t = A("max_t", [PARTS * H, N], BF16)
        denom = A("denom", [128, 512])
        denom_r = A("denom_r", [128, 512])
        mixed = A("mixed", [128, 2, W2G])
        ln_y = A("ln_y", [128, W2G])
        ln_sq = A("ln_sq", [128, W2G])
        ln_r = A("ln_r", [128, W2G])

        scr_parts = nc.dram_tensor("scr_parts", [PAIRS, 128, 2, PARTS, W2G], BF16).ap()
        scr_max = nc.dram_tensor("scr_max", [B, PARTS * H, N], BF16).ap()

        x_in = [sem(f"x_in{n}") for n in range(2)]
        xt_mm, xt_ready, x_kept = sem("xt_mm"), sem("xt_ready"), sem("x_kept")
        qk_mm, qk_whole, qk_rest, qk_split, parts_out = (sem("qk_mm"), sem("qk_whole"), sem("qk_rest"),
                                                         sem("qk_split"), sem("parts_out"))
        stacked = [sem(f"stacked{n}") for n in range(4)]
        s_mm, s_max, max_split, maxt_mm, maxt_ready = (sem("s_mm"), sem("s_max"), sem("max_split"), sem("maxt_mm"),
                                                       sem("maxt_ready"))
        max_out, max_in, msp = sem("max_out"), sem("max_in"), sem("msp")
        st_mm, exp_done, masked, pv_mm = sem("st_mm"), sem("exp_done"), sem("masked"), sem("pv_mm")
        v_mm, v_ready0, v_ready1, v_init, ones_init = (sem("v_mm"), sem("v_ready0"), sem("v_ready1"), sem("v_init"),
                                                       sem("ones_init"))
        den_ready, den_ln, den_inv, normed = sem("den_ready"), sem("den_ln"), sem("den_inv"), sem("normed")
        y_mm, y_read, var_mm, var_ln, rstd, ln_mid, ln_done = (sem("y_mm"), sem("y_read"), sem("var_mm"),
                                                              sem("var_ln"), sem("rstd"), sem("ln_mid"),
                                                              sem("ln_done"))
        vmore_mm, vmore_ready, more_done = sem("vmore_mm"), sem("vmore_ready"), sem("more_done")
        S_BANK, T_BANK, PV_BANK = bank[0:2], bank[2:4], bank[4:6]
        M0, M1 = bank[6], bank[7]

        with nc.Block() as block:
            @block.sync
            def _(sp):
                def x_load(pair, n):
                    sp.dma_start(x_nat[n][:], a["x"][bass.ds(2 * pair, 2)].rearrange(
                        "g (c p) d -> p (g c) d", c=NC)).then_inc(x_in[n], 16)

                def stack_load(i, b, k):
                    G, n = 4 * i + 2 * b + k, (2 * b + k) % 4
                    if not within(i, G, B):
                        return
                    P, gi = 2 * i + b + k // 2, k % 2
                    sp.wait_ge(parts_out, 16 * (P + 1))
                    sp.sem_inc(passed, 1)
                    if due(UNITS * (G - 3)):
                        sp.wait_ge(st_mm, UNITS * (G - 3))
                        sp.sem_inc(passed, 1)
                    src = scr_parts[bass.ds(P, 1)].rearrange("o (h d) t s (g i) -> (o t s) d h g i", d=DH, g=2)
                    for st, t, picks in ((q_st, 0, (0, 1, 2, 0, 1, 0)), (k_st, 1, (0, 0, 0, 1, 1, 2))):
                        for slot, part in enumerate(picks):
                            sp.dma_start(st[n][DH * slot:DH * slot + DH, :, :],
                                         src[t * PARTS + part, :, :, gi, :]).then_inc(stacked[n], 16)

                def max_rows(i, b, k):
                    G, n = 4 * i + 2 * b + k, (2 * b + k) % 4
                    if not within(i, G, B):
                        return
                    sp.wait_ge(maxt_ready, G + 1)
                    sp.sem_inc(passed, 1)
                    sp.dma_start(scr_max[bass.ds(G, 1)].rearrange("o r i -> (o r) i"), max_t[:]).then_inc(max_out, 16)
                    sp.wait_ge(max_out, 16 * (G + 1))
                    sp.sem_inc(passed, 1)
                    sp.dma_start(q_st[n][ROWS:ROWSM, :, :], scr_max[bass.ds(G, 1)].rearrange(
                        "o (s h) i -> (o s) h i", s=PARTS)).then_inc(max_in, 16)

                def step(i, b):
                    p = 2 * i + b
                    if within(i, p + 3, PAIRS):
                        if due(p + 2):
                            sp.wait_ge(xt_mm, p + 2)
                            sp.sem_inc(passed, 1)
                        x_load(p + 3, (b + 1) % 2)
                    stack_load(i, b, 3)
                    max_rows(i, b, 1)
                    if within(i, p + 2, PAIRS):
                        sp.wait_ge(qk_split, 2 * (p + 3))
                        sp.sem_inc(passed, 1)
                        sp.dma_start(scr_parts[bass.ds(p + 2, 1)].rearrange("o r t s n -> (o r) t s n"),
                                     parts[:]).then_inc(parts_out, 16)
                    stack_load(i, b, 4)
                    max_rows(i, b, 2)

                x_load(0, 0)
                pair_loop(sp, step, -2, 1, PAIRS // 2 - 2, PAIRS + 1)

            @block.gpsimd
            def _(pool):
                for n in range(4):
                    nc.gpsimd.memset(k_st[n][ROWS:ROWSM, :, :], 1.0).then_inc(ones_init, 1)

                def split(P, t):
                    pool.wait_ge(qk_whole, 2 * P + t + 1)
                    pool.sem_inc(passed, 1)
                    nc.gpsimd.tensor_tensor(rest[:, t, :], whole[:, t, :], parts[:, t, 0, :],
                                            ALU.subtract).then_inc(qk_rest, 1)
                    pool.wait_ge(qk_rest, 4 * P + 2 * t + 1)
                    pool.sem_inc(passed, 1)
                    nc.gpsimd.tensor_copy(parts[:, t, 1, :], rest[:, t, :]).then_inc(qk_rest, 1)
                    pool.wait_ge(qk_rest, 4 * P + 2 * t + 2)
                    pool.sem_inc(passed, 1)
                    nc.gpsimd.tensor_tensor(parts[:, t, 2, :], rest[:, t, :], parts[:, t, 1, :],
                                            ALU.subtract).then_inc(qk_split, 1)

                def split_max(i, b, k):
                    G, n = 4 * i + 2 * b + k, k % 2
                    if not within(i, G, B):
                        return
                    pool.wait_ge(s_max, UNITS * (G + 1))
                    pool.sem_inc(passed, 1)
                    if due(G):
                        pool.wait_ge(maxt_mm, G)
                        pool.sem_inc(passed, 1)
                    nc.gpsimd.tensor_scalar(neg_max[:], row_max[n][:], -1.0, 0.0, ALU.mult, ALU.add).then_inc(msp, 1)
                    pool.wait_ge(msp, 4 * G + 1)
                    pool.sem_inc(passed, 1)
                    nc.gpsimd.tensor_copy(max_parts[:, :, 0, :], neg_max[:]).then_inc(msp, 1)
                    pool.wait_ge(msp, 4 * G + 2)
                    pool.sem_inc(passed, 1)
                    nc.gpsimd.tensor_tensor(max_rest[:], neg_max[:], max_parts[:, :, 0, :], ALU.subtract).then_inc(msp, 1)
                    pool.wait_ge(msp, 4 * G + 3)
                    pool.sem_inc(passed, 1)
                    nc.gpsimd.tensor_copy(max_parts[:, :, 1, :], max_rest[:]).then_inc(msp, 1)
                    pool.wait_ge(msp, 4 * G + 4)
                    pool.sem_inc(passed, 1)
                    nc.gpsimd.tensor_tensor(max_parts[:, :, 2, :], max_rest[:], max_parts[:, :, 1, :],
                                            ALU.subtract).then_inc(max_split, 1)

                def step(i, b):
                    p = 2 * i + b
                    split_max(i, b, 1)
                    if within(i, p + 2, PAIRS):
                        P = p + 2
                        pool.wait_ge(xt_ready, P + 1)
                        pool.sem_inc(passed, 1)
                        nc.gpsimd.tensor_copy(nodes_of(P), x_t[b][:]).then_inc(x_kept, 1)
                        split(P, 0)
                        split(P, 1)
                    split_max(i, b, 2)

                attend_loop(pool, step)

            @block.scalar
            def _(act):
                act.preload_act_table_set("natural_log_exp_and_others")

                def exp_unit(i, b, k, u):
                    G = 4 * i + 2 * b + k
                    act.wait_ge(st_mm, UNITS * G + u + 1)
                    if due(4 * (G - 1) + u // 2 + 1):
                        act.wait_ge(pv_mm, 4 * (G - 1) + u // 2 + 1)
                    nc.scalar.activation(probs[:, u, :], T_BANK[u % 2][:, :], ACT.Exp).then_inc(exp_done, 1)

                def whole_qk(P, t, src, scale, bias):
                    act.wait_ge(qk_mm, 2 * P + t + 1)
                    if due(2 * P + t - 1):
                        act.wait_ge(qk_split, 2 * P + t - 1)
                    nc.scalar.activation(whole[:, t, :], src[:, :], ACT.Identity, bias=bias, scale=scale)
                    if due(16 * P):
                        act.wait_ge(parts_out, 16 * P)
                    nc.scalar.activation(parts[:, t, 0, :], src[:, :], ACT.Identity, bias=bias,
                                         scale=scale).then_inc(qk_whole, 1)

                def max_copy(i, b, k):
                    G = 4 * i + 2 * b + k
                    if not within(i, G, B):
                        return
                    act.wait_ge(maxt_mm, G + 1)
                    if due(16 * G):
                        act.wait_ge(max_out, 16 * G)
                    nc.scalar.copy(max_t[:], M1[:, :].bitcast(BF16)[0:PARTS * H, 0:N]).then_inc(maxt_ready, 1)

                def inverse_denominators(G):
                    act.wait_ge(den_ready, G + 1)
                    nc.scalar.activation(denom[:], denom[:], ACT.Ln).then_inc(den_ln, 1)
                    act.wait_ge(den_ln, G + 1)
                    if due(G):
                        act.wait_ge(normed, G)
                    nc.scalar.activation(denom_r[:], denom[:], ACT.Exp, scale=-1.0).then_inc(den_inv, 1)

                def step(i, b):
                    p = 2 * i + b
                    for slot in range(2):
                        G = 2 * p + slot
                        for u in range(UNITS):
                            if within(i, G, B):
                                exp_unit(i, b, slot, u)
                            if u == 1:
                                max_copy(i, b, slot + 1)
                            if u == 4 and within(i, G - 1, B):
                                inverse_denominators(G - 1)
                            if slot == 0:
                                P = p + 2
                                if u == 0 and within(i, P, PAIRS):
                                    act.wait_ge(xt_mm, P + 1)
                                    if due(2 * (P - 1)):
                                        act.wait_ge(v_mm, 2 * (P - 1))
                                    if due(P - 1):
                                        act.wait_ge(x_kept, P - 1)
                                    nc.scalar.copy(x_t[b][:], M0[:, :]).then_inc(xt_ready, 1)
                                if u == 2 and within(i, P, PAIRS):
                                    c = COL["L0_gnn_bq"]
                                    whole_qk(P, 0, M0, DH ** -0.5, cols[:, c:c + 1])
                                if u == 3 and within(i, P, PAIRS):
                                    c = COL["L0_gnn_bk"]
                                    whole_qk(P, 1, M1, 1.0, cols[:, c:c + 1])
                                if u == 7 and within(i, p - 1, PAIRS):
                                    act.wait_ge(y_mm, p)
                                    if due(p - 1):
                                        act.wait_ge(ln_done, p - 1)
                                    nc.scalar.activation(ln_y[:], M0[:, :], ACT.Identity, bias=ccols[:, 0:1])
                                    nc.scalar.activation(ln_sq[:], M0[:, :], ACT.Square,
                                                         bias=ccols[:, 0:1]).then_inc(y_read, 1)
                            elif u == 3 and within(i, p - 1, PAIRS):
                                act.wait_ge(var_mm, p)
                                nc.scalar.activation(ln_r[:], M0[:, :], ACT.Ln, bias=eps[:, 0:1]).then_inc(var_ln, 1)
                                act.wait_ge(var_ln, p)
                                nc.scalar.activation(ln_r[:], ln_r[:], ACT.Exp, scale=-0.5).then_inc(rstd, 1)

                attend_loop(act, step)

            def pe_program(pe, more):
                def scores(i, b, k, u):
                    G, n = 4 * i + 2 * b + k, (2 * b + k) % 4
                    if not within(i, G, B):
                        return
                    if u == 0:
                        quarter = i + (2 * b + k) // 4
                        pe.wait_ge(stacked[n], 16 * 2 * TERMS * (quarter + 1))
                    if due(UNITS * G + u - 1):
                        pe.wait_ge(s_max, UNITS * G + u - 1)
                    c = u // 4
                    for j in range(2):
                        h = 2 * (u % 4) + j
                        last = nc.tensor.matmul(S_BANK[u % 2][:, N * j:N * j + N],
                                                q_st[n][0:ROWS, h, 128 * c:128 * c + 128],
                                                k_st[n][0:ROWS, h, :], start=True, stop=True)
                    last.then_inc(s_mm, 1)

                def scores_t(i, b, k, u):
                    G, n = 4 * i + 2 * b + k, (2 * b + k) % 4
                    if not within(i, G, B):
                        return
                    if u == 0:
                        pe.wait_ge(max_in, 16 * (G + 1))
                    if due(UNITS * G + u - 1):
                        pe.wait_ge(exp_done, UNITS * G + u - 1)
                    c = (u // 2) % 2
                    for j in range(2):
                        h = GRP * (u // 4) + 2 * (u % 2) + j
                        last = nc.tensor.matmul(T_BANK[u % 2][:, N * j:N * j + N],
                                                k_st[n][:, h, 128 * c:128 * c + 128],
                                                q_st[n][:, h, :], start=True, stop=True)
                    last.then_inc(st_mm, 1)

                def values(i, b, k, q):
                    G = 4 * i + 2 * b + k
                    if not within(i, G, B):
                        return
                    par, gi = (b + k // 2) % 2, k % 2
                    pe.wait_ge(masked, UNITS * G + 2 * q + 2)
                    if q == 0:
                        if due(G - 1):
                            pe.wait_ge(normed, G - 1)
                        pe.wait_ge(v_ready1, 2 * i + b + k // 2 + 1)
                        if more:
                            pe.wait_ge(vmore_ready, 4 * (2 * i + b + k // 2 + 1))
                    grp, c = q // 2, q % 2
                    terms = 2 + (R - 1 if more else 0)
                    for term in range(terms):
                        for g in range(GRP):
                            h = GRP * grp + g
                            u = 4 * grp + 2 * c + g // 2
                            cut = slice(N * (g % 2), N * (g % 2) + N)
                            if term == 0:
                                w, m, rhs = v_base[par][:, gi, c, h, :], 32, probs[:, u, cut]
                            elif term == 1:
                                w, m, rhs = v_one[par][:, gi, c, h, :], DH, probs_one[:, u, cut]
                            else:
                                w, m, rhs = (v_more[par][:, gi, c, term - 2, h, :], DH,
                                             probs_more[:, term - 2, u % 2, cut])
                            last = nc.tensor.matmul(PV_BANK[k % 2][32 * g:32 * g + m, N * grp:N * grp + N], w, rhs,
                                                    start=(c == 0 and term == 0),
                                                    stop=(c == NC - 1 and term == terms - 1))
                    last.then_inc(pv_mm, 1)

                def turn_max(i, b, k):
                    G = 4 * i + 2 * b + k
                    if not within(i, G, B):
                        return
                    pe.wait_ge(max_split, G + 1)
                    for c in range(NC):
                        last = nc.tensor.transpose(M1[:, :].bitcast(BF16)[0:PARTS * H, 128 * c:128 * c + 128],
                                                   max_parts[:, c, :, :].rearrange("p s h -> p (s h)"), identb[:])
                    last.then_inc(maxt_mm, 1)

                def make_values(Q, par, gi, bk):
                    for c in range(NC):
                        last = nc.tensor.matmul(bk[:, 2 * D * c:2 * D * c + 2 * D],
                                                x_t[par][:, N * gi + 128 * c:N * gi + 128 * c + 128],
                                                wv[:, 0:2, :].rearrange("p r d -> p (r d)"), start=True, stop=True)
                    last.then_inc(v_mm, 1)

                def make_more(Q, par):
                    for n in range(4):
                        bk = (M1, M0)[n % 2]
                        if n < 2:
                            pe.wait_ge((v_ready0, v_ready1)[n], Q + 1)
                        else:
                            pe.wait_ge(vmore_ready, 4 * Q + n - 1)
                        nc.tensor.matmul(bk[:, 0:(R - 1) * D], x_t[par][:, 128 * n:128 * n + 128],
                                         wv[:, 2:R + 1, :].rearrange("p r d -> p (r d)"), start=True,
                                         stop=True).then_inc(vmore_mm, 1)

                def step(i, b):
                    p = 2 * i + b
                    for slot in range(2):
                        G = 2 * p + slot
                        for u in range(UNITS):
                            scores(i, b, slot + 2, u)
                            scores_t(i, b, slot, u)
                            if u == 0:
                                values(i, b, slot - 1, 2)
                            if u == 2:
                                values(i, b, slot - 1, 3)
                            if u == 4:
                                values(i, b, slot, 0)
                            if u == 6:
                                values(i, b, slot, 1)
                            P, Q = p + 2, p + 1
                            if slot == 0:
                                if u == 0 and within(i, P, PAIRS):
                                    half = i + (b + 2) // 2
                                    pe.wait_ge(x_in[b], 16 * (half + 1))
                                    if due(P - 1):
                                        pe.wait_ge(v_ready1, P - 1)
                                    if isinstance(i, int):
                                        if due(2 * (P - 1)):
                                            pe.wait_ge(qk_whole, 2 * (P - 1))
                                    if more:
                                        if due(4 * (P - 1)):
                                            pe.wait_ge(vmore_ready, 4 * (P - 1))
                                    for n in range(2 * NC):
                                        last = nc.tensor.transpose(M0[:, 128 * n:128 * n + 128], x_nat[b][:, n, :],
                                                                   ident[:])
                                    last.then_inc(xt_mm, 1)
                                if u == 1:
                                    if within(i, G + 1, B):
                                        pe.wait_ge(v_ready0, p + 1)
                                        if more:
                                            pe.wait_ge(vmore_ready, 4 * (p + 1))
                                    turn_max(i, b, 1)
                                if u == 2 and within(i, P, PAIRS):
                                    pe.wait_ge(xt_ready, P + 1)
                                    nc.tensor.matmul(M0[:, :], wq[:], x_t[b][:], start=True, stop=True).then_inc(qk_mm, 1)
                                if u == 3 and within(i, P, PAIRS):
                                    if within(i, G + 1, B):
                                        pe.wait_ge(maxt_ready, G + 2)
                                    nc.tensor.matmul(M1[:, :], wk[:], x_t[b][:], start=True, stop=True).then_inc(qk_mm, 1)
                                if u == 7 and within(i, p - 1, PAIRS):
                                    if within(i, P, PAIRS):
                                        pe.wait_ge(qk_whole, 2 * P + 1)
                                    else:
                                        pe.wait_ge(v_ready1, at_most(p + 1, PAIRS))
                                        pe.wait_ge(var_ln, p - 1)
                                    pe.wait_ge(normed, 2 * p)
                                    pe.wait_ge(x_kept, p)
                                    for n in range(2):
                                        nc.tensor.matmul(M0[:, :], wo[:, n, :], mixed[:, n, :], start=(n == 0),
                                                         stop=False)
                                    nc.tensor.matmul(M0[:, :], centre[:], nodes_of(p - 1), start=False,
                                                     stop=True).then_inc(y_mm, 1)
                            else:
                                if u == 1:
                                    if within(i, G + 1, B):
                                        if within(i, P, PAIRS):
                                            pe.wait_ge(qk_whole, 2 * P + 2)
                                        elif within(i, G, B):
                                            pe.wait_ge(maxt_ready, G + 1)
                                    turn_max(i, b, 2)
                                if u == 2 and within(i, p - 1, PAIRS):
                                    pe.wait_ge(y_read, p)
                                    nc.tensor.matmul(M0[:, :], mean_w[:], ln_sq[:], start=True, stop=True).then_inc(var_mm, 1)
                                if u == 4 and within(i, Q, PAIRS):
                                    pe.wait_ge(xt_ready, Q + 1)
                                    pe.wait_ge(maxt_ready, G + 2)
                                    make_values(Q, (b + 1) % 2, 0, M1)
                                if u == 6 and within(i, Q, PAIRS):
                                    if due(p):
                                        pe.wait_ge(var_ln, p)
                                    if within(i, P, PAIRS):
                                        pe.wait_ge(qk_whole, 2 * P + 1)
                                    make_values(Q, (b + 1) % 2, 1, M0)
                                if u == 7 and more and within(i, Q, PAIRS):
                                    make_more(Q, (b + 1) % 2)

                pe.wait_ge(ones_init, 4)
                attend_loop(pe, step)

            def dve_program(dve, more):
                def reduce_max(i, b, k, u):
                    G = 4 * i + 2 * b + k
                    if not within(i, G, B):
                        return
                    dve.wait_ge(s_mm, UNITS * G + u + 1)
                    if u == 0:
                        if due(G - 1):
                            dve.wait_ge(max_split, G - 1)
                    c, hp = u // 4, u % 4
                    nc.vector.tensor_reduce(row_max[k % 2][:, c, 2 * hp:2 * hp + 2],
                                            S_BANK[u % 2][:, :].rearrange("p (h j) -> p h j", h=2), AX,
                                            ALU.max).then_inc(s_max, 1)

                def mask(i, b, k, u):
                    G = 4 * i + 2 * b + k
                    if not within(i, G, B):
                        return
                    dve.wait_ge(exp_done, UNITS * G + u + 1)
                    if due(4 * (G - 1) + u // 2 + 1):
                        dve.wait_ge(pv_mm, 4 * (G - 1) + u // 2 + 1)
                    code = codes[:, bass.ds(G, 1), (u // 2) % 2, :].broadcast_to([128, 2, N])
                    src = probs[:, u, :].rearrange("p (h i) -> p h i", h=2)
                    dst = probs_one[:, u, :].rearrange("p (h i) -> p h i", h=2)
                    one = nc.vector.scalar_tensor_tensor(out=dst, in0=code, scalar=1.0, in1=src, op0=ALU.is_equal,
                                                         op1=ALU.mult)
                    if more:
                        if due(4 * G + u // 2):
                            dve.wait_ge(pv_mm, 4 * G + u // 2)
                        for r in range(2, R):
                            dst = probs_more[:, r - 2, u % 2, :].rearrange("p (h i) -> p h i", h=2)
                            nc.vector.scalar_tensor_tensor(out=dst, in0=code, scalar=float(r), in1=src,
                                                           op0=ALU.is_equal, op1=ALU.mult)
                        last = probs_more[:, R - 2, u % 2, :]
                        dst = last.rearrange("p (h i) -> p h i", h=2)
                        nc.vector.scalar_tensor_tensor(out=dst, in0=code, scalar=0.0, in1=src, op0=ALU.is_lt,
                                                       op1=ALU.mult).then_inc(more_done, 1)
                        dve.wait_ge(more_done, 2 * (UNITS * G + u) + 1)
                        tmp = more_tmp[:, :].rearrange("p (h i) -> p h i", h=2)
                        nc.vector.scalar_tensor_tensor(out=tmp, in0=code, scalar=float(R), in1=src, op0=ALU.is_ge,
                                                       op1=ALU.mult).then_inc(more_done, 1)
                        dve.wait_ge(more_done, 2 * (UNITS * G + u) + 2)
                        nc.vector.tensor_tensor(last, last, more_tmp[:, :], ALU.add).then_inc(masked, 1)
                    else:
                        one.then_inc(masked, 1)

                def spread_denominators(G, k):
                    dve.wait_ge(pv_mm, 4 * (G + 1))
                    if due(G):
                        dve.wait_ge(den_inv, G)
                        dve.sem_inc(passed, 1)
                    nc.vector.stream_shuffle(denom[:], PV_BANK[k % 2][:, :], [DH] * 32).then_inc(den_ready, 1)

                def normalize(i, b, k):
                    G = 4 * i + 2 * b + k
                    gi = k % 2
                    dve.wait_ge(den_inv, G + 1)
                    if due(2 * i + b + k // 2):
                        dve.wait_ge(y_mm, 2 * i + b + k // 2)
                    nc.vector.tensor_tensor(mixed[:, :, N * gi:N * gi + N],
                                            PV_BANK[k % 2][:, :].rearrange("p (n i) -> p n i", n=2),
                                            denom_r[:].rearrange("p (n i) -> p n i", n=2), ALU.mult).then_inc(normed, 1)

                def keep_values(Q, par, gi, bk, done):
                    dve.wait_ge(v_mm, 2 * Q + gi + 1)
                    if due(4 * (2 * Q - 2)):
                        dve.wait_ge(pv_mm, 4 * (2 * Q - 2))
                    src = bk[:, :].rearrange("p (c r h d) -> p c r h d", c=NC, r=2, h=H)
                    for r in range(2):
                        dst = v_base[par][:, gi, :, :, 0:DH] if r == 0 else v_one[par][:, gi, :, :, :]
                        for c in range(NC):
                            last = nc.vector.tensor_tensor(dst[:, c], src[:, c, r],
                                                           bvb[:, r, :].rearrange("p (h d) -> p h d", h=H), ALU.add)
                    last.then_inc(done, 1)

                def keep_more(Q, par):
                    for n in range(4):
                        dve.wait_ge(vmore_mm, 4 * Q + n + 1)
                        nc.vector.tensor_tensor(v_more[par][:, n // 2, n % 2].rearrange("p r h d -> p (r h d)"),
                                                (M1, M0)[n % 2][:, 0:(R - 1) * D],
                                                bvb[:, 2:R + 1, :].rearrange("p r d -> p (r d)"),
                                                ALU.add).then_inc(vmore_ready, 1)

                def step(i, b):
                    p = 2 * i + b
                    for slot in range(2):
                        G = 2 * p + slot
                        for u in range(UNITS):
                            reduce_max(i, b, slot + 2, u)
                            if u == 0:
                                mask(i, b, slot - 1, UNITS - 1)
                            else:
                                mask(i, b, slot, u - 1)
                            if u == 3 and within(i, G - 1, B):
                                spread_denominators(G - 1, slot - 1)
                            if u == 6 and within(i, G - 1, B):
                                normalize(i, b, slot - 1)
                            Q = p + 1
                            if slot == 1:
                                if u == 5 and within(i, p - 1, PAIRS):
                                    dve.wait_ge(rstd, p)
                                    nc.vector.tensor_tensor(ln_y[:], ln_y[:], ln_r[:], ALU.mult).then_inc(ln_mid, 1)
                                    dve.wait_ge(ln_mid, p)
                                    g = COL["L0_gnn_g1"]
                                    nc.vector.tensor_scalar(nodes_of(p - 1), ln_y[:], cols[:, g:g + 1],
                                                            cols[:, g + 1:g + 2], ALU.mult, ALU.add).then_inc(ln_done, 1)
                                if u == 6 and within(i, Q, PAIRS):
                                    keep_values(Q, (b + 1) % 2, 0, M1, v_ready0)
                                if u == 7 and within(i, Q, PAIRS):
                                    keep_values(Q, (b + 1) % 2, 1, M0, v_ready1)
                                    if more:
                                        keep_more(Q, (b + 1) % 2)

                for n in range(2):
                    nc.vector.memset(v_base[n][:, :, :, :, DH:32], 1.0)
                attend_loop(dve, step)

            @block.tensor
            def _(pe):
                odd_one = pe.value_load(flag[0:1, 0:1])
                with pe.If(odd_one > 0):
                    pe_program(pe, True)
                with pe.Else():
                    pe_program(pe, False)
                pe.wait_ge(ln_done, PAIRS)

            @block.vector
            def _(dve):
                odd_one = dve.value_load(flag[0:1, 0:1])
                with dve.If(odd_one > 0):
                    dve_program(dve, True)
                with dve.Else():
                    dve_program(dve, False)
                dve.wait_ge(ln_done, PAIRS)
        attend_ctx.close()

        hidden_bias = sb("hidden_bias", [128, B, NC, N], BF16)
        ff_ctx = ExitStack()
        hid = [sb(f"hid{n}", [128, FC, W2G], F32, ff_ctx) for n in range(2)]

        def ff_pe_hidden(pe, i, b, s, w):
            p = 2 * i + b
            if within(i, p, PAIRS):
                for c in range(FC):
                    if due(FC * (p - 1) + c + 1):
                        pe.wait_ge(s["hid_act"], FC * (p - 1) + c + 1)
                    nc.tensor.matmul(bank[c][:, :], w[:, 128 * c:128 * c + 128], nodes_of(p), start=True,
                                     stop=True).then_inc(s["hid_mm"], 1)

        def ff_pe_out(pe, i, b, s, w):
            p = 2 * i + b
            if within(i, p - 1, PAIRS):
                if due(p - 2):
                    pe.wait_ge(s["y_read"], p - 2)
                for c in range(FC):
                    pe.wait_ge(s["hid_act"], FC * (p - 1) + c + 1)
                    nc.tensor.matmul(bank[4 + (b + 1) % 2][:, :], w[:, c, :], hid[(b + 1) % 2][:, c, :],
                                     start=(c == 0), stop=False)
                nc.tensor.matmul(bank[4 + (b + 1) % 2][:, :], centre[:], nodes_of(p - 1), start=False,
                                 stop=True).then_inc(s["y_mm"], 1)

        def ff_act_hidden(act, i, b, s, func, col):
            p = 2 * i + b
            if within(i, p, PAIRS):
                for c in range(FC):
                    act.wait_ge(s["hid_mm"], FC * p + c + 1)
                    if c == 0:
                        if due(p - 1):
                            act.wait_ge(s["y_mm"], p - 1)
                    nc.scalar.activation(hid[b][:, c, :], bank[c][:, :], func,
                                         bias=cols[:, col + c:col + c + 1]).then_inc(s["hid_act"], 1)

        s1 = {name: sem(f"f1_{name}") for name in ("hid_mm", "hid_act", "y_mm", "y_read")}
        hb_done = sem("hb_done")
        with nc.Block() as block:
            @block.tensor
            def _(pe):
                def step(i, b):
                    ff_pe_hidden(pe, i, b, s1, w1)
                    ff_pe_out(pe, i, b, s1, w2)
                pair_loop(pe, step, 0, 1, PAIRS // 2, PAIRS + 1)

            @block.scalar
            def _(act):
                pair_loop(act, lambda i, b: ff_act_hidden(act, i, b, s1, ACT.Gelu, COL_B1), 0, 1, PAIRS // 2,
                          PAIRS)

            @block.vector
            def _(dve):
                def step(i, b):
                    p = 2 * i + b
                    if within(i, p, PAIRS):
                        nc.vector.tensor_scalar(hidden_bias[:, bass.ds(2 * p, 2)].rearrange("p g c i -> p (g c i)"),
                                                codes[:, bass.ds(2 * p, 2)].rearrange("p g c i -> p (g c i)"), 0.0,
                                                HIDDEN, ALU.is_le, ALU.mult).then_inc(hb_done, 1)
                    if within(i, p - 1, PAIRS):
                        dve.wait_ge(s1["y_mm"], p)
                        nc.vector.tensor_scalar(nodes_of(p - 1), bank[4 + (b + 1) % 2][:, :], ccols[:, 1:2], None,
                                                ALU.add).then_inc(s1["y_read"], 1)
                pair_loop(dve, step, 0, 1, PAIRS // 2, PAIRS + 1)
        ff_ctx.close()

        gat_ctx = ExitStack()
        G_ = lambda name, shape, dt=F32: sb(name, shape, dt, gat_ctx)
        sq_a, sq_b = G_("sq_a", [128, W2G]), G_("sq_b", [128, W2G])
        r_a, r_b = G_("r_a", [128, W2G]), G_("r_b", [128, W2G])
        mid_a, y_b = G_("mid_a", [128, W2G]), G_("y_b", [128, W2G])
        hop_in = [[G_(f"hop_in{h}{n}", [128, W2G]) for n in range(2)] for h in range(2)]
        logits = [G_(f"logits{h}", [128, 2 * NC, N]) for h in range(2)]
        att = [G_(f"att{h}", [128, 2 * NC, N]) for h in range(2)]
        wh = [G_(f"wh{h}", [128, 2 * NC, D]) for h in range(2)]
        top = [G_(f"top{h}", [128, 2 * NC]) for h in range(2)]
        wh2 = [G_(f"wh2{h}", [128, 2 * NC]) for h in range(2)]
        shift = [G_(f"shift{h}", [128, 2, 2 * NC]) for h in range(2)]
        hidden_now = [G_(f"hidden_now{h}", [128, 2 * NC, N], BF16) for h in range(2)]
        total = [G_(f"total{h}", [128, 2 * NC]) for h in range(2)]
        inv = [G_(f"inv{h}", [128, 2 * NC]) for h in range(2)]
        per_hop = lambda name: [sem(f"g_{name}{h}") for h in range(2)]
        bc_mm, wh_mm, summed, shifted, exped, whs, out_mm = (per_hop(n) for n in (
            "bc_mm", "wh_mm", "summed", "shifted", "exped", "whs", "out_mm"))
        hop_ready = per_hop("hop_ready")
        hidden_here = per_hop("hidden_here")
        x2_kept, y3_read = sem("x2_kept"), sem("y3_read")
        sq_ready = sem("g_sq_ready")
        gvar_mm, gvar_ln, grstd, gmid, gln = (per_hop(n) for n in (
            "gvar_mm", "gvar_ln", "grstd", "gmid", "gln"))
        small = sem("small")
        BC, WH, OUTB, VARB = (bank[0], bank[3]), (bank[1:3], bank[4:6]), bank[6], bank[7]
        gat_loop = lambda eng, step: pair_loop(eng, step, 0, 2, PAIRS // 2, PAIRS + 3)

        with nc.Block() as block:
            @block.tensor
            def _(pe):
                def front(i, b, hop):
                    p = 2 * i + b
                    P, par = p - 1 - hop, (b + 1 + hop) % 2
                    if not within(i, P, PAIRS):
                        return
                    pe.wait_ge(hop_ready[hop], P + 1)
                    if due(P):
                        pe.wait_ge(summed[hop], P)
                    nc.tensor.matmul(BC[hop][:, :], ga[:, hop, :], hop_in[hop][par][:], start=True,
                                     stop=True).then_inc(bc_mm[hop], 1)
                    if due(P):
                        pe.wait_ge(whs[hop], P)
                    for g in range(2):
                        for c in range(NC):
                            last = nc.tensor.matmul(WH[hop][g][:, (D + 1) * c:(D + 1) * c + D + 1],
                                                    hop_in[hop][par][:, N * g + 128 * c:N * g + 128 * c + 128],
                                                    gw[:, hop, :], start=True, stop=True)
                    last.then_inc(wh_mm[hop], 1)

                def back(i, b, hop):
                    p = 2 * i + b
                    P = p - 1 - 2 * hop
                    if not within(i, P, PAIRS):
                        return
                    pe.wait_ge(whs[hop], P + 1)
                    if hop == 0:
                        if due(P - 1):
                            pe.wait_ge(y3_read, P - 1)
                    else:
                        pe.wait_ge(hop_ready[1], at_most(P + 2, PAIRS))
                        pe.wait_ge(x2_kept, P + 1)
                        nc.tensor.matmul(OUTB[:, :], centre[:], nodes_of(P), start=True, stop=False)
                    for g in range(2):
                        for c in range(NC):
                            last = nc.tensor.matmul(OUTB[:, N * g:N * g + N], wh[hop][:, NC * g + c, :],
                                                    att[hop][:, NC * g + c, :], start=(hop == 0 and c == 0),
                                                    stop=(c == NC - 1 and (hop == 0 or g == 1)))
                    last.then_inc(out_mm[hop], 1)

                def variance(i, b, n):
                    p = 2 * i + b
                    P = p - 3 * n
                    if not within(i, P, PAIRS):
                        return
                    pe.wait_ge((sq_ready, y3_read)[n], P + 1)
                    if n == 0:
                        if due(p - 3):
                            pe.wait_ge(gvar_ln[1], p - 3)
                    else:
                        pe.wait_ge(gvar_ln[0], at_most(p + 1, PAIRS))
                    nc.tensor.matmul(VARB[:, :], mean_w[:], (sq_a, sq_b)[n][:], start=True,
                                     stop=True).then_inc(gvar_mm[n], 1)

                def step(i, b):
                    front(i, b, 0)
                    variance(i, b, 0)
                    back(i, b, 1)
                    front(i, b, 1)
                    variance(i, b, 1)
                    back(i, b, 0)

                gat_loop(pe, step)

            @block.scalar
            def _(act):
                act.preload_act_table_set("natural_log_exp_and_others")

                def exps(i, b, hop):
                    p = 2 * i + b
                    P = p - 1 - hop
                    if not within(i, P, PAIRS):
                        return
                    act.wait_ge(shifted[hop], P + 1)
                    if due(P):
                        act.wait_ge(out_mm[hop], P)
                    for side, scale, dst in ((0, 1.0, att), (1, SLOPE, logits)):
                        for n in range(2 * NC):
                            last = nc.scalar.activation(dst[hop][:, n, :], logits[hop][:, n, :], ACT.Exp,
                                                        bias=shift[hop][:, side, n:n + 1], scale=scale)
                    last.then_inc(exped[hop], 1)

                def inverse_std(i, b, n):
                    p = 2 * i + b
                    P = p - 3 * n
                    if not within(i, P, PAIRS):
                        return
                    r = (r_a, r_b)[n]
                    act.wait_ge(gvar_mm[n], P + 1)
                    if due(P):
                        act.wait_ge(gmid[n], P)
                    nc.scalar.activation(r[:], VARB[:, :], ACT.Ln, bias=eps[:, 0:1]).then_inc(gvar_ln[n], 1)
                    act.wait_ge(gvar_ln[n], P + 1)
                    nc.scalar.activation(r[:], r[:], ACT.Exp, scale=-0.5).then_inc(grstd[n], 1)

                def step(i, b):
                    p = 2 * i + b
                    if within(i, p, PAIRS):
                        if due(p):
                            act.wait_ge(gvar_mm[0], p)
                        nc.scalar.activation(sq_a[:], nodes_of(p), ACT.Square).then_inc(sq_ready, 1)
                    exps(i, b, 0)
                    inverse_std(i, b, 0)
                    if within(i, p - 3, PAIRS):
                        act.wait_ge(out_mm[1], p - 2)
                        if due(p - 3):
                            act.wait_ge(gln[1], p - 3)
                        nc.scalar.copy(y_b[:], OUTB[:, :])
                        nc.scalar.activation(sq_b[:], OUTB[:, :], ACT.Square).then_inc(y3_read, 1)
                    exps(i, b, 1)
                    inverse_std(i, b, 1)
                    if within(i, p - 1, PAIRS):
                        act.wait_ge(out_mm[0], p)
                        if due(p - 2):
                            act.wait_ge(wh_mm[1], p - 2)
                        nc.scalar.copy(hop_in[1][(b + 1) % 2][:], OUTB[:, :]).then_inc(hop_ready[1], 1)

                gat_loop(act, step)

            @block.gpsimd
            def _(pool):
                def step(i, b):
                    p = 2 * i + b
                    if within(i, p, PAIRS):
                        pool.wait_ge(hop_ready[0], p + 1)
                        pool.sem_inc(passed, 1)
                        nc.gpsimd.tensor_copy(nodes_of(p), hop_in[0][b][:]).then_inc(x2_kept, 1)
                pair_loop(pool, step, 0, 2, PAIRS // 2, PAIRS)

            @block.vector
            def _(dve):
                def score(i, b, hop):
                    p = 2 * i + b
                    P = p - 1 - hop
                    if not within(i, P, PAIRS):
                        return
                    nc.vector.tensor_copy(hidden_now[hop][:].rearrange("p n i -> p (n i)"),
                                          hidden_bias[:, bass.ds(2 * P, 2)].rearrange(
                                              "p g c i -> p (g c i)")).then_inc(hidden_here[hop], 1)
                    dve.wait_ge(hidden_here[hop], P + 1)
                    dve.sem_inc(passed, 1)
                    dve.wait_ge(bc_mm[hop], P + 1)
                    dve.sem_inc(passed, 1)
                    for g in range(2):
                        for c in range(NC):
                            n = NC * g + c
                            last = nc.vector.tensor_tensor_reduce(
                                logits[hop][:, n, :], BC[hop][:, N * g:N * g + N],
                                hidden_now[hop][:, n, :], 1.0,
                                -3.0e38, ALU.add, ALU.max, top[hop][:, n:n + 1])
                    last.then_inc(summed[hop], 1)
                    dve.wait_ge(wh_mm[hop], P + 1)
                    for g in range(2):
                        last = nc.vector.tensor_copy(wh2[hop][:, NC * g:NC * g + NC],
                                                     WH[hop][g][:, D:NC * (D + 1):D + 1])
                    last.then_inc(chain[hop], 1)
                    dve.wait_ge(chain[hop], 3 * P + 1)
                    nc.vector.tensor_tensor(top[hop][:], top[hop][:], wh2[hop][:], ALU.add).then_inc(chain[hop], 1)
                    dve.wait_ge(chain[hop], 3 * P + 2)
                    nc.vector.scalar_tensor_tensor(out=top[hop][:], in0=top[hop][:], scalar=SLOPE, in1=top[hop][:],
                                                   op0=ALU.mult, op1=ALU.max).then_inc(chain[hop], 1)
                    dve.wait_ge(chain[hop], 3 * P + 3)
                    nc.vector.tensor_tensor(shift[hop][:, 0, :], wh2[hop][:], top[hop][:], ALU.subtract)
                    nc.vector.scalar_tensor_tensor(out=shift[hop][:, 1, :], in0=wh2[hop][:], scalar=SLOPE,
                                                   in1=top[hop][:], op0=ALU.mult,
                                                   op1=ALU.subtract).then_inc(shifted[hop], 1)

                def weigh(i, b, hop):
                    p = 2 * i + b
                    P = p - 1 - 2 * hop
                    if not within(i, P, PAIRS):
                        return
                    dve.wait_ge(exped[hop], P + 1)
                    for n in range(2 * NC):
                        last = nc.vector.scalar_tensor_tensor(out=att[hop][:, n, :], in0=att[hop][:, n, :], scalar=1.0,
                                                              in1=logits[hop][:, n, :], op0=ALU.mult, op1=ALU.max,
                                                              accum_out=total[hop][:, n:n + 1])
                    last.then_inc(chain2[hop], 1)
                    dve.wait_ge(chain2[hop], 2 * P + 1)
                    nc.vector.reciprocal(inv[hop][:], total[hop][:]).then_inc(chain2[hop], 1)
                    dve.wait_ge(chain2[hop], 2 * P + 2)
                    for g in range(2):
                        for c in range(NC):
                            n = NC * g + c
                            last = nc.vector.tensor_scalar(wh[hop][:, n, :], WH[hop][g][:, (D + 1) * c:(D + 1) * c + D],
                                                           inv[hop][:, n:n + 1], None, ALU.mult)
                    last.then_inc(whs[hop], 1)

                chain, chain2 = per_hop("chain"), per_hop("chain2")

                def step(i, b):
                    p = 2 * i + b
                    score(i, b, 0)
                    if within(i, p, PAIRS):
                        dve.wait_ge(grstd[0], p + 1)
                        if due(p - 1):
                            dve.wait_ge(wh_mm[0], p - 1)
                        if due(p - 1):
                            dve.wait_ge(x2_kept, p - 1)
                        nc.vector.tensor_tensor(mid_a[:], nodes_of(p), r_a[:], ALU.mult).then_inc(gmid[0], 1)
                        dve.wait_ge(gmid[0], p + 1)
                        g = COL["L0_gnn_g2"]
                        nc.vector.tensor_scalar(hop_in[0][b][:], mid_a[:], cols[:, g:g + 1], cols[:, g + 1:g + 2],
                                                ALU.mult, ALU.add).then_inc(hop_ready[0], 1)
                    weigh(i, b, 1)
                    score(i, b, 1)
                    if within(i, p - 3, PAIRS):
                        dve.wait_ge(grstd[1], p - 2)
                        nc.vector.tensor_tensor(y_b[:], y_b[:], r_b[:], ALU.mult).then_inc(gmid[1], 1)
                        dve.wait_ge(gmid[1], p - 2)
                        g = COL["L1_gnn_g_ln1"]
                        nc.vector.tensor_scalar(nodes_of(p - 3), y_b[:], cols[:, g:g + 1], cols[:, g + 1:g + 2],
                                                ALU.mult, ALU.add).then_inc(gln[1], 1)
                    weigh(i, b, 0)

                gat_loop(dve, step)
        gat_ctx.close()

        ff_ctx = ExitStack()
        F_ = lambda name, shape, dt=F32: sb(name, shape, dt, ff_ctx)
        hid = [F_(f"hid_r{n}", [128, FC, W2G]) for n in range(2)]
        fy, fsq, fr, fmid, fo = (F_(n, [128, W2G]) for n in ("fy", "fsq", "fr", "fmid", "fo"))
        o_nat = [F_(f"o_nat{n}", [128, 2 * NC, D]) for n in range(2)]
        s2 = {name: sem(f"f2_{name}") for name in ("hid_mm", "hid_act", "y_mm", "y_read", "var_mm", "var_ln", "rstd",
                                                  "mid", "normed", "o_mm", "o_ready")}
        o_out = [sem(f"o_out{n}") for n in range(2)]
        last_loop = lambda eng, step: pair_loop(eng, step, 0, 2, PAIRS // 2, PAIRS + 3)

        with nc.Block() as block:
            @block.tensor
            def _(pe):
                def step(i, b):
                    p = 2 * i + b
                    ff_pe_hidden(pe, i, b, s2, wf1)
                    if within(i, p - 2, PAIRS):
                        pe.wait_ge(s2["y_read"], p - 1)
                        if due(p - 2):
                            pe.wait_ge(s2["var_ln"], p - 2)
                        nc.tensor.matmul(bank[6][:, :], mean_w[:], fsq[:], start=True, stop=True).then_inc(s2["var_mm"], 1)
                    ff_pe_out(pe, i, b, s2, wf2)
                    if within(i, p - 3, PAIRS):
                        pe.wait_ge(s2["normed"], p - 2)
                        if due(p - 3):
                            pe.wait_ge(s2["o_ready"], p - 3)
                        for n in range(2 * NC):
                            last = nc.tensor.transpose(bank[7][:, 128 * n:128 * n + 128], fo[:, 128 * n:128 * n + 128],
                                                       ident[:])
                        last.then_inc(s2["o_mm"], 1)
                last_loop(pe, step)

            @block.scalar
            def _(act):
                act.preload_act_table_set("natural_log_exp_and_others")

                def step(i, b):
                    p = 2 * i + b
                    ff_act_hidden(act, i, b, s2, ACT.Relu, COL_BFF1)
                    if within(i, p - 2, PAIRS):
                        act.wait_ge(s2["var_mm"], p - 1)
                        if due(p - 2):
                            act.wait_ge(s2["mid"], p - 2)
                        nc.scalar.activation(fr[:], bank[6][:, :], ACT.Ln, bias=eps[:, 0:1]).then_inc(s2["var_ln"], 1)
                        act.wait_ge(s2["var_ln"], p - 1)
                        nc.scalar.activation(fr[:], fr[:], ACT.Exp, scale=-0.5).then_inc(s2["rstd"], 1)
                    if within(i, p - 1, PAIRS):
                        act.wait_ge(s2["y_mm"], p)
                        if due(at_most(p - 1, PAIRS)):
                            act.wait_ge(s2["mid"], at_most(p - 1, PAIRS))
                        if due(p - 1):
                            act.wait_ge(s2["var_mm"], p - 1)
                        nc.scalar.activation(fy[:], bank[4 + (b + 1) % 2][:, :], ACT.Identity, bias=ccols[:, 2:3])
                        nc.scalar.activation(fsq[:], bank[4 + (b + 1) % 2][:, :], ACT.Square,
                                             bias=ccols[:, 2:3]).then_inc(s2["y_read"], 1)
                last_loop(act, step)

            @block.vector
            def _(dve):
                def step(i, b):
                    p = 2 * i + b
                    if within(i, p - 2, PAIRS):
                        dve.wait_ge(s2["rstd"], p - 1)
                        if due(p - 2):
                            dve.wait_ge(s2["normed"], p - 2)
                        nc.vector.tensor_tensor(fmid[:], fy[:], fr[:], ALU.mult).then_inc(s2["mid"], 1)
                        dve.wait_ge(s2["mid"], p - 1)
                        if due(p - 2):
                            dve.wait_ge(s2["o_mm"], p - 2)
                        g = COL["L1_gnn_g_ln2"]
                        nc.vector.tensor_scalar(fo[:], fmid[:], cols[:, g:g + 1], cols[:, g + 1:g + 2], ALU.mult,
                                                ALU.add).then_inc(s2["normed"], 1)
                    if within(i, p - 3, PAIRS):
                        dve.wait_ge(s2["o_mm"], p - 2)
                        half = i + (b - 5) // 2
                        if due(16 * (half + 1)):
                            dve.wait_ge(o_out[(b + 1) % 2], 16 * (half + 1))
                        nc.vector.tensor_copy(o_nat[(b + 1) % 2][:].rearrange("p n d -> p (n d)"),
                                              bank[7][:, :]).then_inc(s2["o_ready"], 1)
                last_loop(dve, step)

            @block.sync
            def _(sp):
                def step(i, b):
                    p = 2 * i + b
                    if within(i, p - 3, PAIRS):
                        sp.wait_ge(s2["o_ready"], p - 2)
                        sp.sem_inc(passed, 1)
                        sp.dma_start(out[bass.ds(2 * (p - 3), 2)].rearrange("g (c p) d -> p (g c) d", c=NC),
                                     o_nat[(b + 1) % 2][:]).then_inc(o_out[(b + 1) % 2], 16)
                last_loop(sp, step)
                for n in range(2):
                    sp.wait_ge(o_out[n], 16 * PAIRS // 2)
        ff_ctx.close()


_INS = ["x", "adj", "L0_gnn_Wq", "L0_gnn_bq", "L0_gnn_Wk", "L0_gnn_bk", "L0_gnn_Wv", "L0_gnn_bv", "L0_gnn_Wo",
        "L0_gnn_bo", "L0_gnn_W1", "L0_gnn_b1", "L0_gnn_W2", "L0_gnn_b2", "L0_gnn_g1", "L0_gnn_beta1", "L0_gnn_g2",
        "L0_gnn_beta2", "L1_gnn_W1", "L1_gnn_a1", "L1_gnn_W2", "L1_gnn_a2", "L1_gnn_w_ff1", "L1_gnn_b_ff1",
        "L1_gnn_w_ff2", "L1_gnn_b_ff2", "L1_gnn_g_ln1", "L1_gnn_b_ln1", "L1_gnn_g_ln2", "L1_gnn_b_ln2"]


def kernel(**inputs):
    import numpy as _np
    import concourse.bacc as _bacc
    from concourse import mybir as _mybir
    from concourse.bass_utils import run_bass_kernel_spmd as _run

    nc = _bacc.Bacc("TRN2", target_bir_lowering=False, num_devices=1)
    arrays, args = {}, {}
    for name in _INS:
        arr = _np.ascontiguousarray(inputs[name])
        arrays[f"in_{name}"] = arr
        args[name] = nc.dram_tensor(f"in_{name}", arr.shape, _mybir.dt.from_np(arr.dtype), kind="ExternalInput").ap()
    out = nc.dram_tensor("out_0", (B, N, D), _mybir.dt.float32, kind="ExternalOutput").ap()
    build(nc, args, out)
    r = _run(nc, [arrays], core_ids=[0])
    return r.results[0]["out_0"]
```

```python
from contextlib import ExitStack

import concourse.bass as bass
from concourse import mybir

F32 = mybir.dt.float32
BF16 = mybir.dt.bfloat16
I32 = mybir.dt.int32
I8 = mybir.dt.int8
ALU = mybir.AluOpType
ACT = mybir.ActivationFunctionType
AX = mybir.AxisListType.X
RMAX = bass.bass_isa.ReduceOp.max

B, N, D = 32, 256, 128
H, DH = 8, 16
R = 4
FF = 512
FC = FF // D
NC = N // 128
PAIRS = B // 2
W2G = 2 * N
EPS = 1e-5
SLOPE = 0.2
HIDDEN = -(2.0 ** 53)
PARTS = 3
TERMS = 6
ROWS = TERMS * DH
ROWSM = ROWS + PARTS
UNITS = 8
GRP = 4

VECS = ["L0_gnn_bq", "L0_gnn_bk", "L0_gnn_g1", "L0_gnn_beta1", "L0_gnn_g2", "L0_gnn_beta2",
        "L1_gnn_g_ln1", "L1_gnn_b_ln1", "L1_gnn_g_ln2", "L1_gnn_b_ln2"]
CENTRED = ["L0_gnn_bo", "L0_gnn_b2", "L1_gnn_b_ff2"]
COL = {name: n for n, name in enumerate(VECS)}
COL_B1 = len(VECS)
COL_BFF1 = COL_B1 + FC
COL_A = COL_BFF1 + FC
NROWS = COL_A + 4


def due(value):
    return not isinstance(value, int) or value > 0


def pair_loop(eng, step, start, loop_from, loop_to, end):
    for p in range(start, 2 * loop_from):
        step(p // 2, p % 2)
    with eng.Fori(loop_from, loop_to) as i:
        for b in range(2):
            step(i, b)
    for p in range(2 * loop_to, end):
        step(p // 2, p % 2)


def attend_loop(eng, step):
    pair_loop(eng, step, 0, 1, PAIRS // 2 - 1, PAIRS + 1)


def at_most(value, most):
    return min(value, most) if isinstance(value, int) else value


def within(i, index, count):
    return not isinstance(i, int) or 0 <= index < count


def build(nc, a, out):
    ctx = ExitStack()
    with ctx:
        def sb(name, shape, dt=F32, where=ctx):
            return where.enter_context(nc.sbuf_tensor(name, shape, dt))

        def sem(name):
            return ctx.enter_context(nc.semaphore(name))

        bank = [ctx.enter_context(nc.psum_tensor(f"bank{n}", [128, 512], F32)) for n in range(8)]

        x_all = sb("x_all", [128, B * N])
        codes = sb("codes", [128, B, NC, N], I8)
        ident = sb("ident", [128, 128])
        identb = sb("identb", [128, 128], BF16)
        centre = sb("centre", [128, 128])
        mean_w = sb("mean_w", [128, 128])
        eps = sb("eps", [128, 1])
        cols = sb("cols", [128, NROWS])
        ccols = sb("ccols", [128, len(CENTRED)])
        w1 = sb("w1", [128, FF])
        w2 = sb("w2", [128, FC, D])
        wf1 = sb("wf1", [128, FF])
        wf2 = sb("wf2", [128, FC, D])
        gw = sb("gw", [128, 2, D + 1])
        ga = sb("ga", [128, 2, D])

        flag = sb("flag", [128, 1], I32)

        nodes_of = lambda pair: x_all[:, bass.ds(pair * W2G, W2G)]

        attend_ctx = ExitStack()
        A = lambda name, shape, dt=F32: sb(name, shape, dt, attend_ctx)
        wq = A("wq", [128, D])
        wk = A("wk", [128, D])
        wv = A("wv", [128, R + 1, D])
        bvb = A("bvb", [128, R + 1, D])
        wo = A("wo", [128, 2, D])

        parts = A("parts", [128, 2, PARTS, W2G], BF16)
        whole = A("whole", [128, 2, W2G])
        rest = A("rest", [128, 2, W2G])
        x_nat = [A(f"x_nat{n}", [128, 2 * NC, D]) for n in range(2)]
        x_t = [A(f"x_t{n}", [128, W2G]) for n in range(2)]
        q_st = [A(f"q_st{n}", [ROWSM, H, N], BF16) for n in range(4)]
        k_st = [A(f"k_st{n}", [ROWSM, H, N], BF16) for n in range(4)]
        v_base = [A(f"v_base{n}", [128, 2, NC, H, 32]) for n in range(2)]
        v_one = [A(f"v_one{n}", [128, 2, NC, H, DH]) for n in range(2)]
        v_more = [A(f"v_more{n}", [128, 2, NC, R - 1, H, DH]) for n in range(2)]
        probs = A("probs", [128, UNITS, 512])
        probs_one = A("probs_one", [128, UNITS, 512])
        probs_more = A("probs_more", [128, R - 1, 2, 512])
        more_tmp = A("more_tmp", [128, 512])
        row_max = [A(f"row_max{n}", [128, NC, H]) for n in range(2)]
        neg_max = A("neg_max", [128, NC, H])
        max_rest = A("max_rest", [128, NC, H])
        max_parts = A("max_parts", [128, NC, PARTS, H], BF16)
        max_t = A("max_t", [PARTS * H, N], BF16)
        denom = A("denom", [128, 512])
        denom_r = A("denom_r", [128, 512])
        mixed = A("mixed", [128, 2, W2G])
        ln_y = A("ln_y", [128, W2G])
        ln_sq = A("ln_sq", [128, W2G])
        ln_r = A("ln_r", [128, W2G])

        scr_parts = nc.dram_tensor("scr_parts", [PAIRS, 2, PARTS, 2, DH * H, N], BF16).ap()
        scr_max = nc.dram_tensor("scr_max", [B, PARTS * H, N], BF16).ap()

        x_in = [sem(f"x_in{n}") for n in range(2)]
        xt_mm, xt_ready, x_kept = sem("xt_mm"), sem("xt_ready"), sem("x_kept")
        qk_mm, qk_whole, qk_rest, qk_split, parts_out = (sem("qk_mm"), sem("qk_whole"), sem("qk_rest"),
                                                         sem("qk_split"), sem("parts_out"))
        stacked = [sem(f"stacked{n}") for n in range(4)]
        s_mm, s_max, max_split, maxt_mm, maxt_ready = (sem("s_mm"), sem("s_max"), sem("max_split"), sem("maxt_mm"),
                                                       sem("maxt_ready"))
        max_out, max_in, msp = sem("max_out"), sem("max_in"), sem("msp")
        st_mm, exp_done, masked, pv_mm = sem("st_mm"), sem("exp_done"), sem("masked"), sem("pv_mm")
        v_mm, v_ready0, v_ready1, v_init, ones_init = (sem("v_mm"), sem("v_ready0"), sem("v_ready1"), sem("v_init"),
                                                       sem("ones_init"))
        den_ready, den_ln, den_inv, normed = sem("den_ready"), sem("den_ln"), sem("den_inv"), sem("normed")
        y_mm, y_read, var_mm, var_ln, rstd, ln_mid, ln_done = (sem("y_mm"), sem("y_read"), sem("var_mm"),
                                                              sem("var_ln"), sem("rstd"), sem("ln_mid"),
                                                              sem("ln_done"))
        vmore_mm, vmore_ready, more_done = sem("vmore_mm"), sem("vmore_ready"), sem("more_done")
        S_BANK, T_BANK, PV_BANK = bank[0:2], bank[2:4], bank[4:6]
        M0, M1 = bank[6], bank[7]

        passed = sem("passed")

        def attend_sync(sp):
            def x_load(pair, n):
                sp.dma_start(x_nat[n][:], a["x"][bass.ds(2 * pair, 2)].rearrange(
                    "g (c p) d -> p (g c) d", c=NC)).then_inc(x_in[n], 16)

            def stack_load(i, b, k):
                G, n = 4 * i + 2 * b + k, (2 * b + k) % 4
                if not within(i, G, B):
                    return
                P, gi = 2 * i + b + k // 2, k % 2
                sp.wait_ge(parts_out, 16 * (P + 1))
                sp.sem_inc(passed, 1)
                if due(UNITS * (G - 3)):
                    sp.wait_ge(st_mm, UNITS * (G - 3))
                    sp.sem_inc(passed, 1)
                src = scr_parts[bass.ds(P, 1)].rearrange("o t s g (d h) i -> g (o t s) d (h i)", h=H)[gi]
                slot = 0
                for run in range(PARTS, 0, -1):
                    rows_of = slice(DH * slot, DH * (slot + run))
                    sp.dma_start(q_st[n][rows_of].rearrange("p h i -> p (h i)"),
                                 src[0:run]).then_inc(stacked[n], 16)
                    at = PARTS + PARTS - run
                    sp.dma_start(k_st[n][rows_of].rearrange("p h i -> p (h i)"),
                                 src[at:at + 1].broadcast_to([run, DH, H * N])).then_inc(stacked[n], 16)
                    slot += run

            def max_rows(i, b, k):
                G, n = 4 * i + 2 * b + k, (2 * b + k) % 4
                if not within(i, G, B):
                    return
                sp.wait_ge(maxt_ready, G + 1)
                sp.sem_inc(passed, 1)
                sp.dma_start(scr_max[bass.ds(G, 1)].rearrange("o r i -> (o r) i"), max_t[:]).then_inc(max_out, 16)
                sp.wait_ge(max_out, 16 * (G + 1))
                sp.sem_inc(passed, 1)
                sp.dma_start(q_st[n][ROWS:ROWSM, :, :], scr_max[bass.ds(G, 1)].rearrange(
                    "o (s h) i -> (o s) h i", s=PARTS)).then_inc(max_in, 16)

            def step(i, b):
                p = 2 * i + b
                stack_load(i, b, 3)
                if within(i, p + 3, PAIRS):
                    if due(p + 2):
                        sp.wait_ge(xt_mm, p + 2)
                        sp.sem_inc(passed, 1)
                    x_load(p + 3, (b + 1) % 2)
                max_rows(i, b, 1)
                if within(i, p + 2, PAIRS):
                    sp.wait_ge(qk_split, 2 * (p + 3))
                    sp.sem_inc(passed, 1)
                    sp.dma_start(scr_parts[bass.ds(p + 2, 1)].rearrange("o t s g r i -> r (o t s g) i"),
                                 parts[:].rearrange("p t s (g i) -> p (t s g) i", g=2)).then_inc(parts_out, 16)
                max_rows(i, b, 2)
                stack_load(i, b, 4)

            return x_load, step

        def attend_pool(pool):
            def split(P, t):
                pool.wait_ge(qk_whole, 2 * P + t + 1)
                pool.sem_inc(passed, 1)
                nc.gpsimd.tensor_tensor(rest[:, t, :], whole[:, t, :], parts[:, t, 0, :],
                                        ALU.subtract).then_inc(qk_rest, 1)
                pool.wait_ge(qk_rest, 4 * P + 2 * t + 1)
                pool.sem_inc(passed, 1)
                nc.gpsimd.tensor_copy(parts[:, t, 1, :], rest[:, t, :]).then_inc(qk_rest, 1)
                pool.wait_ge(qk_rest, 4 * P + 2 * t + 2)
                pool.sem_inc(passed, 1)
                nc.gpsimd.tensor_tensor(parts[:, t, 2, :], rest[:, t, :], parts[:, t, 1, :],
                                        ALU.subtract).then_inc(qk_split, 1)

            def split_max(i, b, k):
                G, n = 4 * i + 2 * b + k, k % 2
                if not within(i, G, B):
                    return
                pool.wait_ge(s_max, UNITS * (G + 1))
                pool.sem_inc(passed, 1)
                if due(G):
                    pool.wait_ge(maxt_mm, G)
                    pool.sem_inc(passed, 1)
                nc.gpsimd.tensor_scalar(neg_max[:], row_max[n][:], -1.0, 0.0, ALU.mult, ALU.add).then_inc(msp, 1)
                pool.wait_ge(msp, 4 * G + 1)
                pool.sem_inc(passed, 1)
                nc.gpsimd.tensor_copy(max_parts[:, :, 0, :], neg_max[:]).then_inc(msp, 1)
                pool.wait_ge(msp, 4 * G + 2)
                pool.sem_inc(passed, 1)
                nc.gpsimd.tensor_tensor(max_rest[:], neg_max[:], max_parts[:, :, 0, :], ALU.subtract).then_inc(msp, 1)
                pool.wait_ge(msp, 4 * G + 3)
                pool.sem_inc(passed, 1)
                nc.gpsimd.tensor_copy(max_parts[:, :, 1, :], max_rest[:]).then_inc(msp, 1)
                pool.wait_ge(msp, 4 * G + 4)
                pool.sem_inc(passed, 1)
                nc.gpsimd.tensor_tensor(max_parts[:, :, 2, :], max_rest[:], max_parts[:, :, 1, :],
                                        ALU.subtract).then_inc(max_split, 1)

            def step(i, b):
                p = 2 * i + b
                split_max(i, b, 1)
                if within(i, p + 2, PAIRS):
                    P = p + 2
                    pool.wait_ge(xt_ready, P + 1)
                    pool.sem_inc(passed, 1)
                    nc.gpsimd.tensor_copy(nodes_of(P), x_t[b][:]).then_inc(x_kept, 1)
                    split(P, 0)
                    split(P, 1)
                split_max(i, b, 2)

            return step

        def attend_act(act):
            def exp_unit(i, b, k, u):
                G = 4 * i + 2 * b + k
                act.wait_ge(st_mm, UNITS * G + u + 1)
                if due(4 * (G - 1) + u // 2 + 1):
                    act.wait_ge(pv_mm, 4 * (G - 1) + u // 2 + 1)
                nc.scalar.activation(probs[:, u, :], T_BANK[u % 2][:, :], ACT.Exp).then_inc(exp_done, 1)

            def whole_qk(P, t, src, scale, bias):
                act.wait_ge(qk_mm, 2 * P + t + 1)
                if due(2 * P + t - 1):
                    act.wait_ge(qk_split, 2 * P + t - 1)
                nc.scalar.activation(whole[:, t, :], src[:, :], ACT.Identity, bias=bias, scale=scale)
                if due(16 * P):
                    act.wait_ge(parts_out, 16 * P)
                nc.scalar.activation(parts[:, t, 0, :], src[:, :], ACT.Identity, bias=bias,
                                     scale=scale).then_inc(qk_whole, 1)

            def max_copy(i, b, k):
                G = 4 * i + 2 * b + k
                if not within(i, G, B):
                    return
                act.wait_ge(maxt_mm, G + 1)
                if due(16 * G):
                    act.wait_ge(max_out, 16 * G)
                nc.scalar.copy(max_t[:], M1[:, :].bitcast(BF16)[0:PARTS * H, 0:N]).then_inc(maxt_ready, 1)

            def inverse_denominators(G):
                act.wait_ge(den_ready, G + 1)
                nc.scalar.activation(denom[:], denom[:], ACT.Ln).then_inc(den_ln, 1)
                act.wait_ge(den_ln, G + 1)
                if due(G):
                    act.wait_ge(normed, G)
                nc.scalar.activation(denom_r[:], denom[:], ACT.Exp, scale=-1.0).then_inc(den_inv, 1)

            def step(i, b):
                p = 2 * i + b
                for slot in range(2):
                    G = 2 * p + slot
                    for u in range(UNITS):
                        if within(i, G, B):
                            exp_unit(i, b, slot, u)
                        if u == 1:
                            max_copy(i, b, slot + 1)
                        if u == 4 and within(i, G - 1, B):
                            inverse_denominators(G - 1)
                        if slot == 0:
                            P = p + 2
                            if u == 0 and within(i, P, PAIRS):
                                act.wait_ge(xt_mm, P + 1)
                                if due(2 * (P - 1)):
                                    act.wait_ge(v_mm, 2 * (P - 1))
                                if due(P - 1):
                                    act.wait_ge(x_kept, P - 1)
                                nc.scalar.copy(x_t[b][:], M0[:, :]).then_inc(xt_ready, 1)
                            if u == 2 and within(i, P, PAIRS):
                                c = COL["L0_gnn_bq"]
                                whole_qk(P, 0, M0, DH ** -0.5, cols[:, c:c + 1])
                            if u == 3 and within(i, P, PAIRS):
                                c = COL["L0_gnn_bk"]
                                whole_qk(P, 1, M1, 1.0, cols[:, c:c + 1])
                            if u == 7 and within(i, p - 1, PAIRS):
                                act.wait_ge(y_mm, p)
                                if due(p - 1):
                                    act.wait_ge(ln_done, p - 1)
                                nc.scalar.activation(ln_y[:], M0[:, :], ACT.Identity, bias=ccols[:, 0:1])
                                nc.scalar.activation(ln_sq[:], M0[:, :], ACT.Square,
                                                     bias=ccols[:, 0:1]).then_inc(y_read, 1)
                        elif u == 3 and within(i, p - 1, PAIRS):
                            act.wait_ge(var_mm, p)
                            nc.scalar.activation(ln_r[:], M0[:, :], ACT.Ln, bias=eps[:, 0:1]).then_inc(var_ln, 1)
                            act.wait_ge(var_ln, p)
                            nc.scalar.activation(ln_r[:], ln_r[:], ACT.Exp, scale=-0.5).then_inc(rstd, 1)
                        elif u == 6 and within(i, p - 1, PAIRS):
                            act.wait_ge(ln_mid, p)
                            g = COL["L0_gnn_g1"]
                            nc.scalar.activation(nodes_of(p - 1), ln_y[:], ACT.Identity, bias=cols[:, g + 1:g + 2],
                                                 scale=cols[:, g:g + 1]).then_inc(ln_done, 1)

            return step

        def attend_pe(pe, more):
            def scores(i, b, k, u):
                G, n = 4 * i + 2 * b + k, (2 * b + k) % 4
                if not within(i, G, B):
                    return
                if u == 0:
                    quarter = i + (2 * b + k) // 4
                    pe.wait_ge(stacked[n], 16 * 2 * PARTS * (quarter + 1))
                if due(UNITS * G + u - 1):
                    pe.wait_ge(s_max, UNITS * G + u - 1)
                c = u // 4
                for j in range(2):
                    h = 2 * (u % 4) + j
                    last = nc.tensor.matmul(S_BANK[u % 2][:, N * j:N * j + N],
                                            q_st[n][0:ROWS, h, 128 * c:128 * c + 128],
                                            k_st[n][0:ROWS, h, :], start=True, stop=True)
                last.then_inc(s_mm, 1)

            def scores_t(i, b, k, u):
                G, n = 4 * i + 2 * b + k, (2 * b + k) % 4
                if not within(i, G, B):
                    return
                if u == 0:
                    pe.wait_ge(max_in, 16 * (G + 1))
                if due(UNITS * G + u - 1):
                    pe.wait_ge(exp_done, UNITS * G + u - 1)
                c = (u // 2) % 2
                for j in range(2):
                    h = GRP * (u // 4) + 2 * (u % 2) + j
                    last = nc.tensor.matmul(T_BANK[u % 2][:, N * j:N * j + N],
                                            k_st[n][:, h, 128 * c:128 * c + 128],
                                            q_st[n][:, h, :], start=True, stop=True)
                last.then_inc(st_mm, 1)

            def values(i, b, k, q):
                G = 4 * i + 2 * b + k
                if not within(i, G, B):
                    return
                par, gi = (b + k // 2) % 2, k % 2
                pe.wait_ge(masked, UNITS * G + 2 * q + 2)
                if q == 0:
                    if due(G - 1):
                        pe.wait_ge(normed, G - 1)
                    pe.wait_ge(v_ready1, 2 * i + b + k // 2 + 1)
                    if more:
                        pe.wait_ge(vmore_ready, 4 * (2 * i + b + k // 2 + 1))
                grp, c = q // 2, q % 2
                terms = 2 + (R - 1 if more else 0)
                for term in range(terms):
                    for g in range(GRP):
                        h = GRP * grp + g
                        u = 4 * grp + 2 * c + g // 2
                        cut = slice(N * (g % 2), N * (g % 2) + N)
                        if term == 0:
                            w, m, rhs = v_base[par][:, gi, c, h, :], 32, probs[:, u, cut]
                        elif term == 1:
                            w, m, rhs = v_one[par][:, gi, c, h, :], DH, probs_one[:, u, cut]
                        else:
                            w, m, rhs = (v_more[par][:, gi, c, term - 2, h, :], DH,
                                         probs_more[:, term - 2, u % 2, cut])
                        last = nc.tensor.matmul(PV_BANK[k % 2][32 * g:32 * g + m, N * grp:N * grp + N], w, rhs,
                                                start=(c == 0 and term == 0),
                                                stop=(c == NC - 1 and term == terms - 1))
                last.then_inc(pv_mm, 1)

            def turn_max(i, b, k):
                G = 4 * i + 2 * b + k
                if not within(i, G, B):
                    return
                pe.wait_ge(max_split, G + 1)
                for c in range(NC):
                    last = nc.tensor.transpose(M1[:, :].bitcast(BF16)[0:PARTS * H, 128 * c:128 * c + 128],
                                               max_parts[:, c, :, :].rearrange("p s h -> p (s h)"), identb[:])
                last.then_inc(maxt_mm, 1)

            def make_values(Q, par, gi, bk):
                for c in range(NC):
                    last = nc.tensor.matmul(bk[:, 2 * D * c:2 * D * c + 2 * D],
                                            x_t[par][:, N * gi + 128 * c:N * gi + 128 * c + 128],
                                            wv[:, 0:2, :].rearrange("p r d -> p (r d)"), start=True, stop=True)
                last.then_inc(v_mm, 1)

            def make_more(Q, par):
                for n in range(4):
                    bk = (M1, M0)[n % 2]
                    if n < 2:
                        pe.wait_ge((v_ready0, v_ready1)[n], Q + 1)
                    else:
                        pe.wait_ge(vmore_ready, 4 * Q + n - 1)
                    nc.tensor.matmul(bk[:, 0:(R - 1) * D], x_t[par][:, 128 * n:128 * n + 128],
                                     wv[:, 2:R + 1, :].rearrange("p r d -> p (r d)"), start=True,
                                     stop=True).then_inc(vmore_mm, 1)

            def step(i, b):
                p = 2 * i + b
                for slot in range(2):
                    G = 2 * p + slot
                    for u in range(UNITS):
                        scores(i, b, slot + 2, u)
                        scores_t(i, b, slot, u)
                        if u == 0:
                            values(i, b, slot - 1, 2)
                        if u == 2:
                            values(i, b, slot - 1, 3)
                        if u == 4:
                            values(i, b, slot, 0)
                        if u == 6:
                            values(i, b, slot, 1)
                        P, Q = p + 2, p + 1
                        if slot == 0:
                            if u == 0 and within(i, P, PAIRS):
                                half = i + (b + 2) // 2
                                pe.wait_ge(x_in[b], 16 * (half + 1))
                                if due(P - 1):
                                    pe.wait_ge(v_ready1, P - 1)
                                if isinstance(i, int):
                                    if due(2 * (P - 1)):
                                        pe.wait_ge(qk_whole, 2 * (P - 1))
                                if more:
                                    if due(4 * (P - 1)):
                                        pe.wait_ge(vmore_ready, 4 * (P - 1))
                                for n in range(2 * NC):
                                    last = nc.tensor.transpose(M0[:, 128 * n:128 * n + 128], x_nat[b][:, n, :],
                                                               ident[:])
                                last.then_inc(xt_mm, 1)
                            if u == 1:
                                if within(i, G + 1, B):
                                    pe.wait_ge(v_ready0, p + 1)
                                    if more:
                                        pe.wait_ge(vmore_ready, 4 * (p + 1))
                                turn_max(i, b, 1)
                            if u == 2 and within(i, P, PAIRS):
                                pe.wait_ge(xt_ready, P + 1)
                                nc.tensor.matmul(M0[:, :], wq[:], x_t[b][:], start=True, stop=True).then_inc(qk_mm, 1)
                            if u == 3 and within(i, P, PAIRS):
                                if within(i, G + 1, B):
                                    pe.wait_ge(maxt_ready, G + 2)
                                nc.tensor.matmul(M1[:, :], wk[:], x_t[b][:], start=True, stop=True).then_inc(qk_mm, 1)
                            if u == 5 and within(i, p - 1, PAIRS):
                                if within(i, P, PAIRS):
                                    pe.wait_ge(qk_whole, 2 * P + 1)
                                else:
                                    pe.wait_ge(v_ready1, at_most(p + 1, PAIRS))
                                    if due(p - 1):
                                        pe.wait_ge(var_ln, p - 1)
                                pe.wait_ge(x_kept, p)
                                nc.tensor.matmul(M0[:, :], centre[:], nodes_of(p - 1), start=True, stop=False)
                            if u == 7 and within(i, p - 1, PAIRS):
                                pe.wait_ge(normed, 2 * p)
                                for n in range(2):
                                    last = nc.tensor.matmul(M0[:, :], wo[:, n, :], mixed[:, n, :], start=False,
                                                            stop=(n == 1))
                                last.then_inc(y_mm, 1)
                        else:
                            if u == 1:
                                if within(i, G + 1, B):
                                    if within(i, P, PAIRS):
                                        pe.wait_ge(qk_whole, 2 * P + 2)
                                    elif within(i, G, B):
                                        pe.wait_ge(maxt_ready, G + 1)
                                turn_max(i, b, 2)
                            if u == 2 and within(i, p - 1, PAIRS):
                                pe.wait_ge(y_read, p)
                                nc.tensor.matmul(M0[:, :], mean_w[:], ln_sq[:], start=True, stop=True).then_inc(var_mm, 1)
                            if u == 3 and within(i, Q, PAIRS):
                                pe.wait_ge(xt_ready, Q + 1)
                                pe.wait_ge(maxt_ready, G + 2)
                                make_values(Q, (b + 1) % 2, 0, M1)
                            if u == 6 and within(i, Q, PAIRS):
                                if due(p):
                                    pe.wait_ge(var_ln, p)
                                if within(i, P, PAIRS):
                                    pe.wait_ge(qk_whole, 2 * P + 1)
                                make_values(Q, (b + 1) % 2, 1, M0)
                            if u == 7 and more and within(i, Q, PAIRS):
                                make_more(Q, (b + 1) % 2)

            return step, make_more

        def attend_dve(dve, more):
            def reduce_max(i, b, k, u):
                G = 4 * i + 2 * b + k
                if not within(i, G, B):
                    return
                dve.wait_ge(s_mm, UNITS * G + u + 1)
                if u == 0:
                    if due(G - 1):
                        dve.wait_ge(max_split, G - 1)
                c, hp = u // 4, u % 4
                nc.vector.tensor_reduce(row_max[k % 2][:, c, 2 * hp:2 * hp + 2],
                                        S_BANK[u % 2][:, :].rearrange("p (h j) -> p h j", h=2), AX,
                                        ALU.max).then_inc(s_max, 1)

            def mask(i, b, k, u):
                G = 4 * i + 2 * b + k
                if not within(i, G, B):
                    return
                dve.wait_ge(exp_done, UNITS * G + u + 1)
                if due(4 * (G - 1) + u // 2 + 1):
                    dve.wait_ge(pv_mm, 4 * (G - 1) + u // 2 + 1)
                code = codes[:, bass.ds(G, 1), (u // 2) % 2, :].broadcast_to([128, 2, N])
                src = probs[:, u, :].rearrange("p (h i) -> p h i", h=2)
                dst = probs_one[:, u, :].rearrange("p (h i) -> p h i", h=2)
                one = nc.vector.scalar_tensor_tensor(out=dst, in0=code, scalar=1.0, in1=src, op0=ALU.is_equal,
                                                     op1=ALU.mult)
                if more:
                    if due(4 * G + u // 2):
                        dve.wait_ge(pv_mm, 4 * G + u // 2)
                    for r in range(2, R):
                        dst = probs_more[:, r - 2, u % 2, :].rearrange("p (h i) -> p h i", h=2)
                        nc.vector.scalar_tensor_tensor(out=dst, in0=code, scalar=float(r), in1=src,
                                                       op0=ALU.is_equal, op1=ALU.mult)
                    last = probs_more[:, R - 2, u % 2, :]
                    dst = last.rearrange("p (h i) -> p h i", h=2)
                    nc.vector.scalar_tensor_tensor(out=dst, in0=code, scalar=0.0, in1=src, op0=ALU.is_lt,
                                                   op1=ALU.mult).then_inc(more_done, 1)
                    dve.wait_ge(more_done, 2 * (UNITS * G + u) + 1)
                    tmp = more_tmp[:, :].rearrange("p (h i) -> p h i", h=2)
                    nc.vector.scalar_tensor_tensor(out=tmp, in0=code, scalar=float(R), in1=src, op0=ALU.is_ge,
                                                   op1=ALU.mult).then_inc(more_done, 1)
                    dve.wait_ge(more_done, 2 * (UNITS * G + u) + 2)
                    nc.vector.tensor_tensor(last, last, more_tmp[:, :], ALU.add).then_inc(masked, 1)
                else:
                    one.then_inc(masked, 1)

            def spread_denominators(G, k):
                dve.wait_ge(pv_mm, 4 * (G + 1))
                if due(G):
                    dve.wait_ge(den_inv, G)
                    dve.sem_inc(passed, 1)
                nc.vector.stream_shuffle(denom[:], PV_BANK[k % 2][:, :], [DH] * 32).then_inc(den_ready, 1)

            def normalize(i, b, k):
                G = 4 * i + 2 * b + k
                gi = k % 2
                dve.wait_ge(den_inv, G + 1)
                if due(2 * i + b + k // 2):
                    dve.wait_ge(y_mm, 2 * i + b + k // 2)
                nc.vector.tensor_tensor(mixed[:, :, N * gi:N * gi + N],
                                        PV_BANK[k % 2][:, :].rearrange("p (n i) -> p n i", n=2),
                                        denom_r[:].rearrange("p (n i) -> p n i", n=2), ALU.mult).then_inc(normed, 1)

            def keep_values(Q, par, gi, bk, done):
                dve.wait_ge(v_mm, 2 * Q + gi + 1)
                if due(4 * (2 * Q - 2)):
                    dve.wait_ge(pv_mm, 4 * (2 * Q - 2))
                src = bk[:, :].rearrange("p (c r h d) -> p c r h d", c=NC, r=2, h=H)
                for r in range(2):
                    dst = v_base[par][:, gi, :, :, 0:DH] if r == 0 else v_one[par][:, gi, :, :, :]
                    for c in range(NC):
                        last = nc.vector.tensor_tensor(dst[:, c], src[:, c, r],
                                                       bvb[:, r, :].rearrange("p (h d) -> p h d", h=H), ALU.add)
                last.then_inc(done, 1)

            def keep_more(Q, par):
                for n in range(4):
                    dve.wait_ge(vmore_mm, 4 * Q + n + 1)
                    nc.vector.tensor_tensor(v_more[par][:, n // 2, n % 2].rearrange("p r h d -> p (r h d)"),
                                            (M1, M0)[n % 2][:, 0:(R - 1) * D],
                                            bvb[:, 2:R + 1, :].rearrange("p r d -> p (r d)"),
                                            ALU.add).then_inc(vmore_ready, 1)

            def step(i, b):
                p = 2 * i + b
                for slot in range(2):
                    G = 2 * p + slot
                    for u in range(UNITS):
                        reduce_max(i, b, slot + 2, u)
                        if u == 7 and slot == 1 and within(i, p + 1, PAIRS):
                            keep_values(p + 1, (b + 1) % 2, 1, M0, v_ready1)
                            if more:
                                keep_more(p + 1, (b + 1) % 2)
                        if u == 0:
                            mask(i, b, slot - 1, UNITS - 1)
                        else:
                            mask(i, b, slot, u - 1)
                        if u == 3 and within(i, G - 1, B):
                            spread_denominators(G - 1, slot - 1)
                        if u == 6 and within(i, G - 1, B):
                            normalize(i, b, slot - 1)
                        Q = p + 1
                        if slot == 1:
                            if u == 4 and within(i, p - 1, PAIRS):
                                dve.wait_ge(rstd, p)
                                nc.vector.tensor_tensor(ln_y[:], ln_y[:], ln_r[:], ALU.mult).then_inc(ln_mid, 1)
                            if u == 5 and within(i, Q, PAIRS):
                                keep_values(Q, (b + 1) % 2, 0, M1, v_ready0)

            return step, keep_more

        adj_in = [probs[:, 2 * n:2 * n + 2, :].bitcast(I32).rearrange("p g (c i) -> p g c i", c=NC) for n in range(2)]
        wqk_raw = probs[:, 4, 0:2 * D].rearrange("p (n d) -> p n d", n=2)
        graw = probs[:, 4, 2 * D:4 * D].rearrange("p (n d) -> p n d", n=2)
        gt = probs[:, 5, 0:2 * D].rearrange("p (n d) -> p n d", n=2)
        abc = probs[:, 5, 2 * D:4 * D].rearrange("p (n d) -> p n d", n=2)
        rows = probs[0:NROWS, 6, 0:D]
        crows = probs[0:len(CENTRED), 6, D:2 * D]
        crow_mean = probs[0:len(CENTRED), 6, 2 * D:2 * D + 1]
        adj_c = [probs_one[:, n, :].bitcast(BF16).rearrange("p (g c i) -> p g c i", g=2, c=NC) for n in range(2)]
        odd_junk = probs_one[:, 2, :].bitcast(BF16)
        odd = probs_one[:, 3, 0:PAIRS]
        wmean = probs_one[:, 3, PAIRS:PAIRS + 12]
        mhalf, odd_max, odd_all = (probs_one[:, 3, 32 + n:33 + n] for n in range(3))

        rows_in, bo_in, wts_in, wo_in = sem("rows_in"), sem("bo_in"), sem("wts_in"), sem("wo_in")
        gat_in, bv_in = sem("gat_in"), sem("bv_in")
        adj_sem = [sem(f"adj_sem{n}") for n in range(2)]
        const_ready, wo_zero, prep, prep_pe = sem("const_ready"), sem("wo_zero"), sem("prep"), sem("prep_pe")
        clamped, turned, coded, counted = sem("clamped"), sem("turned"), sem("coded"), sem("counted")
        odd_sem = sem("odd_sem")
        vchain = sem("vchain")
        wqk_in, wqk_ready, cols_ready = sem("wqk_in"), sem("wqk_ready"), sem("cols_ready")

        with nc.Block() as block:
            @block.sync
            def _(sp):
                x_load, step = attend_sync(sp)
                x_load(0, 0)
                sp.dma_start(wqk_raw[:, 0, :], a["L0_gnn_Wq"]).then_inc(wqk_in, 16)
                sp.dma_start(wqk_raw[:, 1, :], a["L0_gnn_Wk"]).then_inc(wqk_in, 16)
                for n, name in enumerate(VECS):
                    if name in ("L0_gnn_bq", "L0_gnn_bk"):
                        sp.dma_start(rows[n:n + 1, :].rearrange("o (d h) -> o d h", h=H),
                                     a[name].rearrange("(o h d) -> o d h", o=1, h=H),
                                     allow_slow_non_contiguous=True).then_inc(rows_in, 16)
                    else:
                        sp.dma_start(rows[n:n + 1, :], a[name].rearrange("(o d) -> o d", o=1)).then_inc(rows_in, 16)
                for start, name in ((COL_B1, "L0_gnn_b1"), (COL_BFF1, "L1_gnn_b_ff1")):
                    sp.dma_start(rows[start:start + FC, :], a[name].rearrange("(c d) -> c d", c=FC)).then_inc(rows_in, 16)
                for n, name in enumerate(("L1_gnn_a1", "L1_gnn_a2")):
                    sp.dma_start(rows[COL_A + 2 * n:COL_A + 2 * n + 2, :],
                                 a[name].rearrange("(c d) o -> c (d o)", c=2)).then_inc(rows_in, 16)
                for n, name in enumerate(CENTRED):
                    sp.dma_start(crows[n:n + 1, :], a[name].rearrange("(o d) -> o d", o=1)).then_inc(bo_in, 16)
                sp.dma_start(wv[:, 0:R, :], a["L0_gnn_Wv"].rearrange("r d e -> d r e")).then_inc(wts_in, 16)
                sp.dma_start(bvb[:, 0:R, :], a["L0_gnn_bv"].partition_broadcast(128)).then_inc(bv_in, 16)
                for n, name in enumerate(("L1_gnn_W1", "L1_gnn_W2")):
                    sp.dma_start(graw[:, n, :], a[name]).then_inc(gat_in, 16)
                sp.wait_ge(wo_zero, 1)
                for h in range(H):
                    sp.dma_start(wo[32 * (h % GRP):32 * (h % GRP) + DH, h // GRP, :],
                                 a["L0_gnn_Wo"][DH * h:DH * h + DH, :]).then_inc(wo_in, 16)
                sp.dma_start(w1[:], a["L0_gnn_W1"]).then_inc(wts_in, 16)
                sp.dma_start(w2[:], a["L0_gnn_W2"].rearrange("(c k) d -> k c d", c=FC)).then_inc(wts_in, 16)
                sp.dma_start(wf1[:], a["L1_gnn_w_ff1"]).then_inc(wts_in, 16)
                sp.dma_start(wf2[:], a["L1_gnn_w_ff2"].rearrange("(c k) d -> k c d", c=FC)).then_inc(wts_in, 16)
                step(-1, 0)
                step(-1, 1)

            @block.gpsimd
            def _(pool):
                nc.gpsimd.memset(ident[:], 0.0).then_inc(const_ready, 1)
                pool.wait_ge(const_ready, 1)
                nc.gpsimd.affine_select(out=ident[:], in_=ident[:], compare_op=ALU.not_equal, fill=1.0, base=0,
                                        pattern=[[-1, 128]], channel_multiplier=1).then_inc(const_ready, 1)
                pool.wait_ge(const_ready, 2)
                nc.gpsimd.tensor_copy(identb[:], ident[:]).then_inc(const_ready, 1)
                nc.gpsimd.memset(mhalf, -0.5).then_inc(const_ready, 1)
                nc.gpsimd.tensor_scalar(centre[:], ident[:], 1.0 / D, None, ALU.subtract).then_inc(const_ready, 1)
                nc.gpsimd.memset(mean_w[:], 1.0 / D).then_inc(const_ready, 1)
                nc.gpsimd.memset(eps[:], EPS).then_inc(const_ready, 1)
                pool.wait_ge(const_ready, 7)
                for n in range(4):
                    nc.gpsimd.memset(k_st[n][ROWS:ROWSM, :, :], 1.0).then_inc(ones_init, 1)
                    pool.wait_ge(ones_init, n + 1)
                step = attend_pool(pool)
                step(-1, 0)
                pool.wait_ge(odd_sem, 1)
                nc.gpsimd.partition_all_reduce(odd_all, odd_max, 128, RMAX).then_inc(odd_sem, 1)
                step(-1, 1)

            @block.scalar
            def _(act):
                act.preload_act_table_set("natural_log_exp_and_others")
                step = attend_act(act)

                def load_adj(P, n):
                    act.dma_start(adj_in[n], a["adj"][bass.ds(2 * P, 2)].rearrange(
                        "g (c p) j -> p g c j", c=NC)).then_inc(adj_sem[n], 16)

                def load_and_count(i, n):
                    P = 2 * i + n
                    if within(i, P, PAIRS):
                        act.wait_ge(clamped, P - 1)
                        load_adj(P, n)
                    act.wait_ge(coded, P - 1)
                    if due(P - 2):
                        act.wait_ge(counted, P - 2)
                    nc.scalar.activation(odd_junk, codes[:, bass.ds(2 * P - 4, 2)].rearrange("p g c i -> p (g c i)"),
                                         ACT.Square, bias=mhalf[:, 0:1],
                                         accum_out=odd[:, bass.ds(P - 2, 1)]).then_inc(counted, 1)

                load_adj(0, 0)
                load_adj(1, 1)
                act.wait_ge(const_ready, 7)
                act.wait_ge(cols_ready, 1)
                step(-1, 0)
                pair_loop(act, load_and_count, 2, 2, PAIRS // 2, PAIRS + 2)
                step(-1, 1)

            @block.tensor
            def _(pe):
                step, _more = attend_pe(pe, False)

                def turn_codes(i, n):
                    pe.wait_ge(clamped, 2 * i + n + 1)
                    if due(2 * i + n - 1):
                        pe.wait_ge(coded, 2 * i + n - 1)
                    turned_bank = bank[n][:, :].bitcast(BF16).rearrange("p (g c i) -> p g c i", g=2, c=NC)
                    for g in range(2):
                        for c in range(NC):
                            for k in range(NC):
                                last = nc.tensor.transpose(turned_bank[:, g, c, 128 * k:128 * k + 128],
                                                           adj_c[n][:, g, k, 128 * c:128 * c + 128], identb[:])
                    last.then_inc(turned, 1)

                pe.wait_ge(const_ready, 4)
                pe.wait_ge(rows_in, 16 * (len(VECS) + 4))
                nc.tensor.transpose(bank[2][:, 0:NROWS], rows, ident[0:NROWS, 0:NROWS]).then_inc(prep_pe, 1)
                pe.wait_ge(wqk_ready, 1)
                step(-1, 0)
                pair_loop(pe, turn_codes, 0, 1, PAIRS // 2, PAIRS)
                pe.wait_ge(prep, 1)
                nc.tensor.transpose(bank[3][:, 0:len(CENTRED)], crows,
                                    ident[0:len(CENTRED), 0:len(CENTRED)]).then_inc(prep_pe, 1)
                pe.wait_ge(gat_in, 32)
                for n in range(2):
                    last = nc.tensor.transpose(bank[4][:, 128 * n:128 * n + 128], graw[:, n, :], ident[:])
                last.then_inc(prep_pe, 1)
                pe.wait_ge(prep, 2)
                for n in range(2):
                    nc.tensor.matmul(bank[(5, 2)[n]][:, 0:D], gt[:, n, :], abc[:, n, :], start=True, stop=True)
                for n in range(2):
                    last = nc.tensor.matmul(bank[(5, 2)[n]][:, D:D + 1], gt[:, n, :],
                                            cols[:, COL_A + 2 * n + 1:COL_A + 2 * n + 2], start=True, stop=True)
                last.then_inc(prep_pe, 1)
                pe.wait_ge(coded, PAIRS)
                pe.wait_ge(prep, 3)
                step(-1, 1)

            @block.vector
            def _(dve):
                links = [0]

                def link(ins):
                    links[0] += 1
                    ins.then_inc(vchain, 1)
                    dve.wait_ge(vchain, links[0])

                nc.vector.memset(wo[:], 0.0).then_inc(wo_zero, 1)
                for n in range(2):
                    nc.vector.memset(v_base[n][:, :, :, :, DH:32], 1.0)
                dve.wait_ge(wqk_in, 32)
                for n, w in enumerate((wq, wk)):
                    last = nc.vector.tensor_copy(w[:].rearrange("p (d h) -> p d h", h=H),
                                                 wqk_raw[:, n, :].rearrange("p (h d) -> p d h", h=H))
                last.then_inc(wqk_ready, 1)
                dve.wait_ge(prep_pe, 1)
                link(nc.vector.tensor_copy(cols[:], bank[2][:, 0:NROWS]))
                qcol = cols[:, COL["L0_gnn_bq"]:COL["L0_gnn_bq"] + 1]
                nc.vector.tensor_scalar(qcol, qcol, DH ** -0.5, None, ALU.mult).then_inc(cols_ready, 1)

                def code(i, n):
                    P = 2 * i + n
                    if within(i, P, PAIRS):
                        dve.wait_ge(adj_sem[n], 16 * i + 16)
                        if due(P - 1):
                            dve.wait_ge(turned, P - 1)
                        nc.vector.tensor_scalar(adj_c[n], adj_in[n], -1.0, float(R), ALU.max,
                                                ALU.min).then_inc(clamped, 1)
                    if within(i, P - 1, PAIRS):
                        if due(P):
                            dve.wait_ge(turned, P)
                        nc.vector.tensor_copy(
                            codes[:, bass.ds(2 * (P - 1), 2)],
                            bank[1 - n][:, :].bitcast(BF16).rearrange("p (g c i) -> p g c i", g=2,
                                                                      c=NC)).then_inc(coded, 1)
                pair_loop(dve, code, 0, 1, PAIRS // 2, PAIRS + 1)
                dve.wait_ge(bo_in, 16 * len(CENTRED))
                link(nc.vector.tensor_reduce(crow_mean, crows, AX, ALU.add))
                link(nc.vector.tensor_scalar(crow_mean, crow_mean, 1.0 / D, None, ALU.mult))
                nc.vector.tensor_scalar(crows, crows, crow_mean[:, 0:1], None, ALU.subtract).then_inc(prep, 1)
                for n in range(2):
                    nc.vector.tensor_copy(abc[:, n, :], cols[:, COL_A + 2 * n:COL_A + 2 * n + 1].to_broadcast([128, D]))
                dve.wait_ge(prep_pe, 3)
                nc.vector.tensor_copy(ccols[:], bank[3][:, 0:len(CENTRED)])
                nc.vector.tensor_copy(gt, bank[4][:, 0:2 * D].rearrange("p (n d) -> p n d", n=2)).then_inc(prep, 1)
                dve.wait_ge(wts_in, 16 * 5)
                dve.wait_ge(wo_in, 16 * H)
                dve.wait_ge(bv_in, 16)
                for w in (wv, bvb):
                    nc.vector.tensor_scalar(w[:, R, :], w[:, 0, :], -1.0, None, ALU.mult)
                    for r in range(1, R):
                        last = nc.vector.tensor_tensor(w[:, r, :], w[:, r, :], w[:, 0, :], ALU.subtract)
                last.then_inc(prep, 1)
                dve.wait_ge(counted, PAIRS)
                nc.vector.tensor_reduce(odd_max, odd, AX, ALU.max).then_inc(odd_sem, 1)
                for at, w, k in ((0, wo, 2), (2, w2, FC), (6, wf2, FC)):
                    link(nc.vector.tensor_reduce(wmean[:, at:at + k], w[:], AX, ALU.add))
                    link(nc.vector.tensor_scalar(wmean[:, at:at + k], wmean[:, at:at + k], 1.0 / D, None, ALU.mult))
                    for c in range(k):
                        nc.vector.tensor_scalar(w[:, c, :], w[:, c, :], wmean[:, at + c:at + c + 1], None, ALU.subtract)
                link(nc.vector.tensor_reduce(wmean[:, 10:11], graw[:, 1, :], AX, ALU.add))
                link(nc.vector.tensor_scalar(wmean[:, 10:11], wmean[:, 10:11], 1.0 / D, None, ALU.mult))
                nc.vector.tensor_scalar(gw[:, 1, 0:D], graw[:, 1, :], wmean[:, 10:11], None, ALU.subtract)
                nc.vector.tensor_copy(gw[:, 0, 0:D], graw[:, 0, :])
                dve.wait_ge(prep_pe, 4)
                for n in range(2):
                    nc.vector.tensor_copy(ga[:, n, :], bank[(5, 2)[n]][:, 0:D])
                    nc.vector.tensor_copy(gw[:, n, D:D + 1], bank[(5, 2)[n]][:, D:D + 1])
                attend_dve(dve, False)[0](-1, 1)
                dve.wait_ge(odd_sem, 2)
                nc.vector.tensor_scalar(flag[:], odd_all, 2 * NC * N / 4.0, None, ALU.is_gt)

        with nc.Block() as block:
            @block.sync
            def _(sp):
                pair_loop(sp, attend_sync(sp)[1], 0, 1, PAIRS // 2 - 2, PAIRS + 1)

            @block.gpsimd
            def _(pool):
                attend_loop(pool, attend_pool(pool))

            @block.scalar
            def _(act):
                attend_loop(act, attend_act(act))

            @block.tensor
            def _(pe):
                def program(more):
                    step, make_more = attend_pe(pe, more)
                    if more:
                        make_more(0, 0)
                    attend_loop(pe, step)

                odd_one = pe.value_load(flag[0:1, 0:1])
                with pe.If(odd_one > 0):
                    program(True)
                with pe.Else():
                    program(False)
                pe.wait_ge(ln_done, PAIRS)

            @block.vector
            def _(dve):
                def program(more):
                    step, keep_more = attend_dve(dve, more)
                    if more:
                        keep_more(0, 0)
                    attend_loop(dve, step)

                odd_one = dve.value_load(flag[0:1, 0:1])
                with dve.If(odd_one > 0):
                    program(True)
                with dve.Else():
                    program(False)
                dve.wait_ge(ln_done, PAIRS)
        attend_ctx.close()

        hidden_bias = sb("hidden_bias", [128, B, NC, N], BF16)
        ff_ctx = ExitStack()
        hid = [sb(f"hid{n}", [128, FC, W2G], F32, ff_ctx) for n in range(2)]

        def ff_pe_hidden(pe, i, b, s, w):
            p = 2 * i + b
            if within(i, p, PAIRS):
                for c in range(FC):
                    if due(FC * (p - 1) + c + 1):
                        pe.wait_ge(s["hid_act"], FC * (p - 1) + c + 1)
                    nc.tensor.matmul(bank[c][:, :], w[:, 128 * c:128 * c + 128], nodes_of(p), start=True,
                                     stop=True).then_inc(s["hid_mm"], 1)

        def ff_pe_out(pe, i, b, s, w):
            p = 2 * i + b
            if within(i, p - 1, PAIRS):
                if due(p - 2):
                    pe.wait_ge(s["y_read"], p - 2)
                for c in range(FC):
                    pe.wait_ge(s["hid_act"], FC * (p - 1) + c + 1)
                    nc.tensor.matmul(bank[4 + (b + 1) % 2][:, :], w[:, c, :], hid[(b + 1) % 2][:, c, :],
                                     start=(c == 0), stop=False)
                nc.tensor.matmul(bank[4 + (b + 1) % 2][:, :], centre[:], nodes_of(p - 1), start=False,
                                 stop=True).then_inc(s["y_mm"], 1)

        def ff_act_hidden(act, i, b, s, func, col):
            p = 2 * i + b
            if within(i, p, PAIRS):
                for c in range(FC):
                    act.wait_ge(s["hid_mm"], FC * p + c + 1)
                    if c == 0:
                        if due(p - 1):
                            act.wait_ge(s["y_mm"], p - 1)
                    nc.scalar.activation(hid[b][:, c, :], bank[c][:, :], func,
                                         bias=cols[:, col + c:col + c + 1]).then_inc(s["hid_act"], 1)

        s1 = {name: sem(f"f1_{name}") for name in ("hid_mm", "hid_act", "y_mm", "y_read")}
        hb_done = sem("hb_done")
        with nc.Block() as block:
            @block.tensor
            def _(pe):
                def step(i, b):
                    ff_pe_hidden(pe, i, b, s1, w1)
                    ff_pe_out(pe, i, b, s1, w2)
                pair_loop(pe, step, 0, 1, PAIRS // 2, PAIRS + 1)

            @block.scalar
            def _(act):
                pair_loop(act, lambda i, b: ff_act_hidden(act, i, b, s1, ACT.Gelu, COL_B1), 0, 1, PAIRS // 2,
                          PAIRS)

            @block.vector
            def _(dve):
                def step(i, b):
                    p = 2 * i + b
                    if within(i, p, PAIRS):
                        nc.vector.tensor_scalar(hidden_bias[:, bass.ds(2 * p, 2)].rearrange("p g c i -> p (g c i)"),
                                                codes[:, bass.ds(2 * p, 2)].rearrange("p g c i -> p (g c i)"), 0.0,
                                                HIDDEN, ALU.is_le, ALU.mult).then_inc(hb_done, 1)
                    if within(i, p - 1, PAIRS):
                        dve.wait_ge(s1["y_mm"], p)
                        nc.vector.tensor_scalar(nodes_of(p - 1), bank[4 + (b + 1) % 2][:, :], ccols[:, 1:2], None,
                                                ALU.add).then_inc(s1["y_read"], 1)
                pair_loop(dve, step, 0, 1, PAIRS // 2, PAIRS + 1)
        ff_ctx.close()

        gat_ctx = ExitStack()
        G_ = lambda name, shape, dt=F32: sb(name, shape, dt, gat_ctx)
        sq_a, sq_b = G_("sq_a", [128, W2G]), G_("sq_b", [128, W2G])
        r_a, r_b = G_("r_a", [128, W2G]), G_("r_b", [128, W2G])
        mid_a, mid_b = G_("mid_a", [128, W2G]), G_("mid_b", [128, W2G])
        y_b = [G_(f"y_b{n}", [128, W2G]) for n in range(2)]
        hop_in = [[G_(f"hop_in{h}{n}", [128, W2G]) for n in range(2)] for h in range(2)]
        logits = [G_(f"logits{h}", [128, 2 * NC, N]) for h in range(2)]
        att = [G_(f"att{h}", [128, 2 * NC, N]) for h in range(2)]
        wh_raw = [[G_(f"wh_raw{h}{n}", [128, 2, NC, D + 1]) for n in range(2)] for h in range(2)]
        wh = [G_(f"wh{h}", [128, 2 * NC, D]) for h in range(2)]
        top = [G_(f"top{h}", [128, 2 * NC]) for h in range(2)]
        shift = [G_(f"shift{h}", [128, 2, 2 * NC]) for h in range(2)]
        hidden_now = [G_(f"hidden_now{h}", [128, 2 * NC, N], BF16) for h in range(2)]
        total = [G_(f"total{h}", [128, 2 * NC]) for h in range(2)]
        inv = [G_(f"inv{h}", [128, 2 * NC]) for h in range(2)]
        per_hop = lambda name: [sem(f"g_{name}{h}") for h in range(2)]
        bc_mm, wh_mm, wh_kept, summed, shifted, exped, whs, out_mm = (per_hop(n) for n in (
            "bc_mm", "wh_mm", "wh_kept", "summed", "shifted", "exped", "whs", "out_mm"))
        hop_ready, hidden_here, chain, chain2 = (per_hop(n) for n in ("hop_ready", "hidden_here", "chain", "chain2"))
        x2_kept, y3_read, sq_ready = sem("x2_kept"), sem("y3_read"), sem("g_sq_ready")
        gvar_mm, gvar_ln, grstd, gmid = (per_hop(n) for n in ("gvar_mm", "gvar_ln", "grstd", "gmid"))
        gln = sem("g_gln")
        BC, WH, OUTB, VARB = (bank[0], bank[3]), (bank[1:3], bank[4:6]), bank[6], bank[7]
        LAG_NORM0, LAG_FRONT, LAG_SCORE, LAG_WEIGH, LAG_BACK, LAG_Y, LAG_NORM1 = 1, (1, 3), (2, 3), (2, 4), (2, 4), 4, 5
        LAG_KEEP = (2, 3)
        gat_loop = lambda eng, step: pair_loop(eng, step, 0, 3, PAIRS // 2, PAIRS + LAG_NORM1)

        with nc.Block() as block:
            @block.tensor
            def _(pe):
                def front(i, b, hop):
                    P, par = 2 * i + b - LAG_FRONT[hop], (b + 1) % 2
                    if not within(i, P, PAIRS):
                        return
                    pe.wait_ge(hop_ready[hop], P + 1)
                    if due(P):
                        pe.wait_ge(summed[hop], P)
                    nc.tensor.matmul(BC[hop][:, :], ga[:, hop, :], hop_in[hop][par][:], start=True,
                                     stop=True).then_inc(bc_mm[hop], 1)
                    if due(P):
                        pe.wait_ge(wh_kept[hop], P)
                    for g in range(2):
                        for c in range(NC):
                            last = nc.tensor.matmul(WH[hop][g][:, (D + 1) * c:(D + 1) * c + D + 1],
                                                    hop_in[hop][par][:, N * g + 128 * c:N * g + 128 * c + 128],
                                                    gw[:, hop, :], start=True, stop=True)
                    last.then_inc(wh_mm[hop], 1)

                def back(i, b, hop):
                    p = 2 * i + b
                    P = p - LAG_BACK[hop]
                    if not within(i, P, PAIRS):
                        return
                    if hop == 0:
                        if due(p - 3):
                            pe.wait_ge(y3_read, p - 3)
                    else:
                        pe.wait_ge(hop_ready[1], at_most(p - 2, PAIRS))
                        pe.wait_ge(x2_kept, P + 1)
                        nc.tensor.matmul(OUTB[:, :], centre[:], nodes_of(P), start=True, stop=False)
                    pe.wait_ge(whs[hop], P + 1)
                    for g in range(2):
                        for c in range(NC):
                            last = nc.tensor.matmul(OUTB[:, N * g:N * g + N], wh[hop][:, NC * g + c, :],
                                                    att[hop][:, NC * g + c, :], start=(hop == 0 and c == 0),
                                                    stop=(c == NC - 1 and (hop == 0 or g == 1)))
                    last.then_inc(out_mm[hop], 1)

                def variance0(i, b):
                    P = 2 * i + b
                    if not within(i, P, PAIRS):
                        return
                    pe.wait_ge(sq_ready, P + 1)
                    if due(P - 4):
                        pe.wait_ge(gvar_ln[1], P - 4)
                    nc.tensor.matmul(VARB[:, :], mean_w[:], sq_a[:], start=True, stop=True).then_inc(gvar_mm[0], 1)

                def variance1(i, b):
                    p = 2 * i + b
                    P = p - LAG_Y
                    if not within(i, P, PAIRS):
                        return
                    pe.wait_ge(y3_read, P + 1)
                    pe.wait_ge(gvar_ln[0], at_most(p + 1, PAIRS))
                    nc.tensor.matmul(VARB[:, :], mean_w[:], sq_b[:], start=True, stop=True).then_inc(gvar_mm[1], 1)

                def step(i, b):
                    front(i, b, 1)
                    variance0(i, b)
                    back(i, b, 1)
                    front(i, b, 0)
                    variance1(i, b)
                    back(i, b, 0)

                gat_loop(pe, step)

            @block.scalar
            def _(act):
                act.preload_act_table_set("natural_log_exp_and_others")

                def exps(i, b, hop):
                    P = 2 * i + b - LAG_SCORE[hop]
                    if not within(i, P, PAIRS):
                        return
                    act.wait_ge(shifted[hop], P + 1)
                    if due(P):
                        act.wait_ge(out_mm[hop], P)
                    for side, scale, dst in ((0, 1.0, att), (1, SLOPE, logits)):
                        for n in range(2 * NC):
                            last = nc.scalar.activation(dst[hop][:, n, :], logits[hop][:, n, :], ACT.Exp,
                                                        bias=shift[hop][:, side, n:n + 1], scale=scale)
                    last.then_inc(exped[hop], 1)

                def inverse_std(i, b, n):
                    P = 2 * i + b - (0, LAG_NORM1)[n]
                    if not within(i, P, PAIRS):
                        return
                    r = (r_a, r_b)[n]
                    act.wait_ge(gvar_mm[n], P + 1)
                    if due(P):
                        act.wait_ge(gmid[n], P)
                    nc.scalar.activation(r[:], VARB[:, :], ACT.Ln, bias=eps[:, 0:1]).then_inc(gvar_ln[n], 1)
                    act.wait_ge(gvar_ln[n], P + 1)
                    nc.scalar.activation(r[:], r[:], ACT.Exp, scale=-0.5).then_inc(grstd[n], 1)

                def keep_wh(i, b, hop):
                    P, par = 2 * i + b - LAG_KEEP[hop], (b + LAG_KEEP[hop]) % 2
                    if not within(i, P, PAIRS):
                        return
                    act.wait_ge(wh_mm[hop], P + 1)
                    if due(P - 1):
                        act.wait_ge(whs[hop], P - 1)
                    for g in range(2):
                        last = nc.scalar.copy(wh_raw[hop][par][:, g].rearrange("p c d -> p (c d)"),
                                              WH[hop][g][:, 0:NC * (D + 1)])
                    last.then_inc(wh_kept[hop], 1)

                def second_input(i, b):
                    P, par = 2 * i + b - 3, (b + 1) % 2
                    if not within(i, P, PAIRS):
                        return
                    act.wait_ge(out_mm[0], P + 1)
                    if due(P - 1):
                        act.wait_ge(wh_mm[1], P - 1)
                    nc.scalar.copy(hop_in[1][par][:], OUTB[:, :]).then_inc(hop_ready[1], 1)

                def squares0(i, b):
                    P = 2 * i + b
                    if not within(i, P, PAIRS):
                        return
                    if due(P):
                        act.wait_ge(gvar_mm[0], P)
                    nc.scalar.activation(sq_a[:], nodes_of(P), ACT.Square).then_inc(sq_ready, 1)

                def output(i, b):
                    P = 2 * i + b - LAG_Y
                    if not within(i, P, PAIRS):
                        return
                    act.wait_ge(out_mm[1], P + 1)
                    if due(P - 1):
                        act.wait_ge(gmid[1], P - 1)
                    nc.scalar.copy(y_b[b][:], OUTB[:, :])
                    if due(P):
                        act.wait_ge(gvar_mm[1], P)
                    nc.scalar.activation(sq_b[:], OUTB[:, :], ACT.Square).then_inc(y3_read, 1)

                def step(i, b):
                    keep_wh(i, b, 0)
                    second_input(i, b)
                    inverse_std(i, b, 1)
                    squares0(i, b)
                    exps(i, b, 0)
                    keep_wh(i, b, 1)
                    inverse_std(i, b, 0)
                    output(i, b)
                    exps(i, b, 1)

                gat_loop(act, step)

            @block.gpsimd
            def _(pool):
                def mask_here(i, b, hop):
                    P = 2 * i + b - LAG_FRONT[hop]
                    if not within(i, P, PAIRS):
                        return
                    if due(P):
                        pool.wait_ge(summed[hop], P)
                        pool.sem_inc(passed, 1)
                    nc.gpsimd.tensor_copy(hidden_now[hop][:].rearrange("p n i -> p (n i)"),
                                          hidden_bias[:, bass.ds(2 * P, 2)].rearrange(
                                              "p g c i -> p (g c i)")).then_inc(hidden_here[hop], 1)

                def step(i, b):
                    mask_here(i, b, 1)
                    P = 2 * i + b - LAG_NORM0
                    if within(i, P, PAIRS):
                        pool.wait_ge(hop_ready[0], P + 1)
                        pool.sem_inc(passed, 1)
                        nc.gpsimd.tensor_copy(nodes_of(P), hop_in[0][(b + 1) % 2][:]).then_inc(x2_kept, 1)
                    mask_here(i, b, 0)

                gat_loop(pool, step)

            @block.vector
            def _(dve):
                def score(i, b, hop):
                    P = 2 * i + b - LAG_SCORE[hop]
                    if not within(i, P, PAIRS):
                        return
                    wh2 = wh_raw[hop][(b + LAG_SCORE[hop]) % 2][:, :, :, D].rearrange("p g c -> p (g c)")
                    dve.wait_ge(hidden_here[hop], P + 1)
                    dve.sem_inc(passed, 1)
                    dve.wait_ge(bc_mm[hop], P + 1)
                    dve.sem_inc(passed, 1)
                    for g in range(2):
                        for c in range(NC):
                            n = NC * g + c
                            last = nc.vector.tensor_tensor_reduce(
                                logits[hop][:, n, :], BC[hop][:, N * g:N * g + N],
                                hidden_now[hop][:, n, :], 1.0,
                                -3.0e38, ALU.add, ALU.max, top[hop][:, n:n + 1])
                    last.then_inc(summed[hop], 1)
                    dve.wait_ge(wh_kept[hop], P + 1)
                    dve.wait_ge(summed[hop], P + 1)
                    nc.vector.tensor_tensor(top[hop][:], top[hop][:], wh2, ALU.add).then_inc(chain[hop], 1)
                    dve.wait_ge(chain[hop], 2 * P + 1)
                    nc.vector.scalar_tensor_tensor(out=top[hop][:], in0=top[hop][:], scalar=SLOPE, in1=top[hop][:],
                                                   op0=ALU.mult, op1=ALU.max).then_inc(chain[hop], 1)
                    dve.wait_ge(chain[hop], 2 * P + 2)
                    nc.vector.tensor_tensor(shift[hop][:, 0, :], wh2, top[hop][:], ALU.subtract)
                    nc.vector.scalar_tensor_tensor(out=shift[hop][:, 1, :], in0=wh2, scalar=SLOPE,
                                                   in1=top[hop][:], op0=ALU.mult,
                                                   op1=ALU.subtract).then_inc(shifted[hop], 1)

                def weigh(i, b, hop):
                    P = 2 * i + b - LAG_WEIGH[hop]
                    if not within(i, P, PAIRS):
                        return
                    dve.wait_ge(exped[hop], P + 1)
                    for n in range(2 * NC):
                        last = nc.vector.scalar_tensor_tensor(out=att[hop][:, n, :], in0=att[hop][:, n, :], scalar=1.0,
                                                              in1=logits[hop][:, n, :], op0=ALU.mult, op1=ALU.max,
                                                              accum_out=total[hop][:, n:n + 1])
                    last.then_inc(chain2[hop], 1)
                    dve.wait_ge(chain2[hop], 2 * P + 1)
                    nc.vector.reciprocal(inv[hop][:], total[hop][:]).then_inc(chain2[hop], 1)
                    dve.wait_ge(chain2[hop], 2 * P + 2)
                    if due(P):
                        dve.wait_ge(out_mm[hop], P)
                    for n in range(2 * NC):
                        last = nc.vector.tensor_scalar(wh[hop][:, n, :],
                                                       wh_raw[hop][(b + LAG_WEIGH[hop]) % 2][:, n // NC, n % NC, 0:D],
                                                       inv[hop][:, n:n + 1], None, ALU.mult)
                    last.then_inc(whs[hop], 1)

                def norm0(i, b):
                    P, par = 2 * i + b - LAG_NORM0, (b + 1) % 2
                    if not within(i, P, PAIRS):
                        return
                    dve.wait_ge(grstd[0], P + 1)
                    nc.vector.tensor_tensor(mid_a[:], nodes_of(P), r_a[:], ALU.mult).then_inc(gmid[0], 1)
                    dve.wait_ge(gmid[0], P + 1)
                    if due(P - 1):
                        dve.wait_ge(wh_mm[0], P - 1)
                        dve.wait_ge(x2_kept, P - 1)
                    g = COL["L0_gnn_g2"]
                    nc.vector.tensor_scalar(hop_in[0][par][:], mid_a[:], cols[:, g:g + 1], cols[:, g + 1:g + 2],
                                            ALU.mult, ALU.add).then_inc(hop_ready[0], 1)

                def norm1(i, b):
                    P, par = 2 * i + b - LAG_NORM1, (b + 1) % 2
                    if not within(i, P, PAIRS):
                        return
                    dve.wait_ge(grstd[1], P + 1)
                    if due(P):
                        dve.wait_ge(gln, P)
                    nc.vector.tensor_tensor(mid_b[:], y_b[par][:], r_b[:], ALU.mult).then_inc(gmid[1], 1)
                    dve.wait_ge(gmid[1], P + 1)
                    g = COL["L1_gnn_g_ln1"]
                    nc.vector.tensor_scalar(nodes_of(P), mid_b[:], cols[:, g:g + 1], cols[:, g + 1:g + 2],
                                            ALU.mult, ALU.add).then_inc(gln, 1)

                def step(i, b):
                    score(i, b, 0)
                    weigh(i, b, 1)
                    norm0(i, b)
                    score(i, b, 1)
                    weigh(i, b, 0)
                    norm1(i, b)

                gat_loop(dve, step)
        gat_ctx.close()

        ff_ctx = ExitStack()
        F_ = lambda name, shape, dt=F32: sb(name, shape, dt, ff_ctx)
        hid = [F_(f"hid_r{n}", [128, FC, W2G]) for n in range(2)]
        fy, fsq, fr, fmid, fo = (F_(n, [128, W2G]) for n in ("fy", "fsq", "fr", "fmid", "fo"))
        o_nat = [F_(f"o_nat{n}", [128, 2 * NC, D]) for n in range(2)]
        s2 = {name: sem(f"f2_{name}") for name in ("hid_mm", "hid_act", "y_mm", "y_read", "var_mm", "var_ln", "rstd",
                                                  "mid", "normed", "o_mm", "o_ready")}
        o_out = [sem(f"o_out{n}") for n in range(2)]
        last_loop = lambda eng, step: pair_loop(eng, step, 0, 2, PAIRS // 2, PAIRS + 3)

        with nc.Block() as block:
            @block.tensor
            def _(pe):
                def step(i, b):
                    p = 2 * i + b
                    ff_pe_hidden(pe, i, b, s2, wf1)
                    if within(i, p - 2, PAIRS):
                        pe.wait_ge(s2["y_read"], p - 1)
                        if due(p - 2):
                            pe.wait_ge(s2["var_ln"], p - 2)
                        nc.tensor.matmul(bank[6][:, :], mean_w[:], fsq[:], start=True, stop=True).then_inc(s2["var_mm"], 1)
                    ff_pe_out(pe, i, b, s2, wf2)
                    if within(i, p - 3, PAIRS):
                        pe.wait_ge(s2["normed"], p - 2)
                        if due(p - 3):
                            pe.wait_ge(s2["o_ready"], p - 3)
                        for n in range(2 * NC):
                            last = nc.tensor.transpose(bank[7][:, 128 * n:128 * n + 128], fo[:, 128 * n:128 * n + 128],
                                                       ident[:])
                        last.then_inc(s2["o_mm"], 1)
                last_loop(pe, step)

            @block.scalar
            def _(act):
                act.preload_act_table_set("natural_log_exp_and_others")

                def step(i, b):
                    p = 2 * i + b
                    ff_act_hidden(act, i, b, s2, ACT.Relu, COL_BFF1)
                    if within(i, p - 2, PAIRS):
                        act.wait_ge(s2["var_mm"], p - 1)
                        if due(p - 2):
                            act.wait_ge(s2["mid"], p - 2)
                        nc.scalar.activation(fr[:], bank[6][:, :], ACT.Ln, bias=eps[:, 0:1]).then_inc(s2["var_ln"], 1)
                        act.wait_ge(s2["var_ln"], p - 1)
                        nc.scalar.activation(fr[:], fr[:], ACT.Exp, scale=-0.5).then_inc(s2["rstd"], 1)
                    if within(i, p - 1, PAIRS):
                        act.wait_ge(s2["y_mm"], p)
                        if due(at_most(p - 1, PAIRS)):
                            act.wait_ge(s2["mid"], at_most(p - 1, PAIRS))
                        if due(p - 1):
                            act.wait_ge(s2["var_mm"], p - 1)
                        nc.scalar.activation(fy[:], bank[4 + (b + 1) % 2][:, :], ACT.Identity, bias=ccols[:, 2:3])
                        nc.scalar.activation(fsq[:], bank[4 + (b + 1) % 2][:, :], ACT.Square,
                                             bias=ccols[:, 2:3]).then_inc(s2["y_read"], 1)
                last_loop(act, step)

            @block.vector
            def _(dve):
                def step(i, b):
                    p = 2 * i + b
                    if within(i, p - 2, PAIRS):
                        dve.wait_ge(s2["rstd"], p - 1)
                        if due(p - 2):
                            dve.wait_ge(s2["normed"], p - 2)
                        nc.vector.tensor_tensor(fmid[:], fy[:], fr[:], ALU.mult).then_inc(s2["mid"], 1)
                        dve.wait_ge(s2["mid"], p - 1)
                        if due(p - 2):
                            dve.wait_ge(s2["o_mm"], p - 2)
                        g = COL["L1_gnn_g_ln2"]
                        nc.vector.tensor_scalar(fo[:], fmid[:], cols[:, g:g + 1], cols[:, g + 1:g + 2], ALU.mult,
                                                ALU.add).then_inc(s2["normed"], 1)
                    if within(i, p - 3, PAIRS):
                        dve.wait_ge(s2["o_mm"], p - 2)
                        half = i + (b - 5) // 2
                        if due(16 * (half + 1)):
                            dve.wait_ge(o_out[(b + 1) % 2], 16 * (half + 1))
                        nc.vector.tensor_copy(o_nat[(b + 1) % 2][:].rearrange("p n d -> p (n d)"),
                                              bank[7][:, :]).then_inc(s2["o_ready"], 1)
                last_loop(dve, step)

            @block.sync
            def _(sp):
                def step(i, b):
                    p = 2 * i + b
                    if within(i, p - 3, PAIRS):
                        sp.wait_ge(s2["o_ready"], p - 2)
                        sp.sem_inc(passed, 1)
                        sp.dma_start(out[bass.ds(2 * (p - 3), 2)].rearrange("g (c p) d -> p (g c) d", c=NC),
                                     o_nat[(b + 1) % 2][:]).then_inc(o_out[(b + 1) % 2], 16)
                last_loop(sp, step)
                for n in range(2):
                    sp.wait_ge(o_out[n], 16 * PAIRS // 2)
        ff_ctx.close()


_INS = ["x", "adj", "L0_gnn_Wq", "L0_gnn_bq", "L0_gnn_Wk", "L0_gnn_bk", "L0_gnn_Wv", "L0_gnn_bv", "L0_gnn_Wo",
        "L0_gnn_bo", "L0_gnn_W1", "L0_gnn_b1", "L0_gnn_W2", "L0_gnn_b2", "L0_gnn_g1", "L0_gnn_beta1", "L0_gnn_g2",
        "L0_gnn_beta2", "L1_gnn_W1", "L1_gnn_a1", "L1_gnn_W2", "L1_gnn_a2", "L1_gnn_w_ff1", "L1_gnn_b_ff1",
        "L1_gnn_w_ff2", "L1_gnn_b_ff2", "L1_gnn_g_ln1", "L1_gnn_b_ln1", "L1_gnn_g_ln2", "L1_gnn_b_ln2"]


def kernel(**inputs):
    import numpy as _np
    import concourse.bacc as _bacc
    from concourse import mybir as _mybir
    from concourse.bass_utils import run_bass_kernel_spmd as _run

    nc = _bacc.Bacc("TRN2", target_bir_lowering=False, num_devices=1)
    arrays, args = {}, {}
    for name in _INS:
        arr = _np.ascontiguousarray(inputs[name])
        arrays[f"in_{name}"] = arr
        args[name] = nc.dram_tensor(f"in_{name}", arr.shape, _mybir.dt.from_np(arr.dtype), kind="ExternalInput").ap()
    out = nc.dram_tensor("out_0", (B, N, D), _mybir.dt.float32, kind="ExternalOutput").ap()
    build(nc, args, out)
    r = _run(nc, [arrays], core_ids=[0])
    return r.results[0]["out_0"]
```

```python
from contextlib import ExitStack

import concourse.bass as bass
from concourse import mybir

F32 = mybir.dt.float32
BF16 = mybir.dt.bfloat16
I32 = mybir.dt.int32
I8 = mybir.dt.int8
ALU = mybir.AluOpType
ACT = mybir.ActivationFunctionType
AX = mybir.AxisListType.X
RMAX = bass.bass_isa.ReduceOp.max

B, N, D = 32, 256, 128
H, DH = 8, 16
R = 4
FF = 512
FC = FF // D
NC = N // 128
PAIRS = B // 2
W2G = 2 * N
EPS = 1e-5
SLOPE = 0.2
HIDDEN = -(2.0 ** 53)
PARTS = 3
TERMS = 6
ROWS = TERMS * DH
ROWSM = ROWS + PARTS
ADJ_BUFS = 4
UNITS = 8
GRP = 4

VECS = ["L0_gnn_g1", "L0_gnn_beta1", "L0_gnn_g2", "L0_gnn_beta2",
        "L1_gnn_g_ln1", "L1_gnn_b_ln1", "L1_gnn_g_ln2", "L1_gnn_b_ln2"]
CENTRED = ["L0_gnn_bo", "L0_gnn_b2", "L1_gnn_b_ff2"]
COL = {name: n for n, name in enumerate(VECS)}
COL_B1 = len(VECS)
COL_BFF1 = COL_B1 + FC
COL_A = COL_BFF1 + FC
NROWS = COL_A + 4


def due(value):
    return not isinstance(value, int) or value > 0


def pair_loop(eng, step, start, loop_from, loop_to, end):
    for p in range(start, 2 * loop_from):
        step(p // 2, p % 2)
    with eng.Fori(loop_from, loop_to) as i:
        for b in range(2):
            step(i, b)
    for p in range(2 * loop_to, end):
        step(p // 2, p % 2)


def adj_loop(eng, step, start, end):
    for p in range(start, ADJ_BUFS):
        step(p // ADJ_BUFS, p % ADJ_BUFS)
    with eng.Fori(1, PAIRS // ADJ_BUFS) as i:
        for n in range(ADJ_BUFS):
            step(i, n)
    for p in range(PAIRS, end):
        step(p // ADJ_BUFS, p % ADJ_BUFS)


def attend_loop(eng, step):
    pair_loop(eng, step, 0, 1, PAIRS // 2 - 1, PAIRS + 1)


def at_most(value, most):
    return min(value, most) if isinstance(value, int) else value


def within(i, index, count):
    return not isinstance(i, int) or 0 <= index < count


def build(nc, a, out):
    ctx = ExitStack()
    with ctx:
        def sb(name, shape, dt=F32, where=ctx):
            return where.enter_context(nc.sbuf_tensor(name, shape, dt))

        def sem(name):
            return ctx.enter_context(nc.semaphore(name))

        bank = [ctx.enter_context(nc.psum_tensor(f"bank{n}", [128, 512], F32)) for n in range(8)]

        x_all = sb("x_all", [128, B * N])
        codes = sb("codes", [128, B, NC, N], I8)
        ident = sb("ident", [128, 128])
        identb = sb("identb", [128, 128], BF16)
        centre = sb("centre", [128, 128])
        mean_w = sb("mean_w", [128, 128])
        eps = sb("eps", [128, 1])
        cols = sb("cols", [128, NROWS])
        ccols = sb("ccols", [128, len(CENTRED)])
        w1 = sb("w1", [128, FF])
        w2 = sb("w2", [128, FC, D])
        wf1 = sb("wf1", [128, FF])
        wf2 = sb("wf2", [128, FC, D])
        gw = sb("gw", [128, 2, D + 1])
        ga = sb("ga", [128, 2, D])

        flag = sb("flag", [128, 1], I32)

        nodes_of = lambda pair: x_all[:, bass.ds(pair * W2G, W2G)]

        attend_ctx = ExitStack()
        A = lambda name, shape, dt=F32: sb(name, shape, dt, attend_ctx)
        wq = A("wq", [128, D])
        wk = A("wk", [128, D])
        qk_cols = A("qk_cols", [128, 2])
        wv = A("wv", [128, R + 1, D])
        bvb = A("bvb", [128, R + 1, D])
        wo = A("wo", [128, 2, D])

        parts = A("parts", [128, 2, PARTS, W2G], BF16)
        whole = A("whole", [128, 2, W2G])
        rest = A("rest", [128, 2, W2G])
        x_nat = [A(f"x_nat{n}", [128, 2 * NC, D]) for n in range(2)]
        x_t = [A(f"x_t{n}", [128, W2G]) for n in range(2)]
        q_st = [A(f"q_st{n}", [ROWSM, H, N], BF16) for n in range(4)]
        k_st = [A(f"k_st{n}", [ROWSM, H, N], BF16) for n in range(4)]
        v_base = [A(f"v_base{n}", [128, 2, NC, H, 32]) for n in range(2)]
        v_one = [A(f"v_one{n}", [128, 2, NC, H, DH]) for n in range(2)]
        v_more = [A(f"v_more{n}", [128, 2, NC, R - 1, H, DH]) for n in range(2)]
        probs = A("probs", [128, UNITS, 512])
        probs_one = A("probs_one", [128, UNITS, 512])
        probs_more = A("probs_more", [128, R - 1, 2, 512])
        more_tmp = A("more_tmp", [128, 512])
        row_max = [A(f"row_max{n}", [128, NC, H]) for n in range(2)]
        neg_max = A("neg_max", [128, NC, H])
        max_rest = A("max_rest", [128, NC, H])
        max_parts = A("max_parts", [128, NC, PARTS, H], BF16)
        max_t = A("max_t", [PARTS * H, N], BF16)
        denom = A("denom", [128, 512])
        denom_r = A("denom_r", [128, 512])
        mixed = A("mixed", [128, 2, W2G])
        ln_y = A("ln_y", [128, W2G])
        ln_sq = A("ln_sq", [128, W2G])
        ln_r = A("ln_r", [128, W2G])

        scr_parts = nc.dram_tensor("scr_parts", [PAIRS, 2, PARTS, 2, DH * H, N], BF16).ap()
        scr_max = nc.dram_tensor("scr_max", [B, PARTS * H, N], BF16).ap()

        x_in = [sem(f"x_in{n}") for n in range(2)]
        xt_mm, xt_ready, x_kept = sem("xt_mm"), sem("xt_ready"), sem("x_kept")
        qk_mid = sem("qk_mid")
        qk_mm, qk_whole, qk_rest, qk_split, parts_out = (sem("qk_mm"), sem("qk_whole"), sem("qk_rest"),
                                                         sem("qk_split"), sem("parts_out"))
        stacked = [sem(f"stacked{n}") for n in range(4)]
        s_mm, s_max, max_split, maxt_mm, maxt_ready = (sem("s_mm"), sem("s_max"), sem("max_split"), sem("maxt_mm"),
                                                       sem("maxt_ready"))
        max_out, max_in, msp = sem("max_out"), sem("max_in"), sem("msp")
        st_mm, exp_done, masked, pv_mm = sem("st_mm"), sem("exp_done"), sem("masked"), sem("pv_mm")
        v_mm, v_ready0, v_ready1, v_init, ones_init = (sem("v_mm"), sem("v_ready0"), sem("v_ready1"), sem("v_init"),
                                                       sem("ones_init"))
        den_ready, den_ln, den_inv, normed = sem("den_ready"), sem("den_ln"), sem("den_inv"), sem("normed")
        y_mm, y_read, var_mm, var_ln, rstd, ln_mid, ln_done = (sem("y_mm"), sem("y_read"), sem("var_mm"),
                                                              sem("var_ln"), sem("rstd"), sem("ln_mid"),
                                                              sem("ln_done"))
        vmore_mm, vmore_ready, more_done = sem("vmore_mm"), sem("vmore_ready"), sem("more_done")
        S_BANK, T_BANK, PV_BANK = bank[0:2], bank[2:4], bank[4:6]
        M0, M1 = bank[6], bank[7]

        passed = sem("passed")

        def attend_sync(sp):
            def x_load(pair, n):
                sp.dma_start(x_nat[n][:], a["x"][bass.ds(2 * pair, 2)].rearrange(
                    "g (c p) d -> p (g c) d", c=NC)).then_inc(x_in[n], 16)

            def stack_load(i, b, k):
                G, n = 4 * i + 2 * b + k, (2 * b + k) % 4
                if not within(i, G, B):
                    return
                P, gi = 2 * i + b + k // 2, k % 2
                sp.wait_ge(parts_out, 16 * (P + 1))
                sp.sem_inc(passed, 1)
                if due(UNITS * (G - 3)):
                    sp.wait_ge(st_mm, UNITS * (G - 3))
                    sp.sem_inc(passed, 1)
                src = scr_parts[bass.ds(P, 1)].rearrange("o t s g (d h) i -> g (o t s) d (h i)", h=H)[gi]
                slot = 0
                for run in range(PARTS, 0, -1):
                    rows_of = slice(DH * slot, DH * (slot + run))
                    sp.dma_start(q_st[n][rows_of].rearrange("p h i -> p (h i)"),
                                 src[0:run]).then_inc(stacked[n], 16)
                    at = PARTS + PARTS - run
                    sp.dma_start(k_st[n][rows_of].rearrange("p h i -> p (h i)"),
                                 src[at:at + 1].broadcast_to([run, DH, H * N])).then_inc(stacked[n], 16)
                    slot += run

            def max_rows(i, b, k):
                G, n = 4 * i + 2 * b + k, (2 * b + k) % 4
                if not within(i, G, B):
                    return
                sp.wait_ge(maxt_ready, G + 1)
                sp.sem_inc(passed, 1)
                sp.dma_start(scr_max[bass.ds(G, 1)].rearrange("o r i -> (o r) i"), max_t[:]).then_inc(max_out, 16)
                sp.wait_ge(max_out, 16 * (G + 1))
                sp.sem_inc(passed, 1)
                sp.dma_start(q_st[n][ROWS:ROWSM, :, :], scr_max[bass.ds(G, 1)].rearrange(
                    "o (s h) i -> (o s) h i", s=PARTS)).then_inc(max_in, 16)

            def step(i, b):
                p = 2 * i + b
                stack_load(i, b, 3)
                if within(i, p + 3, PAIRS):
                    if due(p + 2):
                        sp.wait_ge(xt_mm, p + 2)
                        sp.sem_inc(passed, 1)
                    x_load(p + 3, (b + 1) % 2)
                max_rows(i, b, 1)
                if within(i, p + 2, PAIRS):
                    sp.wait_ge(qk_split, 2 * (p + 3))
                    sp.sem_inc(passed, 1)
                    sp.dma_start(scr_parts[bass.ds(p + 2, 1)].rearrange("o t s g r i -> r (o t s g) i"),
                                 parts[:].rearrange("p t s (g i) -> p (t s g) i", g=2)).then_inc(parts_out, 16)
                max_rows(i, b, 2)
                stack_load(i, b, 4)

            return x_load, step

        def attend_pool(pool):
            def split(P):
                for t in range(2):
                    pool.wait_ge(qk_whole, 2 * P + t + 1)
                    pool.sem_inc(passed, 1)
                    nc.gpsimd.tensor_tensor(rest[:, t, :], whole[:, t, :], parts[:, t, 0, :],
                                            ALU.subtract).then_inc(qk_rest, 1)
                for t in range(2):
                    pool.wait_ge(qk_mid, 2 * P + t + 1)
                    pool.sem_inc(passed, 1)
                    nc.gpsimd.tensor_tensor(parts[:, t, 2, :], rest[:, t, :], parts[:, t, 1, :],
                                            ALU.subtract).then_inc(qk_split, 1)

            def split_max(i, b, k):
                G, n = 4 * i + 2 * b + k, k % 2
                if not within(i, G, B):
                    return
                pool.wait_ge(s_max, UNITS * (G + 1))
                pool.sem_inc(passed, 1)
                if due(G):
                    pool.wait_ge(maxt_mm, G)
                    pool.sem_inc(passed, 1)
                nc.gpsimd.tensor_scalar(neg_max[:], row_max[n][:], -1.0, 0.0, ALU.mult, ALU.add).then_inc(msp, 1)
                pool.wait_ge(msp, 4 * G + 1)
                pool.sem_inc(passed, 1)
                nc.gpsimd.tensor_copy(max_parts[:, :, 0, :], neg_max[:]).then_inc(msp, 1)
                pool.wait_ge(msp, 4 * G + 2)
                pool.sem_inc(passed, 1)
                nc.gpsimd.tensor_tensor(max_rest[:], neg_max[:], max_parts[:, :, 0, :], ALU.subtract).then_inc(msp, 1)
                pool.wait_ge(msp, 4 * G + 3)
                pool.sem_inc(passed, 1)
                nc.gpsimd.tensor_copy(max_parts[:, :, 1, :], max_rest[:]).then_inc(msp, 1)
                pool.wait_ge(msp, 4 * G + 4)
                pool.sem_inc(passed, 1)
                nc.gpsimd.tensor_tensor(max_parts[:, :, 2, :], max_rest[:], max_parts[:, :, 1, :],
                                        ALU.subtract).then_inc(max_split, 1)

            def step(i, b):
                p = 2 * i + b
                split_max(i, b, 1)
                if within(i, p + 2, PAIRS):
                    split(p + 2)
                split_max(i, b, 2)

            return step

        def attend_act(act):
            def exp_unit(i, b, k, u):
                G = 4 * i + 2 * b + k
                act.wait_ge(st_mm, UNITS * G + u + 1)
                if due(4 * (G - 1) + u // 2 + 1):
                    act.wait_ge(pv_mm, 4 * (G - 1) + u // 2 + 1)
                nc.scalar.activation(probs[:, u, :], T_BANK[u % 2][:, :], ACT.Exp).then_inc(exp_done, 1)

            def whole_qk(P, t, src, scale, bias):
                act.wait_ge(qk_mm, 2 * P + t + 1)
                if due(2 * P + t - 1):
                    act.wait_ge(qk_split, 2 * P + t - 1)
                nc.scalar.activation(whole[:, t, :], src[:, :], ACT.Identity, bias=bias, scale=scale)
                if due(16 * P):
                    act.wait_ge(parts_out, 16 * P)
                nc.scalar.activation(parts[:, t, 0, :], src[:, :], ACT.Identity, bias=bias,
                                     scale=scale).then_inc(qk_whole, 1)

            def max_copy(i, b, k):
                G = 4 * i + 2 * b + k
                if not within(i, G, B):
                    return
                act.wait_ge(maxt_mm, G + 1)
                if due(16 * G):
                    act.wait_ge(max_out, 16 * G)
                nc.scalar.copy(max_t[:], M1[:, :].bitcast(BF16)[0:PARTS * H, 0:N]).then_inc(maxt_ready, 1)

            def inverse_denominators(G):
                act.wait_ge(den_ready, G + 1)
                nc.scalar.activation(denom[:], denom[:], ACT.Ln).then_inc(den_ln, 1)
                act.wait_ge(den_ln, G + 1)
                if due(G):
                    act.wait_ge(normed, G)
                nc.scalar.activation(denom_r[:], denom[:], ACT.Exp, scale=-1.0).then_inc(den_inv, 1)

            def step(i, b):
                p = 2 * i + b
                for slot in range(2):
                    G = 2 * p + slot
                    for u in range(UNITS):
                        if within(i, G, B):
                            exp_unit(i, b, slot, u)
                        if u == 1 + slot:
                            max_copy(i, b, slot + 1)
                        if u == 4 and within(i, G - 1, B):
                            inverse_denominators(G - 1)
                        if slot == 0:
                            P = p + 2
                            if u == 0 and within(i, P, PAIRS):
                                act.wait_ge(xt_mm, P + 1)
                                if due(2 * (P - 1)):
                                    act.wait_ge(v_mm, 2 * (P - 1))
                                nc.scalar.copy(x_t[b][:], M0[:, :]).then_inc(xt_ready, 1)
                                nc.scalar.copy(nodes_of(P), M0[:, :]).then_inc(x_kept, 1)
                            if u == 2 and within(i, P, PAIRS):
                                whole_qk(P, 0, M0, DH ** -0.5, qk_cols[:, 0:1])
                            if u == 3 and within(i, P, PAIRS):
                                whole_qk(P, 1, M1, 1.0, qk_cols[:, 1:2])
                            if u in (4, 5) and within(i, P, PAIRS):
                                t = u - 4
                                act.wait_ge(qk_rest, 2 * P + t + 1)
                                nc.scalar.copy(parts[:, t, 1, :], rest[:, t, :]).then_inc(qk_mid, 1)
                            if u == 7 and within(i, p - 1, PAIRS):
                                act.wait_ge(y_mm, p)
                                if due(p - 1):
                                    act.wait_ge(ln_done, p - 1)
                                nc.scalar.activation(ln_y[:], M0[:, :], ACT.Identity, bias=ccols[:, 0:1])
                                nc.scalar.activation(ln_sq[:], M0[:, :], ACT.Square,
                                                     bias=ccols[:, 0:1]).then_inc(y_read, 1)
                        elif u == 3 and within(i, p - 1, PAIRS):
                            act.wait_ge(var_mm, p)
                            nc.scalar.activation(ln_r[:], M0[:, :], ACT.Ln, bias=eps[:, 0:1]).then_inc(var_ln, 1)
                            act.wait_ge(var_ln, p)
                            nc.scalar.activation(ln_r[:], ln_r[:], ACT.Exp, scale=-0.5).then_inc(rstd, 1)
                        elif u == 6 and within(i, p - 1, PAIRS):
                            act.wait_ge(ln_mid, p)
                            g = COL["L0_gnn_g1"]
                            nc.scalar.activation(nodes_of(p - 1), ln_y[:], ACT.Identity, bias=cols[:, g + 1:g + 2],
                                                 scale=cols[:, g:g + 1]).then_inc(ln_done, 1)

            return step

        def attend_pe(pe, more):
            def scores(i, b, k, u):
                G, n = 4 * i + 2 * b + k, (2 * b + k) % 4
                if not within(i, G, B):
                    return
                if u == 0:
                    quarter = i + (2 * b + k) // 4
                    pe.wait_ge(stacked[n], 16 * 2 * PARTS * (quarter + 1))
                if due(UNITS * G + u - 1):
                    pe.wait_ge(s_max, UNITS * G + u - 1)
                c = u // 4
                for j in range(2):
                    h = 2 * (u % 4) + j
                    last = nc.tensor.matmul(S_BANK[u % 2][:, N * j:N * j + N],
                                            q_st[n][0:ROWS, h, 128 * c:128 * c + 128],
                                            k_st[n][0:ROWS, h, :], start=True, stop=True)
                last.then_inc(s_mm, 1)

            def scores_t(i, b, k, u):
                G, n = 4 * i + 2 * b + k, (2 * b + k) % 4
                if not within(i, G, B):
                    return
                if u == 0:
                    pe.wait_ge(max_in, 16 * (G + 1))
                if due(UNITS * G + u - 1):
                    pe.wait_ge(exp_done, UNITS * G + u - 1)
                c = (u // 2) % 2
                for j in range(2):
                    h = GRP * (u // 4) + 2 * (u % 2) + j
                    last = nc.tensor.matmul(T_BANK[u % 2][:, N * j:N * j + N],
                                            k_st[n][:, h, 128 * c:128 * c + 128],
                                            q_st[n][:, h, :], start=True, stop=True)
                last.then_inc(st_mm, 1)

            def values(i, b, k, q):
                G = 4 * i + 2 * b + k
                if not within(i, G, B):
                    return
                par, gi = (b + k // 2) % 2, k % 2
                pe.wait_ge(masked, 4 * G + q + 1)
                if q == 0:
                    if due(G - 1):
                        pe.wait_ge(normed, G - 1)
                    pe.wait_ge(v_ready1, 2 * i + b + k // 2 + 1)
                    if more:
                        pe.wait_ge(vmore_ready, 4 * (2 * i + b + k // 2 + 1))
                grp, c = q // 2, q % 2
                terms = 2 + (R - 1 if more else 0)
                for term in range(terms):
                    for g in range(GRP):
                        h = GRP * grp + g
                        u = 4 * grp + 2 * c + g // 2
                        cut = slice(N * (g % 2), N * (g % 2) + N)
                        if term == 0:
                            w, m, rhs = v_base[par][:, gi, c, h, :], 32, probs[:, u, cut]
                        elif term == 1:
                            w, m, rhs = v_one[par][:, gi, c, h, :], DH, probs_one[:, u, cut]
                        else:
                            w, m, rhs = (v_more[par][:, gi, c, term - 2, h, :], DH,
                                         probs_more[:, term - 2, u % 2, cut])
                        last = nc.tensor.matmul(PV_BANK[k % 2][32 * g:32 * g + m, N * grp:N * grp + N], w, rhs,
                                                start=(c == 0 and term == 0),
                                                stop=(c == NC - 1 and term == terms - 1))
                last.then_inc(pv_mm, 1)

            def turn_max(i, b, k):
                G = 4 * i + 2 * b + k
                if not within(i, G, B):
                    return
                pe.wait_ge(max_split, G + 1)
                for c in range(NC):
                    last = nc.tensor.transpose(M1[:, :].bitcast(BF16)[0:PARTS * H, 128 * c:128 * c + 128],
                                               max_parts[:, c, :, :].rearrange("p s h -> p (s h)"), identb[:])
                last.then_inc(maxt_mm, 1)

            def make_values(Q, par, gi, bk):
                for c in range(NC):
                    last = nc.tensor.matmul(bk[:, 2 * D * c:2 * D * c + 2 * D],
                                            x_t[par][:, N * gi + 128 * c:N * gi + 128 * c + 128],
                                            wv[:, 0:2, :].rearrange("p r d -> p (r d)"), start=True, stop=True)
                last.then_inc(v_mm, 1)

            def make_more(Q, par):
                for n in range(4):
                    bk = (M1, M0)[n % 2]
                    if n < 2:
                        pe.wait_ge((v_ready0, v_ready1)[n], Q + 1)
                    else:
                        pe.wait_ge(vmore_ready, 4 * Q + n - 1)
                    nc.tensor.matmul(bk[:, 0:(R - 1) * D], x_t[par][:, 128 * n:128 * n + 128],
                                     wv[:, 2:R + 1, :].rearrange("p r d -> p (r d)"), start=True,
                                     stop=True).then_inc(vmore_mm, 1)

            def step(i, b):
                p = 2 * i + b
                for slot in range(2):
                    G = 2 * p + slot
                    for u in range(UNITS):
                        scores(i, b, slot + 2, u)
                        scores_t(i, b, slot, u)
                        if u == 0:
                            values(i, b, slot - 1, 2)
                        if u == 2:
                            values(i, b, slot - 1, 3)
                        if u == 4:
                            values(i, b, slot, 0)
                        if u == 6:
                            values(i, b, slot, 1)
                        P, Q = p + 2, p + 1
                        if slot == 0:
                            if u == 0 and within(i, P, PAIRS):
                                half = i + (b + 2) // 2
                                pe.wait_ge(x_in[b], 16 * (half + 1))
                                if due(P - 1):
                                    pe.wait_ge(v_ready1, P - 1)
                                if isinstance(i, int):
                                    if due(2 * (P - 1)):
                                        pe.wait_ge(qk_whole, 2 * (P - 1))
                                if more:
                                    if due(4 * (P - 1)):
                                        pe.wait_ge(vmore_ready, 4 * (P - 1))
                                for n in range(2 * NC):
                                    last = nc.tensor.transpose(M0[:, 128 * n:128 * n + 128], x_nat[b][:, n, :],
                                                               ident[:])
                                last.then_inc(xt_mm, 1)
                            if u == 1:
                                if within(i, G + 1, B):
                                    pe.wait_ge(v_ready0, p + 1)
                                    if more:
                                        pe.wait_ge(vmore_ready, 4 * (p + 1))
                                turn_max(i, b, 1)
                            if u == 2 and within(i, P, PAIRS):
                                pe.wait_ge(x_kept, P + 1)
                                nc.tensor.matmul(M0[:, :], wq[:], x_t[b][:], start=True, stop=True).then_inc(qk_mm, 1)
                            if u == 3 and within(i, P, PAIRS):
                                if within(i, G + 1, B):
                                    pe.wait_ge(maxt_ready, G + 2)
                                nc.tensor.matmul(M1[:, :], wk[:], x_t[b][:], start=True, stop=True).then_inc(qk_mm, 1)
                            if u == 5 and within(i, p - 1, PAIRS):
                                if within(i, P, PAIRS):
                                    pe.wait_ge(qk_whole, 2 * P + 1)
                                else:
                                    pe.wait_ge(v_ready1, at_most(p + 1, PAIRS))
                                    if due(p - 1):
                                        pe.wait_ge(var_ln, p - 1)
                                pe.wait_ge(x_kept, p)
                                nc.tensor.matmul(M0[:, :], centre[:], nodes_of(p - 1), start=True, stop=False)
                            if u == 7 and within(i, p - 1, PAIRS):
                                pe.wait_ge(normed, 2 * p)
                                for n in range(2):
                                    last = nc.tensor.matmul(M0[:, :], wo[:, n, :], mixed[:, n, :], start=False,
                                                            stop=(n == 1))
                                last.then_inc(y_mm, 1)
                        else:
                            if u == 2:
                                if within(i, G + 1, B):
                                    if within(i, P, PAIRS):
                                        pe.wait_ge(qk_whole, 2 * P + 2)
                                    elif within(i, G, B):
                                        pe.wait_ge(maxt_ready, G + 1)
                                turn_max(i, b, 2)
                            if u == 2 and within(i, p - 1, PAIRS):
                                pe.wait_ge(y_read, p)
                                nc.tensor.matmul(M0[:, :], mean_w[:], ln_sq[:], start=True, stop=True).then_inc(var_mm, 1)
                            if u == 4 and within(i, Q, PAIRS):
                                pe.wait_ge(xt_ready, Q + 1)
                                pe.wait_ge(maxt_ready, G + 2)
                                make_values(Q, (b + 1) % 2, 0, M1)
                            if u == 6 and within(i, Q, PAIRS):
                                if due(p):
                                    pe.wait_ge(var_ln, p)
                                if within(i, P, PAIRS):
                                    pe.wait_ge(qk_whole, 2 * P + 1)
                                make_values(Q, (b + 1) % 2, 1, M0)
                            if u == 7 and more and within(i, Q, PAIRS):
                                make_more(Q, (b + 1) % 2)

            return step, make_more

        def attend_dve(dve, more):
            def reduce_max(i, b, k, u):
                G = 4 * i + 2 * b + k
                if not within(i, G, B):
                    return
                dve.wait_ge(s_mm, UNITS * G + u + 1)
                if u == 0:
                    if due(G - 1):
                        dve.wait_ge(max_split, G - 1)
                c, hp = u // 4, u % 4
                nc.vector.tensor_reduce(row_max[k % 2][:, c, 2 * hp:2 * hp + 2],
                                        S_BANK[u % 2][:, :].rearrange("p (h j) -> p h j", h=2), AX,
                                        ALU.max).then_inc(s_max, 1)

            def mask(i, b, k, q):
                G = 4 * i + 2 * b + k
                if not within(i, G, B):
                    return
                dve.wait_ge(exp_done, UNITS * G + 2 * q + 2)
                if due(4 * (G - 1) + q + 1):
                    dve.wait_ge(pv_mm, 4 * (G - 1) + q + 1)
                code = codes[:, bass.ds(G, 1), q % 2, :]
                both = slice(2 * q, 2 * q + 2)
                one = nc.vector.scalar_tensor_tensor(out=probs_one[:, both, :].rearrange("p u (h i) -> p (u h) i", h=2),
                                                     in0=code.broadcast_to([128, GRP, N]), scalar=1.0,
                                                     in1=probs[:, both, :].rearrange("p u (h i) -> p (u h) i", h=2),
                                                     op0=ALU.is_equal, op1=ALU.mult)
                if not more:
                    one.then_inc(masked, 1)
                    return
                if due(4 * G + q):
                    dve.wait_ge(pv_mm, 4 * G + q)
                code = code.broadcast_to([128, 2, N])
                for n in range(2):
                    src = probs[:, 2 * q + n, :].rearrange("p (h i) -> p h i", h=2)
                    for r in range(2, R):
                        dst = probs_more[:, r - 2, n, :].rearrange("p (h i) -> p h i", h=2)
                        nc.vector.scalar_tensor_tensor(out=dst, in0=code, scalar=float(r), in1=src,
                                                       op0=ALU.is_equal, op1=ALU.mult)
                    last = probs_more[:, R - 2, n, :]
                    dst = last.rearrange("p (h i) -> p h i", h=2)
                    nc.vector.scalar_tensor_tensor(out=dst, in0=code, scalar=0.0, in1=src, op0=ALU.is_lt,
                                                   op1=ALU.mult).then_inc(more_done, 1)
                    dve.wait_ge(more_done, 3 * (UNITS * G + 2 * q + n) + 1)
                    tmp = more_tmp[:, :].rearrange("p (h i) -> p h i", h=2)
                    nc.vector.scalar_tensor_tensor(out=tmp, in0=code, scalar=float(R), in1=src, op0=ALU.is_ge,
                                                   op1=ALU.mult).then_inc(more_done, 1)
                    dve.wait_ge(more_done, 3 * (UNITS * G + 2 * q + n) + 2)
                    nc.vector.tensor_tensor(last, last, more_tmp[:, :], ALU.add).then_inc(more_done, 1)
                    dve.wait_ge(more_done, 3 * (UNITS * G + 2 * q + n) + 3)
                dve.sem_inc(masked, 1)

            def spread_denominators(G, k):
                dve.wait_ge(pv_mm, 4 * (G + 1))
                if due(G):
                    dve.wait_ge(den_inv, G)
                    dve.sem_inc(passed, 1)
                nc.vector.stream_shuffle(denom[:], PV_BANK[k % 2][:, :], [DH] * 32).then_inc(den_ready, 1)

            def normalize(i, b, k):
                G = 4 * i + 2 * b + k
                gi = k % 2
                dve.wait_ge(den_inv, G + 1)
                if due(2 * i + b + k // 2):
                    dve.wait_ge(y_mm, 2 * i + b + k // 2)
                nc.vector.tensor_tensor(mixed[:, :, N * gi:N * gi + N],
                                        PV_BANK[k % 2][:, :].rearrange("p (n i) -> p n i", n=2),
                                        denom_r[:].rearrange("p (n i) -> p n i", n=2), ALU.mult).then_inc(normed, 1)

            def keep_values(Q, par, gi, bk, done):
                dve.wait_ge(v_mm, 2 * Q + gi + 1)
                if due(4 * (2 * Q - 2)):
                    dve.wait_ge(pv_mm, 4 * (2 * Q - 2))
                src = bk[:, :].rearrange("p (c r h d) -> p c r h d", c=NC, r=2, h=H)
                for r in range(2):
                    dst = v_base[par][:, gi, :, :, 0:DH] if r == 0 else v_one[par][:, gi, :, :, :]
                    bias = bvb[:, r:r + 1, :].rearrange("p o (h d) -> p o h d", h=H).broadcast_to([128, NC, H, DH])
                    last = nc.vector.tensor_tensor(dst, src[:, :, r], bias, ALU.add)
                last.then_inc(done, 1)

            def keep_more(Q, par):
                for n in range(4):
                    dve.wait_ge(vmore_mm, 4 * Q + n + 1)
                    nc.vector.tensor_tensor(v_more[par][:, n // 2, n % 2].rearrange("p r h d -> p (r h d)"),
                                            (M1, M0)[n % 2][:, 0:(R - 1) * D],
                                            bvb[:, 2:R + 1, :].rearrange("p r d -> p (r d)"),
                                            ALU.add).then_inc(vmore_ready, 1)

            def step(i, b):
                p = 2 * i + b
                for slot in range(2):
                    G = 2 * p + slot
                    for u in range(UNITS):
                        reduce_max(i, b, slot + 2, u)
                        if u == 7 and slot == 1 and within(i, p + 1, PAIRS):
                            keep_values(p + 1, (b + 1) % 2, 1, M0, v_ready1)
                            if more:
                                keep_more(p + 1, (b + 1) % 2)
                        if u == 0:
                            mask(i, b, slot - 1, 3)
                        elif u % 2 == 0:
                            mask(i, b, slot, u // 2 - 1)
                        if u == 3 and within(i, G - 1, B):
                            spread_denominators(G - 1, slot - 1)
                        if u == 5 and within(i, G - 1, B):
                            normalize(i, b, slot - 1)
                        Q = p + 1
                        if slot == 1:
                            if u == 4 and within(i, p - 1, PAIRS):
                                dve.wait_ge(rstd, p)
                                nc.vector.tensor_tensor(ln_y[:], ln_y[:], ln_r[:], ALU.mult).then_inc(ln_mid, 1)
                            if u == 5 and within(i, Q, PAIRS):
                                keep_values(Q, (b + 1) % 2, 0, M1, v_ready0)

            return step, keep_more

        adj_in = [probs[:, 2 * n:2 * n + 2, :].bitcast(I32).rearrange("p g (c i) -> p g c i", c=NC) for n in range(ADJ_BUFS)]
        wqk_raw = probs_one[:, 4, 0:2 * D].rearrange("p (n d) -> p n d", n=2)
        rows = probs_one[0:NROWS, 5, 0:D]
        qk_rows = probs_one[0:2, 6, 0:D]
        crows = probs_one[0:len(CENTRED), 7, 0:D]
        crow_mean = probs_one[0:len(CENTRED), 7, D:D + 1]
        adj_c = [probs_one[:, n, :].bitcast(BF16).rearrange("p (g c i) -> p g c i", g=2, c=NC) for n in range(2)]
        odd_junk = probs_one[:, 2, :].bitcast(BF16)
        odd = probs_one[:, 3, 0:PAIRS]
        wmean = probs_one[:, 3, PAIRS:PAIRS + 2]
        mhalf, odd_max, odd_all = (probs_one[:, 3, 32 + n:33 + n] for n in range(3))

        rows_in, bo_in, wts_in, wo_in = sem("rows_in"), sem("bo_in"), sem("wts_in"), sem("wo_in")
        gat_in, bv_in = sem("gat_in"), sem("bv_in")
        adj_sem = [sem(f"adj_sem{n}") for n in range(ADJ_BUFS)]
        const_ready, wo_zero, prep, prep_pe = sem("const_ready"), sem("wo_zero"), sem("prep"), sem("prep_pe")
        clamped, turned, coded, counted = sem("clamped"), sem("turned"), sem("coded"), sem("counted")
        odd_sem = sem("odd_sem")
        vchain = sem("vchain")
        wqk_in, wqk_ready, cols_ready = sem("wqk_in"), sem("wqk_ready"), sem("cols_ready")
        qk_rows_in, qk_rows_turned = sem("qk_rows_in"), sem("qk_rows_turned")

        with nc.Block() as block:
            @block.sync
            def _(sp):
                x_load, step = attend_sync(sp)
                x_load(0, 0)
                sp.dma_start(wqk_raw[:, 0, :], a["L0_gnn_Wq"]).then_inc(wqk_in, 16)
                sp.dma_start(wqk_raw[:, 1, :], a["L0_gnn_Wk"]).then_inc(wqk_in, 16)
                for n, name in enumerate(("L0_gnn_bq", "L0_gnn_bk")):
                    sp.dma_start(qk_rows[n:n + 1, :].rearrange("o (d h) -> o d h", h=H),
                                 a[name].rearrange("(o h d) -> o d h", o=1, h=H),
                                 allow_slow_non_contiguous=True).then_inc(qk_rows_in, 16)
                for n, name in enumerate(VECS):
                    sp.dma_start(rows[n:n + 1, :], a[name].rearrange("(o d) -> o d", o=1)).then_inc(rows_in, 16)
                for start, name in ((COL_B1, "L0_gnn_b1"), (COL_BFF1, "L1_gnn_b_ff1")):
                    sp.dma_start(rows[start:start + FC, :], a[name].rearrange("(c d) -> c d", c=FC)).then_inc(rows_in, 16)
                for n, name in enumerate(("L1_gnn_a1", "L1_gnn_a2")):
                    sp.dma_start(rows[COL_A + 2 * n:COL_A + 2 * n + 2, :],
                                 a[name].rearrange("(c d) o -> c (d o)", c=2)).then_inc(rows_in, 16)
                for n, name in enumerate(CENTRED):
                    sp.dma_start(crows[n:n + 1, :], a[name].rearrange("(o d) -> o d", o=1)).then_inc(bo_in, 16)
                sp.dma_start(wv[:, 0:R, :], a["L0_gnn_Wv"].rearrange("r d e -> d r e")).then_inc(wts_in, 16)
                sp.dma_start(bvb[:, 0:R, :], a["L0_gnn_bv"].partition_broadcast(128)).then_inc(bv_in, 16)
                for n, name in enumerate(("L1_gnn_W1", "L1_gnn_W2")):
                    sp.dma_start(gw[:, n, 0:D], a[name]).then_inc(gat_in, 16)
                sp.wait_ge(wo_zero, 1)
                for h in range(H):
                    sp.dma_start(wo[32 * (h % GRP):32 * (h % GRP) + DH, h // GRP, :],
                                 a["L0_gnn_Wo"][DH * h:DH * h + DH, :]).then_inc(wo_in, 16)
                sp.dma_start(w1[:], a["L0_gnn_W1"]).then_inc(wts_in, 16)
                sp.dma_start(w2[:], a["L0_gnn_W2"].rearrange("(c k) d -> k c d", c=FC)).then_inc(wts_in, 16)
                sp.dma_start(wf1[:], a["L1_gnn_w_ff1"]).then_inc(wts_in, 16)
                sp.dma_start(wf2[:], a["L1_gnn_w_ff2"].rearrange("(c k) d -> k c d", c=FC)).then_inc(wts_in, 16)
                step(-1, 0)
                step(-1, 1)

            @block.gpsimd
            def _(pool):
                nc.gpsimd.memset(ident[:], 0.0).then_inc(const_ready, 1)
                pool.wait_ge(const_ready, 1)
                nc.gpsimd.affine_select(out=ident[:], in_=ident[:], compare_op=ALU.not_equal, fill=1.0, base=0,
                                        pattern=[[-1, 128]], channel_multiplier=1).then_inc(const_ready, 1)
                pool.wait_ge(const_ready, 2)
                nc.gpsimd.tensor_copy(identb[:], ident[:]).then_inc(const_ready, 1)
                nc.gpsimd.memset(mhalf, -0.5).then_inc(const_ready, 1)
                nc.gpsimd.tensor_scalar(centre[:], ident[:], 1.0 / D, None, ALU.subtract).then_inc(const_ready, 1)
                nc.gpsimd.memset(mean_w[:], 1.0 / D).then_inc(const_ready, 1)
                nc.gpsimd.memset(eps[:], EPS).then_inc(const_ready, 1)
                pool.wait_ge(const_ready, 7)
                for n in range(4):
                    nc.gpsimd.memset(k_st[n][ROWS:ROWSM, :, :], 1.0).then_inc(ones_init, 1)
                    pool.wait_ge(ones_init, n + 1)
                step = attend_pool(pool)
                step(-1, 0)
                pool.wait_ge(odd_sem, 1)
                nc.gpsimd.partition_all_reduce(odd_all, odd_max, 128, RMAX).then_inc(odd_sem, 1)
                step(-1, 1)

            @block.scalar
            def _(act):
                act.preload_act_table_set("natural_log_exp_and_others")
                step = attend_act(act)

                def load_adj(P, n):
                    act.dma_start(adj_in[n], a["adj"][bass.ds(2 * P, 2)].rearrange(
                        "g (c p) j -> p g c j", c=NC)).then_inc(adj_sem[n], 16)

                def load_and_count(i, n):
                    P = ADJ_BUFS * i + n
                    if within(i, P, PAIRS):
                        act.wait_ge(clamped, P - ADJ_BUFS + 1)
                        load_adj(P, n)
                    Q = P - ADJ_BUFS
                    act.wait_ge(coded, Q + 1)
                    if due(Q):
                        act.wait_ge(counted, Q)
                    nc.scalar.activation(odd_junk, codes[:, bass.ds(2 * Q, 2)].rearrange("p g c i -> p (g c i)"),
                                         ACT.Square, bias=mhalf,
                                         accum_out=odd[:, bass.ds(Q, 1)]).then_inc(counted, 1)

                for n in range(ADJ_BUFS):
                    load_adj(n, n)
                act.wait_ge(const_ready, 7)
                act.wait_ge(cols_ready, 1)
                step(-1, 0)
                for n in range(ADJ_BUFS):
                    load_and_count(1, n)
                with act.Fori(2, PAIRS // ADJ_BUFS) as i:
                    for n in range(ADJ_BUFS):
                        load_and_count(i, n)
                for n in range(ADJ_BUFS):
                    load_and_count(PAIRS // ADJ_BUFS, n)
                step(-1, 1)

            @block.tensor
            def _(pe):
                step, _more = attend_pe(pe, False)

                def turn_codes(i, n):
                    P = ADJ_BUFS * i + n
                    pe.wait_ge(clamped, P + 1)
                    if due(P - 1):
                        pe.wait_ge(coded, P - 1)
                    turned_bank = bank[n % 2][:, :].bitcast(BF16).rearrange("p (g c i) -> p g c i", g=2, c=NC)
                    for g in range(2):
                        for c in range(NC):
                            for k in range(NC):
                                last = nc.tensor.transpose(turned_bank[:, g, c, 128 * k:128 * k + 128],
                                                           adj_c[n % 2][:, g, k, 128 * c:128 * c + 128], identb[:])
                    last.then_inc(turned, 1)

                pe.wait_ge(const_ready, 4)
                pe.wait_ge(qk_rows_in, 32)
                nc.tensor.transpose(bank[2][:, 0:2], qk_rows, ident[0:2, 0:2]).then_inc(qk_rows_turned, 1)
                pe.wait_ge(wqk_ready, 1)
                step(-1, 0)
                adj_loop(pe, turn_codes, 0, PAIRS)
                pe.wait_ge(rows_in, 16 * (len(VECS) + 4))
                nc.tensor.transpose(bank[4][:, 0:NROWS], rows, ident[0:NROWS, 0:NROWS]).then_inc(prep_pe, 1)
                pe.wait_ge(prep, 1)
                nc.tensor.transpose(bank[3][:, 0:len(CENTRED)], crows,
                                    ident[0:len(CENTRED), 0:len(CENTRED)]).then_inc(prep_pe, 1)
                pe.wait_ge(coded, PAIRS)
                pe.wait_ge(prep, 2)
                step(-1, 1)

            @block.vector
            def _(dve):
                links = [0]

                def link(ins):
                    links[0] += 1
                    ins.then_inc(vchain, 1)
                    dve.wait_ge(vchain, links[0])

                nc.vector.memset(wo[:], 0.0).then_inc(wo_zero, 1)
                for n in range(2):
                    nc.vector.memset(v_base[n][:, :, :, :, DH:32], 1.0)
                dve.wait_ge(wqk_in, 32)
                for n, w in enumerate((wq, wk)):
                    last = nc.vector.tensor_copy(w[:].rearrange("p (d h) -> p d h", h=H),
                                                 wqk_raw[:, n, :].rearrange("p (h d) -> p d h", h=H))
                last.then_inc(wqk_ready, 1)
                dve.wait_ge(qk_rows_turned, 1)
                nc.vector.tensor_scalar(qk_cols[:, 0:1], bank[2][:, 0:1], DH ** -0.5, None, ALU.mult)
                nc.vector.tensor_copy(qk_cols[:, 1:2], bank[2][:, 1:2]).then_inc(cols_ready, 1)

                def code(i, n):
                    P = ADJ_BUFS * i + n
                    if within(i, P, PAIRS):
                        dve.wait_ge(adj_sem[n], 16 * i + 16)
                        if due(P - 1):
                            dve.wait_ge(turned, P - 1)
                        nc.vector.tensor_scalar(adj_c[n % 2], adj_in[n], -1.0, float(R), ALU.max,
                                                ALU.min).then_inc(clamped, 1)
                    if within(i, P - 1, PAIRS):
                        if due(P):
                            dve.wait_ge(turned, P)
                        nc.vector.tensor_copy(
                            codes[:, bass.ds(2 * (P - 1), 2)],
                            bank[1 - n % 2][:, :].bitcast(BF16).rearrange("p (g c i) -> p g c i", g=2,
                                                                      c=NC)).then_inc(coded, 1)
                adj_loop(dve, code, 0, PAIRS + 1)
                dve.wait_ge(bo_in, 16 * len(CENTRED))
                link(nc.vector.tensor_reduce(crow_mean, crows, AX, ALU.add))
                link(nc.vector.tensor_scalar(crow_mean, crow_mean, 1.0 / D, None, ALU.mult))
                nc.vector.tensor_scalar(crows, crows, crow_mean[:, 0:1], None, ALU.subtract).then_inc(prep, 1)
                dve.wait_ge(prep_pe, 2)
                nc.vector.tensor_copy(cols[:], bank[4][:, 0:NROWS])
                nc.vector.tensor_copy(ccols[:], bank[3][:, 0:len(CENTRED)])
                dve.wait_ge(wts_in, 16 * 5)
                dve.wait_ge(wo_in, 16 * H)
                dve.wait_ge(bv_in, 16)
                for w in (wv, bvb):
                    nc.vector.tensor_scalar(w[:, R, :], w[:, 0, :], -1.0, None, ALU.mult)
                    for r in range(1, R):
                        last = nc.vector.tensor_tensor(w[:, r, :], w[:, r, :], w[:, 0, :], ALU.subtract)
                last.then_inc(prep, 1)
                dve.wait_ge(counted, PAIRS)
                nc.vector.tensor_reduce(odd_max, odd, AX, ALU.max).then_inc(odd_sem, 1)
                link(nc.vector.tensor_reduce(wmean, wo[:], AX, ALU.add))
                link(nc.vector.tensor_scalar(wmean, wmean, 1.0 / D, None, ALU.mult))
                for c in range(2):
                    nc.vector.tensor_scalar(wo[:, c, :], wo[:, c, :], wmean[:, c:c + 1], None, ALU.subtract)
                attend_dve(dve, False)[0](-1, 1)
                dve.wait_ge(odd_sem, 2)
                nc.vector.tensor_scalar(flag[:], odd_all, 2 * NC * N / 4.0, None, ALU.is_gt)

        with nc.Block() as block:
            @block.sync
            def _(sp):
                pair_loop(sp, attend_sync(sp)[1], 0, 1, PAIRS // 2 - 2, PAIRS + 1)

            @block.gpsimd
            def _(pool):
                attend_loop(pool, attend_pool(pool))

            @block.scalar
            def _(act):
                attend_loop(act, attend_act(act))

            @block.tensor
            def _(pe):
                def program(more):
                    step, make_more = attend_pe(pe, more)
                    if more:
                        make_more(0, 0)
                    attend_loop(pe, step)

                odd_one = pe.value_load(flag[0:1, 0:1])
                with pe.If(odd_one > 0):
                    program(True)
                with pe.Else():
                    program(False)
                pe.wait_ge(ln_done, PAIRS)

            @block.vector
            def _(dve):
                def program(more):
                    step, keep_more = attend_dve(dve, more)
                    if more:
                        keep_more(0, 0)
                    attend_loop(dve, step)

                odd_one = dve.value_load(flag[0:1, 0:1])
                with dve.If(odd_one > 0):
                    program(True)
                with dve.Else():
                    program(False)
                dve.wait_ge(ln_done, PAIRS)
        attend_ctx.close()

        hidden_bias = sb("hidden_bias", [128, B, NC, N], BF16)
        ff_ctx = ExitStack()
        hid = [sb(f"hid{n}", [128, FC, W2G], F32, ff_ctx) for n in range(2)]
        gt, abc = sb("gt", [128, 2, D], F32, ff_ctx), sb("abc", [128, 2, D], F32, ff_ctx)
        wmean2 = sb("wmean2", [128, 2 * FC + 1], F32, ff_ctx)

        def ff_pe_hidden(pe, i, b, s, w):
            p = 2 * i + b
            if within(i, p, PAIRS):
                for c in range(FC):
                    if due(FC * (p - 1) + c + 1):
                        pe.wait_ge(s["hid_act"], FC * (p - 1) + c + 1)
                    nc.tensor.matmul(bank[c][:, :], w[:, 128 * c:128 * c + 128], nodes_of(p), start=True,
                                     stop=True).then_inc(s["hid_mm"], 1)

        def ff_pe_out(pe, i, b, s, w):
            p = 2 * i + b
            if within(i, p - 1, PAIRS):
                if due(p - 2):
                    pe.wait_ge(s["y_read"], p - 2)
                for c in range(FC):
                    pe.wait_ge(s["hid_act"], FC * (p - 1) + c + 1)
                    nc.tensor.matmul(bank[4 + (b + 1) % 2][:, :], w[:, c, :], hid[(b + 1) % 2][:, c, :],
                                     start=(c == 0), stop=False)
                nc.tensor.matmul(bank[4 + (b + 1) % 2][:, :], centre[:], nodes_of(p - 1), start=False,
                                 stop=True).then_inc(s["y_mm"], 1)

        def ff_act_hidden(act, i, b, s, func, col):
            p = 2 * i + b
            if within(i, p, PAIRS):
                for c in range(FC):
                    act.wait_ge(s["hid_mm"], FC * p + c + 1)
                    if c == 0:
                        if due(p - 1):
                            act.wait_ge(s["y_mm"], p - 1)
                    nc.scalar.activation(hid[b][:, c, :], bank[c][:, :], func,
                                         bias=cols[:, col + c:col + c + 1]).then_inc(s["hid_act"], 1)

        s1 = {name: sem(f"f1_{name}") for name in ("hid_mm", "hid_act", "y_mm", "y_read")}
        hb_done = sem("hb_done")
        hop_turned, hop_there, hop_mm, fchain, w2_ready = (sem("hop_turned"), sem("hop_there"), sem("hop_mm"),
                                                          sem("fchain"), sem("w2_ready"))
        HT, HP = bank[6], bank[7]
        with nc.Block() as block:
            @block.tensor
            def _(pe):
                def step(i, b):
                    ff_pe_hidden(pe, i, b, s1, w1)
                    ff_pe_out(pe, i, b, s1, w2)
                for n in range(2):
                    last = nc.tensor.transpose(HT[:, 128 * n:128 * n + 128], gw[:, n, 0:D], ident[:])
                last.then_inc(hop_turned, 1)
                step(0, 0)
                pe.wait_ge(hop_there, 1)
                for n in range(2):
                    nc.tensor.matmul(HP[:, (D + 1) * n:(D + 1) * n + D], gt[:, n, :], abc[:, n, :], start=True,
                                     stop=True)
                    last = nc.tensor.matmul(HP[:, (D + 1) * n + D:(D + 1) * n + D + 1], gt[:, n, :],
                                            cols[:, COL_A + 2 * n + 1:COL_A + 2 * n + 2], start=True, stop=True)
                last.then_inc(hop_mm, 1)
                pe.wait_ge(w2_ready, 1)
                step(0, 1)
                pair_loop(pe, step, 2, 1, PAIRS // 2, PAIRS + 1)

            @block.scalar
            def _(act):
                pair_loop(act, lambda i, b: ff_act_hidden(act, i, b, s1, ACT.Gelu, COL_B1), 0, 1, PAIRS // 2,
                          PAIRS)

            @block.vector
            def _(dve):
                def step(i, b):
                    p = 2 * i + b
                    if within(i, p, PAIRS):
                        nc.vector.tensor_scalar(hidden_bias[:, bass.ds(2 * p, 2)].rearrange("p g c i -> p (g c i)"),
                                                codes[:, bass.ds(2 * p, 2)].rearrange("p g c i -> p (g c i)"), 0.0,
                                                HIDDEN, ALU.is_le, ALU.mult).then_inc(hb_done, 1)
                    if within(i, p - 1, PAIRS):
                        dve.wait_ge(s1["y_mm"], p)
                        nc.vector.tensor_scalar(nodes_of(p - 1), bank[4 + (b + 1) % 2][:, :], ccols[:, 1:2], None,
                                                ALU.add).then_inc(s1["y_read"], 1)

                links = [0]

                def link(ins):
                    links[0] += 1
                    ins.then_inc(fchain, 1)
                    dve.wait_ge(fchain, links[0])

                def centre_weights(at, w, k):
                    link(nc.vector.tensor_reduce(wmean2[:, at:at + k], w, AX, ALU.add))
                    link(nc.vector.tensor_scalar(wmean2[:, at:at + k], wmean2[:, at:at + k], 1.0 / D, None, ALU.mult))
                    for c in range(k):
                        last = nc.vector.tensor_scalar(w[:, c, :], w[:, c, :], wmean2[:, at + c:at + c + 1], None,
                                                       ALU.subtract)
                    return last

                centre_weights(0, w2[:], FC).then_inc(w2_ready, 1)
                for n in range(2):
                    nc.vector.tensor_copy(abc[:, n, :], cols[:, COL_A + 2 * n:COL_A + 2 * n + 1].to_broadcast([128, D]))
                dve.wait_ge(hop_turned, 1)
                nc.vector.tensor_copy(gt[:], HT[:, 0:2 * D].rearrange("p (n d) -> p n d", n=2)).then_inc(hop_there, 1)
                centre_weights(FC, wf2[:], FC)
                centre_weights(2 * FC, gw[:, 1:2, 0:D], 1)
                dve.wait_ge(hop_mm, 1)
                for n in range(2):
                    nc.vector.tensor_copy(ga[:, n, :], HP[:, (D + 1) * n:(D + 1) * n + D])
                    nc.vector.tensor_copy(gw[:, n, D:D + 1], HP[:, (D + 1) * n + D:(D + 1) * n + D + 1])
                pair_loop(dve, step, 0, 1, PAIRS // 2, PAIRS + 1)
        ff_ctx.close()

        gat_ctx = ExitStack()
        G_ = lambda name, shape, dt=F32: sb(name, shape, dt, gat_ctx)
        sq_a, sq_b = G_("sq_a", [128, W2G]), G_("sq_b", [128, W2G])
        r_a, r_b = G_("r_a", [128, W2G]), G_("r_b", [128, W2G])
        mid_a, mid_b = G_("mid_a", [128, W2G]), G_("mid_b", [128, W2G])
        y_b = [G_(f"y_b{n}", [128, W2G]) for n in range(2)]
        hop_in = [[G_(f"hop_in{h}{n}", [128, W2G]) for n in range(2)] for h in range(2)]
        logits = [G_(f"logits{h}", [128, 2 * NC, N]) for h in range(2)]
        att = [G_(f"att{h}", [128, 2 * NC, N]) for h in range(2)]
        wh_raw = [[G_(f"wh_raw{h}{n}", [128, 2, NC, D + 1]) for n in range(2)] for h in range(2)]
        wh = [G_(f"wh{h}", [128, 2 * NC, D]) for h in range(2)]
        top = [G_(f"top{h}", [128, 2 * NC]) for h in range(2)]
        shift = [G_(f"shift{h}", [128, 2, 2 * NC]) for h in range(2)]
        hidden_now = [G_(f"hidden_now{h}", [128, 2 * NC, N], BF16) for h in range(2)]
        total = [G_(f"total{h}", [128, 2 * NC]) for h in range(2)]
        inv = [G_(f"inv{h}", [128, 2 * NC]) for h in range(2)]
        per_hop = lambda name: [sem(f"g_{name}{h}") for h in range(2)]
        bc_mm, wh_mm, wh_kept, summed, shifted, exped, whs, out_mm = (per_hop(n) for n in (
            "bc_mm", "wh_mm", "wh_kept", "summed", "shifted", "exped", "whs", "out_mm"))
        hop_ready, hidden_here, chain, chain2 = (per_hop(n) for n in ("hop_ready", "hidden_here", "chain", "chain2"))
        x2_kept, y3_read, sq_ready = sem("x2_kept"), sem("y3_read"), sem("g_sq_ready")
        gvar_mm, gvar_ln, grstd, gmid = (per_hop(n) for n in ("gvar_mm", "gvar_ln", "grstd", "gmid"))
        gln = sem("g_gln")
        BC, WH, OUTB, VARB, HIDB, YB = bank[0:2], bank[2:4], bank[4], bank[5], bank[6], bank[7]
        TURNB = BC[0]
        hid = [G_(f"hid_r{n}", [128, FC, W2G]) for n in range(2)]
        fy = [G_(f"fy{n}", [128, W2G]) for n in range(2)]
        fsq, fr, fmid, fo = (G_(n, [128, W2G]) for n in ("fsq", "fr", "fmid", "fo"))
        o_nat = G_("o_nat", [128, 2 * NC, D])
        s2 = {name: sem(f"f2_{name}") for name in ("hid_mm", "hid_act", "y_mm", "y_read", "var_mm", "var_ln", "rstd",
                                                  "mid", "normed", "o_mm", "o_ready")}
        o_out = sem("o_out")
        LAG_NORM0, LAG_FRONT, LAG_SCORE, LAG_WEIGH, LAG_BACK, LAG_Y, LAG_NORM1 = 1, (1, 3), (2, 3), (2, 4), (2, 4), 4, 5
        LAG_KEEP, LAG_HID, LAG_SUM, LAG_NORM2, LAG_OUT = (2, 3), 6, 7, 8, 9
        gat_loop = lambda eng, step: pair_loop(eng, step, 0, 5, PAIRS // 2, PAIRS + LAG_OUT)

        with nc.Block() as block:
            @block.tensor
            def _(pe):
                def front(i, b, hop):
                    p, par = 2 * i + b, (b + 1) % 2
                    P = p - LAG_FRONT[hop]
                    if not within(i, P, PAIRS):
                        return
                    if hop == 0 and due(p - LAG_OUT + 1):
                        pe.wait_ge(s2["o_ready"], p - LAG_OUT + 1)
                    pe.wait_ge(hop_ready[hop], P + 1)
                    if due(P):
                        pe.wait_ge(summed[hop], P)
                    nc.tensor.matmul(BC[hop][:, :], ga[:, hop, :], hop_in[hop][par][:], start=True,
                                     stop=True).then_inc(bc_mm[hop], 1)
                    other = at_most(p - (1, 2)[1 - hop], PAIRS)
                    if due(other):
                        pe.wait_ge(wh_kept[1 - hop], other)
                    if due(P) and not within(i, p - (3, 2)[hop], PAIRS):
                        pe.wait_ge(wh_kept[hop], P)
                    for g in range(2):
                        for c in range(NC):
                            last = nc.tensor.matmul(WH[g][:, (D + 1) * c:(D + 1) * c + D + 1],
                                                    hop_in[hop][par][:, N * g + 128 * c:N * g + 128 * c + 128],
                                                    gw[:, hop, :], start=True, stop=True)
                    last.then_inc(wh_mm[hop], 1)

                def back(i, b, hop):
                    p = 2 * i + b
                    P = p - LAG_BACK[hop]
                    if not within(i, P, PAIRS):
                        return
                    if hop == 0:
                        if due(p - 3):
                            pe.wait_ge(y3_read, p - 3)
                    else:
                        pe.wait_ge(hop_ready[1], at_most(p - 2, PAIRS))
                        pe.wait_ge(x2_kept, P + 1)
                        nc.tensor.matmul(OUTB[:, :], centre[:], nodes_of(P), start=True, stop=False)
                    pe.wait_ge(whs[hop], P + 1)
                    for g in range(2):
                        for c in range(NC):
                            last = nc.tensor.matmul(OUTB[:, N * g:N * g + N], wh[hop][:, NC * g + c, :],
                                                    att[hop][:, NC * g + c, :], start=(hop == 0 and c == 0),
                                                    stop=(c == NC - 1 and (hop == 0 or g == 1)))
                    last.then_inc(out_mm[hop], 1)

                def variance0(i, b):
                    P = 2 * i + b
                    if not within(i, P, PAIRS):
                        return
                    pe.wait_ge(sq_ready, P + 1)
                    if due(P - 4):
                        pe.wait_ge(gvar_ln[1], P - 4)
                    nc.tensor.matmul(VARB[:, :], mean_w[:], sq_a[:], start=True, stop=True).then_inc(gvar_mm[0], 1)

                def variance1(i, b):
                    p = 2 * i + b
                    P = p - LAG_Y
                    if not within(i, P, PAIRS):
                        return
                    pe.wait_ge(y3_read, P + 1)
                    pe.wait_ge(gvar_ln[0], at_most(p + 1, PAIRS))
                    if due(p - LAG_NORM2 + 1):
                        pe.wait_ge(s2["var_ln"], p - LAG_NORM2 + 1)
                    nc.tensor.matmul(VARB[:, :], mean_w[:], sq_b[:], start=True, stop=True).then_inc(gvar_mm[1], 1)

                def hidden(i, b, c):
                    P = 2 * i + b - LAG_HID
                    if not within(i, P, PAIRS):
                        return
                    if c == 0:
                        pe.wait_ge(gln, P + 1)
                    if due(FC * P + c):
                        pe.wait_ge(s2["hid_act"], FC * P + c)
                    nc.tensor.matmul(HIDB[:, :], wf1[:, 128 * c:128 * c + 128], nodes_of(P), start=True,
                                     stop=True).then_inc(s2["hid_mm"], 1)

                def output_sum(i, b, half):
                    P, par = 2 * i + b - LAG_SUM, (b + LAG_SUM) % 2
                    if not within(i, P, PAIRS):
                        return
                    if half == 0:
                        if due(P):
                            pe.wait_ge(s2["y_read"], P)
                        nc.tensor.matmul(YB[:, :], centre[:], nodes_of(P), start=True, stop=False)
                        pe.wait_ge(s2["hid_act"], FC * (P + 1))
                    for c in range(FC // 2 * half, FC // 2 * (half + 1)):
                        last = nc.tensor.matmul(YB[:, :], wf2[:, c, :], hid[par][:, c, :], start=False,
                                                stop=(c == FC - 1))
                    if half == 1:
                        last.then_inc(s2["y_mm"], 1)

                def variance2(i, b):
                    p = 2 * i + b
                    P = p - LAG_NORM2
                    if not within(i, P, PAIRS):
                        return
                    pe.wait_ge(s2["y_read"], P + 1)
                    pe.wait_ge(gvar_ln[0], at_most(p + 1, PAIRS))
                    pe.wait_ge(gvar_ln[1], at_most(p - 4, PAIRS))
                    nc.tensor.matmul(VARB[:, :], mean_w[:], fsq[:], start=True, stop=True).then_inc(s2["var_mm"], 1)

                def turn_result(i, b):
                    p = 2 * i + b
                    P = p - LAG_OUT
                    if not within(i, P, PAIRS):
                        return
                    pe.wait_ge(s2["normed"], P + 1)
                    pe.wait_ge(summed[0], at_most(p - 1, PAIRS))
                    if due(P):
                        pe.wait_ge(s2["o_ready"], P)
                    for n in range(2 * NC):
                        last = nc.tensor.transpose(TURNB[:, 128 * n:128 * n + 128], fo[:, 128 * n:128 * n + 128],
                                                   ident[:])
                    last.then_inc(s2["o_mm"], 1)

                def step(i, b):
                    front(i, b, 1)
                    hidden(i, b, 0)
                    turn_result(i, b)
                    variance0(i, b)
                    back(i, b, 1)
                    hidden(i, b, 1)
                    output_sum(i, b, 0)
                    front(i, b, 0)
                    hidden(i, b, 2)
                    variance2(i, b)
                    output_sum(i, b, 1)
                    hidden(i, b, 3)
                    back(i, b, 0)
                    variance1(i, b)

                gat_loop(pe, step)

            @block.scalar
            def _(act):
                act.preload_act_table_set("natural_log_exp_and_others")

                def exps(i, b, hop, side):
                    P = 2 * i + b - LAG_SCORE[hop]
                    if not within(i, P, PAIRS):
                        return
                    if side == 0:
                        act.wait_ge(shifted[hop], P + 1)
                        if due(P):
                            act.wait_ge(out_mm[hop], P)
                    for n in range(2 * NC):
                        last = nc.scalar.activation((att, logits)[side][hop][:, n, :], logits[hop][:, n, :], ACT.Exp,
                                                    bias=shift[hop][:, side, n:n + 1], scale=(1.0, SLOPE)[side])
                    if side == 1:
                        last.then_inc(exped[hop], 1)

                def inverse_std(i, b, n):
                    P = 2 * i + b - (0, LAG_NORM1)[n]
                    if not within(i, P, PAIRS):
                        return
                    r = (r_a, r_b)[n]
                    act.wait_ge(gvar_mm[n], P + 1)
                    if due(P):
                        act.wait_ge(gmid[n], P)
                    nc.scalar.activation(r[:], VARB[:, :], ACT.Ln, bias=eps[:, 0:1]).then_inc(gvar_ln[n], 1)
                    act.wait_ge(gvar_ln[n], P + 1)
                    nc.scalar.activation(r[:], r[:], ACT.Exp, scale=-0.5).then_inc(grstd[n], 1)

                def keep_wh(i, b, hop):
                    P, par = 2 * i + b - LAG_KEEP[hop], (b + LAG_KEEP[hop]) % 2
                    if not within(i, P, PAIRS):
                        return
                    act.wait_ge(wh_mm[hop], P + 1)
                    if due(P - 1):
                        act.wait_ge(whs[hop], P - 1)
                    for g in range(2):
                        last = nc.scalar.copy(wh_raw[hop][par][:, g].rearrange("p c d -> p (c d)"),
                                              WH[g][:, 0:NC * (D + 1)])
                    last.then_inc(wh_kept[hop], 1)

                def second_input(i, b):
                    P, par = 2 * i + b - 3, (b + 1) % 2
                    if not within(i, P, PAIRS):
                        return
                    act.wait_ge(out_mm[0], P + 1)
                    if due(P - 1):
                        act.wait_ge(wh_mm[1], P - 1)
                    nc.scalar.copy(hop_in[1][par][:], OUTB[:, :]).then_inc(hop_ready[1], 1)

                def squares0(i, b):
                    P = 2 * i + b
                    if not within(i, P, PAIRS):
                        return
                    if due(P):
                        act.wait_ge(gvar_mm[0], P)
                    nc.scalar.activation(sq_a[:], nodes_of(P), ACT.Square).then_inc(sq_ready, 1)

                def output(i, b):
                    P = 2 * i + b - LAG_Y
                    if not within(i, P, PAIRS):
                        return
                    act.wait_ge(out_mm[1], P + 1)
                    if due(P - 1):
                        act.wait_ge(gmid[1], P - 1)
                    nc.scalar.copy(y_b[b][:], OUTB[:, :])
                    if due(P):
                        act.wait_ge(gvar_mm[1], P)
                    nc.scalar.activation(sq_b[:], OUTB[:, :], ACT.Square).then_inc(y3_read, 1)

                def relu(i, b, c):
                    P = 2 * i + b - LAG_HID
                    if not within(i, P, PAIRS):
                        return
                    act.wait_ge(s2["hid_mm"], FC * P + c + 1)
                    if c == 0 and due(P - 1):
                        act.wait_ge(s2["y_mm"], P - 1)
                    nc.scalar.activation(hid[b][:, c, :], HIDB[:, :], ACT.Relu,
                                         bias=cols[:, COL_BFF1 + c:COL_BFF1 + c + 1]).then_inc(s2["hid_act"], 1)

                def last_sum(i, b):
                    P, par = 2 * i + b - LAG_SUM, (b + LAG_SUM) % 2
                    if not within(i, P, PAIRS):
                        return
                    act.wait_ge(s2["y_mm"], P + 1)
                    if due(P - 1):
                        act.wait_ge(s2["mid"], P - 1)
                    nc.scalar.activation(fy[par][:], YB[:, :], ACT.Identity, bias=ccols[:, 2:3])
                    if due(P):
                        act.wait_ge(s2["var_mm"], P)
                    nc.scalar.activation(fsq[:], YB[:, :], ACT.Square, bias=ccols[:, 2:3]).then_inc(s2["y_read"], 1)

                def inverse_std2(i, b):
                    P = 2 * i + b - LAG_NORM2
                    if not within(i, P, PAIRS):
                        return
                    act.wait_ge(s2["var_mm"], P + 1)
                    if due(P):
                        act.wait_ge(s2["mid"], P)
                    nc.scalar.activation(fr[:], VARB[:, :], ACT.Ln, bias=eps[:, 0:1]).then_inc(s2["var_ln"], 1)
                    act.wait_ge(s2["var_ln"], P + 1)
                    nc.scalar.activation(fr[:], fr[:], ACT.Exp, scale=-0.5).then_inc(s2["rstd"], 1)

                def step(i, b):
                    keep_wh(i, b, 0)
                    second_input(i, b)
                    inverse_std(i, b, 1)
                    squares0(i, b)
                    exps(i, b, 0, 0)
                    relu(i, b, 0)
                    exps(i, b, 0, 1)
                    keep_wh(i, b, 1)
                    inverse_std(i, b, 0)
                    output(i, b)
                    relu(i, b, 1)
                    exps(i, b, 1, 0)
                    relu(i, b, 2)
                    inverse_std2(i, b)
                    exps(i, b, 1, 1)
                    last_sum(i, b)
                    relu(i, b, 3)

                gat_loop(act, step)

            @block.gpsimd
            def _(pool):
                def mask_here(i, b, hop):
                    P = 2 * i + b - LAG_FRONT[hop]
                    if not within(i, P, PAIRS):
                        return
                    if due(P):
                        pool.wait_ge(summed[hop], P)
                        pool.sem_inc(passed, 1)
                    nc.gpsimd.tensor_copy(hidden_now[hop][:].rearrange("p n i -> p (n i)"),
                                          hidden_bias[:, bass.ds(2 * P, 2)].rearrange(
                                              "p g c i -> p (g c i)")).then_inc(hidden_here[hop], 1)

                def step(i, b):
                    mask_here(i, b, 1)
                    P = 2 * i + b - LAG_NORM0
                    if within(i, P, PAIRS):
                        pool.wait_ge(hop_ready[0], P + 1)
                        pool.sem_inc(passed, 1)
                        nc.gpsimd.tensor_copy(nodes_of(P), hop_in[0][(b + 1) % 2][:]).then_inc(x2_kept, 1)
                    mask_here(i, b, 0)

                gat_loop(pool, step)

            @block.vector
            def _(dve):
                def score(i, b, hop):
                    P = 2 * i + b - LAG_SCORE[hop]
                    if not within(i, P, PAIRS):
                        return
                    wh2 = wh_raw[hop][(b + LAG_SCORE[hop]) % 2][:, :, :, D].rearrange("p g c -> p (g c)")
                    dve.wait_ge(hidden_here[hop], P + 1)
                    dve.sem_inc(passed, 1)
                    dve.wait_ge(bc_mm[hop], P + 1)
                    dve.sem_inc(passed, 1)
                    for g in range(2):
                        for c in range(NC):
                            n = NC * g + c
                            last = nc.vector.tensor_tensor_reduce(
                                logits[hop][:, n, :], BC[hop][:, N * g:N * g + N],
                                hidden_now[hop][:, n, :], 1.0,
                                -3.0e38, ALU.add, ALU.max, top[hop][:, n:n + 1])
                    last.then_inc(summed[hop], 1)
                    dve.wait_ge(wh_kept[hop], P + 1)
                    dve.wait_ge(summed[hop], P + 1)
                    nc.vector.tensor_tensor(top[hop][:], top[hop][:], wh2, ALU.add).then_inc(chain[hop], 1)
                    dve.wait_ge(chain[hop], 2 * P + 1)
                    nc.vector.scalar_tensor_tensor(out=top[hop][:], in0=top[hop][:], scalar=SLOPE, in1=top[hop][:],
                                                   op0=ALU.mult, op1=ALU.max).then_inc(chain[hop], 1)
                    dve.wait_ge(chain[hop], 2 * P + 2)
                    nc.vector.tensor_tensor(shift[hop][:, 0, :], wh2, top[hop][:], ALU.subtract)
                    nc.vector.scalar_tensor_tensor(out=shift[hop][:, 1, :], in0=wh2, scalar=SLOPE,
                                                   in1=top[hop][:], op0=ALU.mult,
                                                   op1=ALU.subtract).then_inc(shifted[hop], 1)

                def weigh(i, b, hop):
                    P = 2 * i + b - LAG_WEIGH[hop]
                    if not within(i, P, PAIRS):
                        return
                    dve.wait_ge(exped[hop], P + 1)
                    for n in range(2 * NC):
                        last = nc.vector.scalar_tensor_tensor(out=att[hop][:, n, :], in0=att[hop][:, n, :], scalar=1.0,
                                                              in1=logits[hop][:, n, :], op0=ALU.mult, op1=ALU.max,
                                                              accum_out=total[hop][:, n:n + 1])
                    last.then_inc(chain2[hop], 1)
                    dve.wait_ge(chain2[hop], 2 * P + 1)
                    nc.vector.reciprocal(inv[hop][:], total[hop][:]).then_inc(chain2[hop], 1)
                    dve.wait_ge(chain2[hop], 2 * P + 2)
                    if due(P):
                        dve.wait_ge(out_mm[hop], P)
                    for n in range(2 * NC):
                        last = nc.vector.tensor_scalar(wh[hop][:, n, :],
                                                       wh_raw[hop][(b + LAG_WEIGH[hop]) % 2][:, n // NC, n % NC, 0:D],
                                                       inv[hop][:, n:n + 1], None, ALU.mult)
                    last.then_inc(whs[hop], 1)

                def norm0(i, b):
                    P, par = 2 * i + b - LAG_NORM0, (b + 1) % 2
                    if not within(i, P, PAIRS):
                        return
                    dve.wait_ge(grstd[0], P + 1)
                    nc.vector.tensor_tensor(mid_a[:], nodes_of(P), r_a[:], ALU.mult).then_inc(gmid[0], 1)
                    dve.wait_ge(gmid[0], P + 1)
                    if due(P - 1):
                        dve.wait_ge(wh_mm[0], P - 1)
                        dve.wait_ge(x2_kept, P - 1)
                    g = COL["L0_gnn_g2"]
                    nc.vector.tensor_scalar(hop_in[0][par][:], mid_a[:], cols[:, g:g + 1], cols[:, g + 1:g + 2],
                                            ALU.mult, ALU.add).then_inc(hop_ready[0], 1)

                def norm1(i, b):
                    P, par = 2 * i + b - LAG_NORM1, (b + 1) % 2
                    if not within(i, P, PAIRS):
                        return
                    dve.wait_ge(grstd[1], P + 1)
                    if due(P):
                        dve.wait_ge(gln, P)
                    nc.vector.tensor_tensor(mid_b[:], y_b[par][:], r_b[:], ALU.mult).then_inc(gmid[1], 1)
                    dve.wait_ge(gmid[1], P + 1)
                    g = COL["L1_gnn_g_ln1"]
                    nc.vector.tensor_scalar(nodes_of(P), mid_b[:], cols[:, g:g + 1], cols[:, g + 1:g + 2],
                                            ALU.mult, ALU.add).then_inc(gln, 1)

                def norm2(i, b):
                    P, par = 2 * i + b - LAG_NORM2, (b + LAG_NORM2) % 2
                    if not within(i, P, PAIRS):
                        return
                    dve.wait_ge(s2["rstd"], P + 1)
                    if due(P):
                        dve.wait_ge(s2["normed"], P)
                    nc.vector.tensor_tensor(fmid[:], fy[par][:], fr[:], ALU.mult).then_inc(s2["mid"], 1)
                    dve.wait_ge(s2["mid"], P + 1)
                    if due(P):
                        dve.wait_ge(s2["o_mm"], P)
                    g = COL["L1_gnn_g_ln2"]
                    nc.vector.tensor_scalar(fo[:], fmid[:], cols[:, g:g + 1], cols[:, g + 1:g + 2], ALU.mult,
                                            ALU.add).then_inc(s2["normed"], 1)

                def result(i, b):
                    P = 2 * i + b - LAG_OUT
                    if not within(i, P, PAIRS):
                        return
                    dve.wait_ge(s2["o_mm"], P + 1)
                    if due(P):
                        dve.wait_ge(o_out, 16 * P)
                    nc.vector.tensor_copy(o_nat[:].rearrange("p n d -> p (n d)"),
                                          TURNB[:, :]).then_inc(s2["o_ready"], 1)

                def step(i, b):
                    score(i, b, 0)
                    weigh(i, b, 1)
                    result(i, b)
                    norm0(i, b)
                    score(i, b, 1)
                    weigh(i, b, 0)
                    norm1(i, b)
                    norm2(i, b)

                gat_loop(dve, step)

            @block.sync
            def _(sp):
                def step(i, b):
                    P = 2 * i + b - LAG_OUT
                    if within(i, P, PAIRS):
                        sp.wait_ge(s2["o_ready"], P + 1)
                        sp.sem_inc(passed, 1)
                        sp.dma_start(out[bass.ds(2 * P, 2)].rearrange("g (c p) d -> p (g c) d", c=NC),
                                     o_nat[:]).then_inc(o_out, 16)
                gat_loop(sp, step)
                sp.wait_ge(o_out, 16 * PAIRS)
        gat_ctx.close()


_INS = ["x", "adj", "L0_gnn_Wq", "L0_gnn_bq", "L0_gnn_Wk", "L0_gnn_bk", "L0_gnn_Wv", "L0_gnn_bv", "L0_gnn_Wo",
        "L0_gnn_bo", "L0_gnn_W1", "L0_gnn_b1", "L0_gnn_W2", "L0_gnn_b2", "L0_gnn_g1", "L0_gnn_beta1", "L0_gnn_g2",
        "L0_gnn_beta2", "L1_gnn_W1", "L1_gnn_a1", "L1_gnn_W2", "L1_gnn_a2", "L1_gnn_w_ff1", "L1_gnn_b_ff1",
        "L1_gnn_w_ff2", "L1_gnn_b_ff2", "L1_gnn_g_ln1", "L1_gnn_b_ln1", "L1_gnn_g_ln2", "L1_gnn_b_ln2"]


def kernel(**inputs):
    import numpy as _np
    import concourse.bacc as _bacc
    from concourse import mybir as _mybir
    from concourse.bass_utils import run_bass_kernel_spmd as _run

    nc = _bacc.Bacc("TRN2", target_bir_lowering=False, num_devices=1)
    arrays, args = {}, {}
    for name in _INS:
        arr = _np.ascontiguousarray(inputs[name])
        arrays[f"in_{name}"] = arr
        args[name] = nc.dram_tensor(f"in_{name}", arr.shape, _mybir.dt.from_np(arr.dtype), kind="ExternalInput").ap()
    out = nc.dram_tensor("out_0", (B, N, D), _mybir.dt.float32, kind="ExternalOutput").ap()
    build(nc, args, out)
    r = _run(nc, [arrays], core_ids=[0])
    return r.results[0]["out_0"]
```
